# Optimizing a Trainium2 kernel written in Bass

```python
import numpy as np
import jax
import jax.numpy as jnp

def _softmax(x, axis=-1):
    return jax.nn.softmax(x, axis=axis)

def _gelu(x):
    return jax.nn.gelu(x, approximate=True)

def _silu(x):
    return jax.nn.silu(x)

def _sigmoid(x):
    return jax.nn.sigmoid(x)

def _layernorm(x, axis=-1, eps=1e-05):
    m = jnp.mean(x, axis=axis, keepdims=True)
    v = jnp.var(x, axis=axis, keepdims=True)
    return (x - m) / jnp.sqrt(v + eps)

def _scatter_add(tgt, idx, src, axis=0):
    return tgt.at[idx].add(src)

def _segment_sum(src, seg, n):
    return jax.ops.segment_sum(src, seg, n)
kernel_name = 'mk_decoder_postln_d2_seqx_r4_eb6af3'

def setup_inputs(seed: int=0):
    np.random.seed(seed)
    _w = jnp.asarray

    def _rec_inputs():
        import jax
        import jax.numpy as jnp
        _rk = jax.random.key(seed)
        x = -0.0002928 + 1 * jax.random.normal(jax.random.fold_in(_rk, 1), (16, 256, 256), jnp.float32)
        _lenS = 256 - jax.random.randint(jax.random.fold_in(_rk, 7), (16,), 0, max(1, 256 // 4) + 1, jnp.int32)
        _lenS2 = 256 - jax.random.randint(jax.random.fold_in(_rk, 8), (16,), 0, max(1, 256 // 4) + 1, jnp.int32)
        _ctx_1024P = jax.random.normal(jax.random.fold_in(_rk, 11), (16, 16, 256), jnp.float32)
        _ctx_1024c = jax.random.dirichlet(jax.random.fold_in(_rk, 511), 0.3 * jnp.ones((16,), jnp.float32), (16, 256))
        _ctx_1024t = jnp.einsum('bsk,bkd->bsd', _ctx_1024c, _ctx_1024P)
        _ctx_1024t = _ctx_1024t * jax.lax.rsqrt(jnp.mean(jnp.square(_ctx_1024t)) + 1e-12) * 0.953939
        ctx_1024 = -1.39393e-06 + 0.999914 * (_ctx_1024t + 0.3 * jax.random.normal(jax.random.fold_in(_rk, 611), (16, 256, 256), jnp.float32))
        _validS = jnp.arange(256)[None, :] < _lenS[:, None]
        _validS2 = jnp.arange(256)[None, :] < _lenS2[:, None]
        _causal = jnp.tril(jnp.ones((256, 256), dtype=bool))
        mask_1x1xSxS2_ik0 = jnp.where(jnp.broadcast_to(_validS2[0:1, None, None, :], (1, 1, 256, 256)), 0, 1).astype(jnp.int32)
        return (x, ctx_1024, mask_1x1xSxS2_ik0)
    x, ctx_1024, mask_1x1xSxS2_ik0 = _rec_inputs()

    def _L0_attn_setup():
        import jax, jax.numpy as jnp
        import numpy as np
        EPS = 1e-05

        def _ln(x, g, b):
            m = x.mean(-1, keepdims=True)
            v = ((x - m) ** 2).mean(-1, keepdims=True)
            return (x - m) * jax.lax.rsqrt(v + EPS) * g + b

        def _tshift(x):
            return jnp.concatenate([jnp.zeros_like(x[:, :1]), x[:, :-1]], axis=1)

        def _wkv(time_decay, time_first, k, v):
            w = -jnp.exp(time_decay)
            u = time_first
            kT = jnp.swapaxes(k, 0, 1)
            vT = jnp.swapaxes(v, 0, 1)
            a0 = jnp.zeros(kT.shape[1:], k.dtype)
            init = (a0, a0, jnp.full_like(a0, -1e+30))

            def step(carry, kv_t):
                a, b, p = carry
                kt, vt = kv_t
                ww = u + kt
                q = jnp.maximum(p, ww)
                e1 = jnp.exp(p - q)
                e2 = jnp.exp(ww - q)
                y = (e1 * a + e2 * vt) / (e1 * b + e2)
                ww2 = p + w
                q2 = jnp.maximum(ww2, kt)
                e1b = jnp.exp(ww2 - q2)
                e2b = jnp.exp(kt - q2)
                return ((e1b * a + e2b * vt, e1b * b + e2b, q2), y)
            _, y = jax.lax.scan(step, init, (kT, vT))
            return jnp.swapaxes(y, 0, 1)
        key = jax.random.key(seed)
        B, T, C, DA, DF = (8, 512, 256, 256, 1024)
        n_layer, layer_id = (12, 1)
        ks = jax.random.split(key, 10)
        s = 0.02
        r01 = layer_id / (n_layer - 1)
        r1a0 = 1.0 - layer_id / n_layer
        ddd = (np.arange(C) / C).astype(np.float32)
        decay_speed = (-5 + 8 * (np.arange(DA) / (DA - 1)) ** (0.7 + 1.3 * r01)).astype(np.float32)
        zigzag = np.array([(i + 1) % 3 - 1 for i in range(DA)], dtype=np.float32) * 0.5
        inp = {'x': jax.random.normal(ks[0], (B, T, C), jnp.float32), 'ln1_g': jnp.ones((C,)), 'ln1_b': jnp.zeros((C,)), 'ln2_g': jnp.ones((C,)), 'ln2_b': jnp.zeros((C,)), 'tm_k': jnp.asarray(ddd ** r1a0), 'tm_v': jnp.asarray(ddd ** r1a0 + 0.3 * r01), 'tm_r': jnp.asarray(ddd ** (0.5 * r1a0)), 'time_decay': jnp.asarray(decay_speed), 'time_first': jnp.asarray(np.float32(np.log(0.3)) + zigzag), 'Wk': jax.random.normal(ks[1], (DA, C), jnp.float32) * s, 'Wv': jax.random.normal(ks[2], (DA, C), jnp.float32) * s, 'Wr': jax.random.normal(ks[3], (DA, C), jnp.float32) * s, 'Wo': jax.random.normal(ks[4], (C, DA), jnp.float32) * s, 'fm_k': jnp.asarray(ddd ** r1a0), 'fm_r': jnp.asarray(ddd ** r1a0), 'Fk': jax.random.normal(ks[5], (DF, C), jnp.float32) * s, 'Fr': jax.random.normal(ks[6], (C, C), jnp.float32) * s, 'Fv': jax.random.normal(ks[7], (C, DF), jnp.float32) * s}
        return inp
    _L0_attn_all = _L0_attn_setup()
    _L0_attn_in = {k: v for k, v in _L0_attn_all.items() if k in ('ln1_g', 'ln1_b', 'ln2_g', 'ln2_b', 'tm_k', 'tm_v', 'tm_r', 'time_decay', 'time_first', 'Wk', 'Wv', 'Wr', 'Wo', 'fm_k', 'fm_r', 'Fk', 'Fr', 'Fv')}
    del _L0_attn_all

    def _L0_xattn_setup():
        import jax, jax.numpy as jnp
        import numpy as np
        import math
        D_MODEL = 256
        NUM_HEADS = 16
        B, S = (2, 512)
        key = jax.random.key(seed)
        ks = jax.random.split(key, 11)

        def w(k):
            return jax.random.normal(k, (D_MODEL, D_MODEL), dtype=jnp.float32) * 0.02

        def b(k):
            return jax.random.normal(k, (D_MODEL,), dtype=jnp.float32) * 0.02
        mask = jnp.tril(jnp.ones((S, S), dtype=jnp.int32))[None, None, :, :]
        return {'q': jax.random.normal(ks[0], (B, S, D_MODEL), dtype=jnp.float32), 'k': jax.random.normal(ks[1], (B, S, D_MODEL), dtype=jnp.float32), 'v': jax.random.normal(ks[2], (B, S, D_MODEL), dtype=jnp.float32), 'mask': mask, 'w_q': w(ks[3]), 'b_q': b(ks[4]), 'w_k': w(ks[5]), 'b_k': b(ks[6]), 'w_v': w(ks[7]), 'b_v': b(ks[8]), 'w_o': w(ks[9]), 'b_o': b(ks[10])}
    _L0_xattn_all = _L0_xattn_setup()
    _L0_xattn_in = {k: v for k, v in _L0_xattn_all.items() if k in ('w_q', 'b_q', 'w_k', 'b_k', 'w_v', 'b_v', 'w_o', 'b_o')}
    del _L0_xattn_all

    def _L0_ffn_setup():
        import jax, jax.numpy as jnp
        import numpy as np
        D_MODEL = 256
        HIDDEN = 1024
        NUM_ROUTED = 7
        TOP_K = 2

        def _swiglu(x_flat, wg, wu, wd):
            g = jnp.einsum('nd,edh->enh', x_flat, wg)
            u = jnp.einsum('nd,edh->enh', x_flat, wu)
            h = jax.nn.silu(g) * u
            return jnp.einsum('enh,ehd->end', h, wd)
        key = jax.random.key(seed)
        ks = jax.random.split(key, 8)
        s = 0.02
        return {'x': jax.random.normal(ks[0], (4, 512, D_MODEL), jnp.float32), 'router_w': jax.random.normal(ks[1], (NUM_ROUTED, D_MODEL), jnp.float32) * s, 'w_gate': jax.random.normal(ks[2], (NUM_ROUTED, D_MODEL, HIDDEN), jnp.float32) * s, 'w_up': jax.random.normal(ks[3], (NUM_ROUTED, D_MODEL, HIDDEN), jnp.float32) * s, 'w_down': jax.random.normal(ks[4], (NUM_ROUTED, HIDDEN, D_MODEL), jnp.float32) * s, 'sw_gate': jax.random.normal(ks[5], (1, D_MODEL, HIDDEN), jnp.float32) * s, 'sw_up': jax.random.normal(ks[6], (1, D_MODEL, HIDDEN), jnp.float32) * s, 'sw_down': jax.random.normal(ks[7], (1, HIDDEN, D_MODEL), jnp.float32) * s}
    _L0_ffn_all = _L0_ffn_setup()
    _L0_ffn_in = {k: v for k, v in _L0_ffn_all.items() if k in ('router_w', 'w_gate', 'w_up', 'w_down', 'sw_gate', 'sw_up', 'sw_down')}
    del _L0_ffn_all

    def _L1_attn_setup():
        import jax, jax.numpy as jnp
        import numpy as np
        DIM = 256
        NUM_HEADS = 16
        HEAD_DIM = DIM // NUM_HEADS
        TAU = 2.0
        V_TH = 1.0
        BN_EPS = 1e-05

        def _branch(x, W, gamma, beta):
            B, N, D = x.shape
            h = jnp.einsum('bnd,ed->bne', x, W)
            hf = h.reshape(B * N, D)
            mean = jnp.mean(hf, axis=0)
            var = jnp.var(hf, axis=0)
            hn = (hf - mean) * jax.lax.rsqrt(var + BN_EPS) * gamma + beta
            hn = hn.reshape(B, N, D)
            return jax.nn.sigmoid(4.0 * (hn - V_TH))

        def _heads(x):
            B, N, D = x.shape
            return x.reshape(B, N, NUM_HEADS, HEAD_DIM).transpose(0, 2, 1, 3)
        key = jax.random.key(seed)
        ks = jax.random.split(key, 12)
        B, N, D = (8, 1024, DIM)
        s = 0.02
        return {'x': jax.random.normal(ks[0], (B, N, D), dtype=jnp.float32), 'Wq': jax.random.normal(ks[1], (D, D), dtype=jnp.float32) * s, 'gq': jnp.ones((D,), jnp.float32), 'bq': jnp.zeros((D,), jnp.float32), 'Wk': jax.random.normal(ks[2], (D, D), dtype=jnp.float32) * s, 'gk': jnp.ones((D,), jnp.float32), 'bk': jnp.zeros((D,), jnp.float32), 'Wv': jax.random.normal(ks[3], (D, D), dtype=jnp.float32) * s, 'gv': jnp.ones((D,), jnp.float32), 'bv': jnp.zeros((D,), jnp.float32), 'Wp': jax.random.normal(ks[4], (D, D), dtype=jnp.float32) * s, 'bp': jnp.zeros((D,), jnp.float32)}
    _L1_attn_all = _L1_attn_setup()
    _L1_attn_in = {k: v for k, v in _L1_attn_all.items() if k in ('Wq', 'gq', 'bq', 'Wk', 'gk', 'bk', 'Wv', 'gv', 'bv', 'Wp', 'bp')}
    del _L1_attn_all

    def _L1_xattn_setup():
        import jax, jax.numpy as jnp
        import numpy as np
        D_MODEL = 256
        NUM_HEADS = 16
        D_K = D_MODEL // NUM_HEADS

        def _split_heads(x, B, S):
            return x.reshape(B, S, NUM_HEADS, D_K).transpose(0, 2, 1, 3)
        key = jax.random.key(seed)
        ks = jax.random.split(key, 12)
        B, S, D = (2, 512, D_MODEL)
        s = 1.0 / np.sqrt(D)
        inp = {'Q': jax.random.normal(ks[0], (B, S, D), jnp.float32), 'K': jax.random.normal(ks[1], (B, S, D), jnp.float32), 'V': jax.random.normal(ks[2], (B, S, D), jnp.float32), 'Wq': jax.random.normal(ks[3], (D, D), jnp.float32) * s, 'bq': jax.random.normal(ks[4], (D,), jnp.float32) * s, 'Wk': jax.random.normal(ks[5], (D, D), jnp.float32) * s, 'bk': jax.random.normal(ks[6], (D,), jnp.float32) * s, 'Wv': jax.random.normal(ks[7], (D, D), jnp.float32) * s, 'bv': jax.random.normal(ks[8], (D,), jnp.float32) * s, 'Wo': jax.random.normal(ks[9], (D, D), jnp.float32) * s, 'bo': jax.random.normal(ks[10], (D,), jnp.float32) * s}
        return inp
    _L1_xattn_all = _L1_xattn_setup()
    _L1_xattn_in = {k: v for k, v in _L1_xattn_all.items() if k in ('Wq', 'bq', 'Wk', 'bk', 'Wv', 'bv', 'Wo', 'bo')}
    del _L1_xattn_all

    def _L1_ffn_setup():
        import jax, jax.numpy as jnp
        import numpy as np
        D = 256
        I = 128
        E = 32
        K = 4
        T = 2 * 512
        C = 2 * T * K // E
        key = jax.random.key(seed)
        ks = jax.random.split(key, 9)
        bf = jnp.bfloat16
        std = 0.02
        x = jax.random.normal(ks[0], (2, 512, D), dtype=jnp.float32).astype(bf)
        gate_w = (std * jax.random.normal(ks[1], (E, D), dtype=jnp.float32)).astype(bf)
        bias = jnp.zeros((E,), jnp.float32)
        W1 = (std * jax.random.normal(ks[2], (E, D, I), dtype=jnp.float32)).astype(bf)
        W3 = (std * jax.random.normal(ks[3], (E, D, I), dtype=jnp.float32)).astype(bf)
        W2 = (std * jax.random.normal(ks[4], (E, I, D), dtype=jnp.float32)).astype(bf)
        sw1 = (std * jax.random.normal(ks[5], (I, D), dtype=jnp.float32)).astype(bf)
        sw3 = (std * jax.random.normal(ks[6], (I, D), dtype=jnp.float32)).astype(bf)
        sw2 = (std * jax.random.normal(ks[7], (D, I), dtype=jnp.float32)).astype(bf)
        return {'x': x, 'gate_w': gate_w, 'bias': bias, 'W1': W1, 'W3': W3, 'W2': W2, 'sw1': sw1, 'sw3': sw3, 'sw2': sw2}
    _L1_ffn_all = _L1_ffn_setup()
    _L1_ffn_in = {k: v for k, v in _L1_ffn_all.items() if k in ('gate_w', 'bias', 'W1', 'W3', 'W2', 'sw1', 'sw3', 'sw2')}
    del _L1_ffn_all
    return {'x': x, 'ctx_1024': ctx_1024, 'mask_1x1xSxS2_ik0': mask_1x1xSxS2_ik0, 'L0_attn_ln1_g': _L0_attn_in['ln1_g'], 'L0_attn_ln1_b': _L0_attn_in['ln1_b'], 'L0_attn_ln2_g': _L0_attn_in['ln2_g'], 'L0_attn_ln2_b': _L0_attn_in['ln2_b'], 'L0_attn_tm_k': _L0_attn_in['tm_k'], 'L0_attn_tm_v': _L0_attn_in['tm_v'], 'L0_attn_tm_r': _L0_attn_in['tm_r'], 'L0_attn_time_decay': _L0_attn_in['time_decay'], 'L0_attn_time_first': _L0_attn_in['time_first'], 'L0_attn_Wk': _L0_attn_in['Wk'], 'L0_attn_Wv': _L0_attn_in['Wv'], 'L0_attn_Wr': _L0_attn_in['Wr'], 'L0_attn_Wo': _L0_attn_in['Wo'], 'L0_attn_fm_k': _L0_attn_in['fm_k'], 'L0_attn_fm_r': _L0_attn_in['fm_r'], 'L0_attn_Fk': _L0_attn_in['Fk'], 'L0_attn_Fr': _L0_attn_in['Fr'], 'L0_attn_Fv': _L0_attn_in['Fv'], 'L0_xattn_w_q': _L0_xattn_in['w_q'], 'L0_xattn_b_q': _L0_xattn_in['b_q'], 'L0_xattn_w_k': _L0_xattn_in['w_k'], 'L0_xattn_b_k': _L0_xattn_in['b_k'], 'L0_xattn_w_v': _L0_xattn_in['w_v'], 'L0_xattn_b_v': _L0_xattn_in['b_v'], 'L0_xattn_w_o': _L0_xattn_in['w_o'], 'L0_xattn_b_o': _L0_xattn_in['b_o'], 'L0_ffn_router_w': _L0_ffn_in['router_w'], 'L0_ffn_w_gate': _L0_ffn_in['w_gate'], 'L0_ffn_w_up': _L0_ffn_in['w_up'], 'L0_ffn_w_down': _L0_ffn_in['w_down'], 'L0_ffn_sw_gate': _L0_ffn_in['sw_gate'], 'L0_ffn_sw_up': _L0_ffn_in['sw_up'], 'L0_ffn_sw_down': _L0_ffn_in['sw_down'], 'L1_attn_Wq': _L1_attn_in['Wq'], 'L1_attn_gq': _L1_attn_in['gq'], 'L1_attn_bq': _L1_attn_in['bq'], 'L1_attn_Wk': _L1_attn_in['Wk'], 'L1_attn_gk': _L1_attn_in['gk'], 'L1_attn_bk': _L1_attn_in['bk'], 'L1_attn_Wv': _L1_attn_in['Wv'], 'L1_attn_gv': _L1_attn_in['gv'], 'L1_attn_bv': _L1_attn_in['bv'], 'L1_attn_Wp': _L1_attn_in['Wp'], 'L1_attn_bp': _L1_attn_in['bp'], 'L1_xattn_Wq': _L1_xattn_in['Wq'], 'L1_xattn_bq': _L1_xattn_in['bq'], 'L1_xattn_Wk': _L1_xattn_in['Wk'], 'L1_xattn_bk': _L1_xattn_in['bk'], 'L1_xattn_Wv': _L1_xattn_in['Wv'], 'L1_xattn_bv': _L1_xattn_in['bv'], 'L1_xattn_Wo': _L1_xattn_in['Wo'], 'L1_xattn_bo': _L1_xattn_in['bo'], 'L1_ffn_gate_w': _L1_ffn_in['gate_w'], 'L1_ffn_bias': _L1_ffn_in['bias'], 'L1_ffn_W1': _L1_ffn_in['W1'], 'L1_ffn_W3': _L1_ffn_in['W3'], 'L1_ffn_W2': _L1_ffn_in['W2'], 'L1_ffn_sw1': _L1_ffn_in['sw1'], 'L1_ffn_sw3': _L1_ffn_in['sw3'], 'L1_ffn_sw2': _L1_ffn_in['sw2']}

def reference(x, ctx_1024, mask_1x1xSxS2_ik0, L0_attn_ln1_g, L0_attn_ln1_b, L0_attn_ln2_g, L0_attn_ln2_b, L0_attn_tm_k, L0_attn_tm_v, L0_attn_tm_r, L0_attn_time_decay, L0_attn_time_first, L0_attn_Wk, L0_attn_Wv, L0_attn_Wr, L0_attn_Wo, L0_attn_fm_k, L0_attn_fm_r, L0_attn_Fk, L0_attn_Fr, L0_attn_Fv, L0_xattn_w_q, L0_xattn_b_q, L0_xattn_w_k, L0_xattn_b_k, L0_xattn_w_v, L0_xattn_b_v, L0_xattn_w_o, L0_xattn_b_o, L0_ffn_router_w, L0_ffn_w_gate, L0_ffn_w_up, L0_ffn_w_down, L0_ffn_sw_gate, L0_ffn_sw_up, L0_ffn_sw_down, L1_attn_Wq, L1_attn_gq, L1_attn_bq, L1_attn_Wk, L1_attn_gk, L1_attn_bk, L1_attn_Wv, L1_attn_gv, L1_attn_bv, L1_attn_Wp, L1_attn_bp, L1_xattn_Wq, L1_xattn_bq, L1_xattn_Wk, L1_xattn_bk, L1_xattn_Wv, L1_xattn_bv, L1_xattn_Wo, L1_xattn_bo, L1_ffn_gate_w, L1_ffn_bias, L1_ffn_W1, L1_ffn_W3, L1_ffn_W2, L1_ffn_sw1, L1_ffn_sw3, L1_ffn_sw2):
    import jax
    import jax.numpy as jnp

    def _L0_attn_ref(x, ln1_g, ln1_b, ln2_g, ln2_b, tm_k, tm_v, tm_r, time_decay, time_first, Wk, Wv, Wr, Wo, fm_k, fm_r, Fk, Fr, Fv):
        import jax, jax.numpy as jnp
        import numpy as np
        EPS = 1e-05

        def _ln(x, g, b):
            m = x.mean(-1, keepdims=True)
            v = ((x - m) ** 2).mean(-1, keepdims=True)
            return (x - m) * jax.lax.rsqrt(v + EPS) * g + b

        def _tshift(x):
            return jnp.concatenate([jnp.zeros_like(x[:, :1]), x[:, :-1]], axis=1)

        def _wkv(time_decay, time_first, k, v):
            w = -jnp.exp(time_decay)
            u = time_first
            kT = jnp.swapaxes(k, 0, 1)
            vT = jnp.swapaxes(v, 0, 1)
            a0 = jnp.zeros(kT.shape[1:], k.dtype)
            init = (a0, a0, jnp.full_like(a0, -1e+30))

            def step(carry, kv_t):
                a, b, p = carry
                kt, vt = kv_t
                ww = u + kt
                q = jnp.maximum(p, ww)
                e1 = jnp.exp(p - q)
                e2 = jnp.exp(ww - q)
                y = (e1 * a + e2 * vt) / (e1 * b + e2)
                ww2 = p + w
                q2 = jnp.maximum(ww2, kt)
                e1b = jnp.exp(ww2 - q2)
                e2b = jnp.exp(kt - q2)
                return ((e1b * a + e2b * vt, e1b * b + e2b, q2), y)
            _, y = jax.lax.scan(step, init, (kT, vT))
            return jnp.swapaxes(y, 0, 1)
        h = _ln(x, ln1_g, ln1_b)
        hh = _tshift(h)
        xk = h * tm_k + hh * (1 - tm_k)
        xv = h * tm_v + hh * (1 - tm_v)
        xr = h * tm_r + hh * (1 - tm_r)
        k = jnp.einsum('btc,dc->btd', xk, Wk)
        v = jnp.einsum('btc,dc->btd', xv, Wv)
        sr = jax.nn.sigmoid(jnp.einsum('btc,dc->btd', xr, Wr))
        rwkv = sr * _wkv(time_decay, time_first, k, v)
        x = x + jnp.einsum('btd,cd->btc', rwkv, Wo)
        g = _ln(x, ln2_g, ln2_b)
        gg = _tshift(g)
        gk = g * fm_k + gg * (1 - fm_k)
        gr = g * fm_r + gg * (1 - fm_r)
        kf = jnp.square(jax.nn.relu(jnp.einsum('btc,fc->btf', gk, Fk)))
        kv = jnp.einsum('btf,cf->btc', kf, Fv)
        x = x + jax.nn.sigmoid(jnp.einsum('btc,dc->btd', gr, Fr)) * kv
        return x

    def _L0_xattn_ref(q, k, v, mask, w_q, b_q, w_k, b_k, w_v, b_v, w_o, b_o):
        import jax, jax.numpy as jnp
        import numpy as np
        import math
        D_MODEL = 256
        NUM_HEADS = 16
        B, S = (2, 512)
        B_, S_, D = q.shape
        H = NUM_HEADS
        dk = D // H

        def proj(x, W, b):
            return (x @ W.T + b).reshape(B_, S_, H, dk).transpose(0, 2, 1, 3)
        Q = proj(q, w_q, b_q)
        K = proj(k, w_k, b_k)
        V = proj(v, w_v, b_v)
        scores = jnp.einsum('bhqd,bhkd->bhqk', Q, K) / math.sqrt(dk)
        scores = jnp.where(mask == 0, jnp.float32(-1000000000.0), scores)
        attn = jax.nn.softmax(scores, axis=-1)
        x = jnp.einsum('bhqk,bhkd->bhqd', attn, V)
        x = x.transpose(0, 2, 1, 3).reshape(B_, S_, D)
        return x @ w_o.T + b_o

    def _L0_ffn_ref(x, router_w, w_gate, w_up, w_down, sw_gate, sw_up, sw_down):
        import jax, jax.numpy as jnp
        import numpy as np
        D_MODEL = 256
        HIDDEN = 1024
        NUM_ROUTED = 7
        TOP_K = 2

        def _swiglu(x_flat, wg, wu, wd):
            g = jnp.einsum('nd,edh->enh', x_flat, wg)
            u = jnp.einsum('nd,edh->enh', x_flat, wu)
            h = jax.nn.silu(g) * u
            return jnp.einsum('enh,ehd->end', h, wd)
        orig_shape = x.shape
        x_flat = x.reshape(-1, orig_shape[-1])
        N = x_flat.shape[0]
        logits = x_flat @ router_w.T
        top_vals, top_idx = jax.lax.top_k(logits, TOP_K)
        top_w = jax.nn.softmax(top_vals, axis=-1)
        combine = jnp.sum(jax.nn.one_hot(top_idx, NUM_ROUTED, dtype=x.dtype) * top_w[..., None], axis=1)
        routed_out = _swiglu(x_flat, w_gate, w_up, w_down)
        mixed = jnp.einsum('end,ne->nd', routed_out, combine)
        shared_out = _swiglu(x_flat, sw_gate, sw_up, sw_down)
        mixed = mixed + jnp.mean(shared_out, axis=0)
        return mixed.reshape(orig_shape)

    def _L1_attn_ref(x, Wq, gq, bq, Wk, gk, bk, Wv, gv, bv, Wp, bp):
        import jax, jax.numpy as jnp
        import numpy as np
        DIM = 256
        NUM_HEADS = 16
        HEAD_DIM = DIM // NUM_HEADS
        TAU = 2.0
        V_TH = 1.0
        BN_EPS = 1e-05

        def _branch(x, W, gamma, beta):
            B, N, D = x.shape
            h = jnp.einsum('bnd,ed->bne', x, W)
            hf = h.reshape(B * N, D)
            mean = jnp.mean(hf, axis=0)
            var = jnp.var(hf, axis=0)
            hn = (hf - mean) * jax.lax.rsqrt(var + BN_EPS) * gamma + beta
            hn = hn.reshape(B, N, D)
            return jax.nn.sigmoid(4.0 * (hn - V_TH))

        def _heads(x):
            B, N, D = x.shape
            return x.reshape(B, N, NUM_HEADS, HEAD_DIM).transpose(0, 2, 1, 3)
        B, N, D = x.shape
        scale = HEAD_DIM ** (-0.5)
        q = _branch(x, Wq, gq, bq)
        k = _branch(x, Wk, gk, bk)
        v = _branch(x, Wv, gv, bv)
        qk = _heads(q * k) * scale
        v_h = _heads(v)
        vv = jnp.einsum('bhnd,bhne->bhde', v_h, v_h)
        out = jnp.einsum('bhnd,bhde->bhne', qk, vv)
        out = out.transpose(0, 2, 1, 3).reshape(B, N, D)
        return jnp.einsum('bnd,ed->bne', out, Wp) + bp

    def _L1_xattn_ref(Q, K, V, Wq, bq, Wk, bk, Wv, bv, Wo, bo):
        import jax, jax.numpy as jnp
        import numpy as np
        D_MODEL = 256
        NUM_HEADS = 16
        D_K = D_MODEL // NUM_HEADS

        def _split_heads(x, B, S):
            return x.reshape(B, S, NUM_HEADS, D_K).transpose(0, 2, 1, 3)
        B, S, D = Q.shape
        q = _split_heads(Q @ Wq.T + bq, B, S)
        k = _split_heads(K @ Wk.T + bk, B, S)
        v = _split_heads(V @ Wv.T + bv, B, S)
        scale = 1.0 / np.sqrt(D_K).astype(np.float32)
        scores = jnp.einsum('bhqd,bhkd->bhqk', q, k) * scale
        probs = jax.nn.softmax(scores, axis=-1)
        out = jnp.einsum('bhqk,bhkd->bhqd', probs, v)
        out = out.transpose(0, 2, 1, 3).reshape(B, S, D)
        return out @ Wo.T + bo

    def _L1_ffn_ref(x, gate_w, bias, W1, W3, W2, sw1, sw3, sw2):
        import jax, jax.numpy as jnp
        import numpy as np
        D = 256
        I = 128
        E = 32
        K = 4
        T = 2 * 512
        C = 2 * T * K // E
        X = x.reshape(-1, D)
        logits = (X @ gate_w.T).astype(jnp.float32)
        scores = jax.nn.sigmoid(logits)
        _, idx = jax.lax.top_k(scores + bias[None, :], K)
        w = jnp.take_along_axis(scores, idx, axis=-1)
        w = w / jnp.clip(jnp.sum(w, axis=-1, keepdims=True), 1e-12, None)
        w = w.astype(x.dtype)
        eid = idx.reshape(-1)
        onehot = (eid[:, None] == jnp.arange(E)[None, :]).astype(jnp.int32)
        pos = jnp.take_along_axis(jnp.cumsum(onehot, axis=0) - 1, eid[:, None], axis=1)[:, 0]
        valid = pos < C
        posc = jnp.minimum(pos, C - 1)
        Xrep = jnp.repeat(X, K, axis=0)
        xe = jnp.zeros((E, C, D), x.dtype).at[eid, posc].add(jnp.where(valid[:, None], Xrep, jnp.zeros((), x.dtype)))
        h = jax.nn.silu(jnp.einsum('ecd,edi->eci', xe, W1)) * jnp.einsum('ecd,edi->eci', xe, W3)
        ye = jnp.einsum('eci,eid->ecd', h, W2)
        gflat = jnp.where(valid, w.reshape(-1), jnp.zeros((), x.dtype))
        yrows = ye[eid, posc] * gflat[:, None]
        out = yrows.reshape(-1, K, D).sum(axis=1)
        out = out + jax.nn.silu(X @ sw1.T) * (X @ sw3.T) @ sw2.T
        return out.reshape(x.shape)
    x = _layernorm(x + _L0_attn_ref(x, L0_attn_ln1_g, L0_attn_ln1_b, L0_attn_ln2_g, L0_attn_ln2_b, L0_attn_tm_k, L0_attn_tm_v, L0_attn_tm_r, L0_attn_time_decay, L0_attn_time_first, L0_attn_Wk, L0_attn_Wv, L0_attn_Wr, L0_attn_Wo, L0_attn_fm_k, L0_attn_fm_r, L0_attn_Fk, L0_attn_Fr, L0_attn_Fv), axis=-1)
    x = _layernorm(x + _L0_xattn_ref(x, ctx_1024, ctx_1024, mask_1x1xSxS2_ik0, L0_xattn_w_q, L0_xattn_b_q, L0_xattn_w_k, L0_xattn_b_k, L0_xattn_w_v, L0_xattn_b_v, L0_xattn_w_o, L0_xattn_b_o), axis=-1)
    x = _layernorm(x + _L0_ffn_ref(x, L0_ffn_router_w, L0_ffn_w_gate, L0_ffn_w_up, L0_ffn_w_down, L0_ffn_sw_gate, L0_ffn_sw_up, L0_ffn_sw_down), axis=-1)
    x = _layernorm(x + _L1_attn_ref(x, L1_attn_Wq, L1_attn_gq, L1_attn_bq, L1_attn_Wk, L1_attn_gk, L1_attn_bk, L1_attn_Wv, L1_attn_gv, L1_attn_bv, L1_attn_Wp, L1_attn_bp), axis=-1)
    x = _layernorm(x + _L1_xattn_ref(x, ctx_1024, ctx_1024, L1_xattn_Wq, L1_xattn_bq, L1_xattn_Wk, L1_xattn_bk, L1_xattn_Wv, L1_xattn_bv, L1_xattn_Wo, L1_xattn_bo), axis=-1)
    x = _layernorm(x + _L1_ffn_ref(x, L1_ffn_gate_w, L1_ffn_bias, L1_ffn_W1, L1_ffn_W3, L1_ffn_W2, L1_ffn_sw1, L1_ffn_sw3, L1_ffn_sw2), axis=-1)
    return x

_drawn_inputs = setup_inputs


def setup_inputs(seed=0):
    import zlib

    import numpy as np

    out = dict(_drawn_inputs(seed))
    spreads = {'L0_attn_ln1_g': (1.0, 0.6),
     'L0_attn_ln1_b': (0.0, 0.8),
     'L0_attn_ln2_g': (1.0, 0.6),
     'L0_attn_ln2_b': (0.0, 0.8),
     'L1_attn_gq': (1.0, 0.2),
     'L1_attn_bq': (0.0, 0.1),
     'L1_attn_gk': (1.0, 0.2),
     'L1_attn_bk': (0.0, 0.1),
     'L1_attn_gv': (1.0, 0.2),
     'L1_attn_bv': (0.0, 0.1),
     'L1_attn_bp': (0.0, 0.1),
     'L1_ffn_bias': (0.0, 0.8)}
    factors = {'L0_attn_tm_k': 8.0,
     'L0_attn_tm_v': 8.0,
     'L0_attn_tm_r': 8.0,
     'L0_attn_time_decay': 6.306,
     'L0_attn_time_first': 8.0,
     'L0_attn_Wk': 8.0,
     'L0_attn_Wv': 4.36,
     'L0_attn_Wr': 8.0,
     'L0_attn_Wo': 4.338,
     'L0_attn_fm_k': 6.41,
     'L0_attn_fm_r': 8.0,
     'L0_attn_Fk': 4.305,
     'L0_attn_Fr': 8.0,
     'L0_attn_Fv': 4.023,
     'L0_xattn_w_q': 8.0,
     'L0_xattn_b_q': 8.0,
     'L0_xattn_w_k': 8.0,
     'L0_xattn_b_k': 8.0,
     'L0_xattn_b_v': 8.0,
     'L0_xattn_b_o': 3.675,
     'L0_ffn_router_w': 2.925,
     'L1_xattn_bq': 4.702,
     'L1_xattn_bk': 8.0,
     'L1_ffn_gate_w': 8.0,
     'L1_ffn_W1': 8.0,
     'L1_ffn_W3': 8.0,
     'L1_ffn_W2': 8.0,
     'L1_ffn_sw1': 4.874,
     'L1_ffn_sw3': 4.667,
     'L1_ffn_sw2': 4.682}
    for name, (base, spread) in spreads.items():
        noise = np.random.default_rng([zlib.crc32(name.encode()), seed]).standard_normal(out[name].shape)
        drawn = base * np.exp(spread * noise) if base else spread * noise
        out[name] = jnp.asarray(drawn.astype(out[name].dtype))
    for name, factor in factors.items():
        out[name] = (out[name] * factor).astype(out[name].dtype)
    return out
```

```python
from contextlib import ExitStack

import numpy as np

import concourse.bass as bass
from concourse import mybir

F32 = mybir.dt.float32
BF16 = mybir.dt.bfloat16
I32 = mybir.dt.int32
U32 = mybir.dt.uint32
ALU = mybir.AluOpType
ACT = mybir.ActivationFunctionType
AX = mybir.AxisListType

P = 128
B, S, D = 16, 256, 256
N = B * S
KC = D // P
TB = S // P
U = 2
STEPS = B // U
NBLK = N // P
HEADS, DH = 16, 16
HPC = P // DH
QUADS = HEADS // 4
F = 1024
FC = F // P
E0, K0 = 7, 2
E0P = 8
REG0 = N + S
TILES_SHARED = N // S
E1, K1, I1 = 32, 4, 128
CAP1 = 2 * (2 * 512) * K1 // E1
SHARED1 = E1 * CAP1
DUMP1 = SHARED1 + N
ROWS1 = DUMP1 + S
TILES1 = (SHARED1 + N) // S
ZERO_ROWS = 8 * P
MAX_TILES = TILES_SHARED + N * K0 // S + E0
EPS = 1e-5
NEG = -1e30
EXP_MAX = 80.0
SCALE = 1.0 / DH ** 0.5
FAR = float(1 << 17)
DVE_STEPS = [26, 41]

VECS = ["L0_attn_ln1_g", "L0_attn_ln1_b", "L0_attn_ln2_g", "L0_attn_ln2_b", "L0_attn_tm_k", "L0_attn_tm_v",
        "L0_attn_tm_r", "L0_attn_time_decay", "L0_attn_time_first", "L0_attn_fm_k", "L0_attn_fm_r",
        "L0_xattn_b_q", "L0_xattn_b_k", "L1_xattn_bq", "L1_xattn_bk",
        "L1_attn_gq", "L1_attn_gk", "L1_attn_gv", "L1_attn_bq", "L1_attn_bk", "L1_attn_bv"]
ROWS = ["L0_xattn_b_v", "L0_xattn_b_o", "L1_xattn_bv", "L1_xattn_bo", "L1_attn_bp"]


class Steps:

    def __init__(self, eng, sem, i, per):
        self.eng, self.sem, self.base, self.n, self.per = eng, sem, i * per, 0, per

    def mark(self, ins):
        self.n += 1
        ins.then_inc(self.sem, 1)
        return self.n

    def after(self, n):
        self.eng.wait_ge(self.sem, self.base + n)

    def do(self, ins):
        self.after(self.mark(ins))

    def close(self):
        assert self.n == self.per, (self.n, self.per)


class Store:

    def __init__(self):
        self.stage_sems = []

    def semaphore(self, nc, name):
        self.stage_sems.append(nc.alloc_semaphore(name=name))
        return self.stage_sems[-1]

    def end_stage(self, nc):
        nc.clear_and_free_semaphores(self.stage_sems)
        nc.all_engine_barrier()
        self.stage_sems = []


def vec(st, name, c):
    n = 2 * VECS.index(name) + c
    return st.vecs[:, n:n + 1]


def col(w):
    return w.rearrange("(k p) n -> p k n", p=P)


def setup_stage(nc, st, d):
    with ExitStack() as ctx:
        loaded = st.semaphore(nc, "consts_loaded")
        zeroed = st.semaphore(nc, "consts_zeroed")
        shaped = st.semaphore(nc, "consts_shaped")
        padded = st.semaphore(nc, "slots_zeroed")
        decay = st.semaphore(nc, "decay_ready")
        block = ctx.enter_context(nc.Block())

        @block.sync
        def _(sp):
            sp.dma_start(st.vecs[:], d["vecs"]).then_inc(loaded, 16)
            sp.dma_start(st.rows[:], d["rows"].partition_broadcast(P)).then_inc(loaded, 16)
            sp.dma_start(st.ebias[:], d["L1_ffn_bias"].partition_broadcast(P)).then_inc(loaded, 16)
            sp.wait_ge(loaded, 48)
            sp.wait_ge(zeroed, 1)
            for r in range(0, SHARED1, 8 * P):
                n = min(8 * P, SHARED1 - r)
                sp.dma_start(st.xs1[r:r + n, :].rearrange("(n p) c -> p n c", p=P),
                             st.zero[:].unsqueeze(1).to_broadcast([P, n // P, D])).then_inc(padded, 16)
            sp.dma_start(st.ys1[DUMP1:ROWS1, :].rearrange("(n p) c -> p n c", p=P),
                         st.zero[:].unsqueeze(1).to_broadcast([P, TB, D])).then_inc(padded, 16)
            sp.wait_ge(padded, 16 * (-(-SHARED1 // (8 * P)) + 1))

        @block.gpsimd
        def _(pool):
            pool.memset(st.zero[:], 0.0).then_inc(zeroed, 1)
            pool.memset(st.ident[:], 0.0).then_inc(zeroed, 1)
            pool.memset(st.lower[:], 1.0).then_inc(zeroed, 1)
            pool.memset(st.ones[:], 1.0).then_inc(zeroed, 1)
            pool.memset(st.hmask[:], 1.0).then_inc(zeroed, 1)
            pool.memset(st.selrow[:], 1.0).then_inc(zeroed, 1)
            pool.memset(st.eps[:], EPS).then_inc(zeroed, 1)
            pool.memset(st.blk[:], SCALE).then_inc(zeroed, 1)
            pool.memset(st.neghalf[:], -0.5).then_inc(zeroed, 1)
            pool.iota(st.iota[:], pattern=[[1, E1]], base=0, channel_multiplier=0,
                      allow_small_or_imprecise_dtypes=True).then_inc(zeroed, 1)
            pool.iota(st.base0[:], pattern=[[REG0, E0P]], base=REG0, channel_multiplier=0,
                      allow_small_or_imprecise_dtypes=True).then_inc(zeroed, 1)
            pool.iota(st.base1[:], pattern=[[CAP1, E1]], base=0, channel_multiplier=0,
                      allow_small_or_imprecise_dtypes=True).then_inc(zeroed, 1)
            pool.wait_ge(zeroed, 12)
            pool.affine_select(out=st.ident[:], in_=st.ident[:], compare_op=ALU.not_equal, fill=1.0, base=0,
                               pattern=[[-1, P]], channel_multiplier=1).then_inc(shaped, 1)
            pool.affine_select(out=st.lower[:], in_=st.lower[:], compare_op=ALU.is_gt, fill=0.0, base=0,
                               pattern=[[1, P]], channel_multiplier=-1).then_inc(shaped, 1)
            pool.affine_select(out=st.hmask[:], in_=st.hmask[:], compare_op=ALU.is_ge, fill=0.0, base=0,
                               pattern=[[-DH, HPC]], channel_multiplier=1).then_inc(shaped, 1)
            pool.wait_ge(shaped, 3)
            pool.affine_select(out=st.hmask[:], in_=st.hmask[:], compare_op=ALU.is_ge, fill=0.0, base=DH - 1,
                               pattern=[[DH, HPC]], channel_multiplier=-1).then_inc(shaped, 1)
            pool.affine_select(out=st.selrow[:], in_=st.selrow[:], compare_op=ALU.is_equal, fill=0.0, base=0,
                               pattern=[[-1, HEADS], [0, P]], channel_multiplier=1).then_inc(shaped, 1)
            blk = st.blk[:].rearrange("p (h r) -> p h r", r=DH)
            pool.affine_select(out=blk, in_=blk, compare_op=ALU.is_ge, fill=0.0, base=0,
                               pattern=[[-DH, HPC], [0, DH]], channel_multiplier=1).then_inc(shaped, 1)
            pool.wait_ge(shaped, 6)
            pool.affine_select(out=blk, in_=blk, compare_op=ALU.is_ge, fill=0.0, base=DH - 1,
                               pattern=[[DH, HPC], [0, DH]], channel_multiplier=-1).then_inc(shaped, 1)
            pool.tensor_copy(st.identb[:], st.ident[:]).then_inc(shaped, 1)
            pool.wait_ge(shaped, 8)
            pool.memset(st.eps[:], EPS).then_inc(st.consts_ready, 1)

        @block.scalar
        def _(act):
            act.wait_ge(loaded, 48)
            n = 2 * VECS.index("L0_attn_time_decay")
            act.activation(st.w[:], st.vecs[:, n:n + KC], ACT.Exp).then_inc(decay, 1)

        @block.vector
        def _(dve):
            dve.memset(st.macc0[:], 0.0).then_inc(decay, 1)
            dve.memset(st.macc1[:], 0.0).then_inc(decay, 1)
            dve.wait_ge(decay, 3)
            dve.wait_ge(zeroed, 12)
            dve.tensor_scalar(st.w[:], st.w[:], -1.0, None, ALU.mult).then_inc(decay, 1)
            dve.wait_ge(decay, 4)
            for c in range(KC):
                dve.tensor_scalar(st.wdec[:, c, :], st.zero[:, 0:S], st.w[:, c:c + 1], None, ALU.add).then_inc(decay, 1)
            dve.wait_ge(decay, 4 + KC)


def pool_rstd(pool, st, var, rstd, u, var_ready, rstd_ready, eps_added, count):
    pool.wait_ge(var_ready, count)
    pool.tensor_tensor(rstd[:, u, :], var[:, u, :, 1], st.eps[:, 0:TB], ALU.add).then_inc(eps_added, 1)
    pool.wait_ge(eps_added, count)
    pool.tensor_tensor(rstd[:, u, :], rstd[:, u, :], st.neghalf[:, 0:TB], ALU.pow).then_inc(rstd_ready, 1)


def dve_stats(dve, st, steps, x, stats, var, u, var_ready):
    for t in range(TB):
        n = steps.mark(dve.bn_stats(stats[:, u, t, :], x[:, t, :]))
    steps.after(n)
    dve.sem_inc(st.dve_passed, 1)
    dve.bn_aggr(var[:, u, 0, :], stats[:, u, 0, :])
    dve.bn_aggr(var[:, u, 1, :], stats[:, u, 1, :]).then_inc(var_ready, 1)


def dve_normalize(dve, out, x, var, rstd, u):
    for t in range(TB):
        ins = dve.tensor_scalar(out[:, t, :], x[:, t, :], var[:, u, t, 0:1], rstd[:, u, t:t + 1],
                                ALU.subtract, ALU.mult)
    return ins


def rwkv_stage(nc, st, d):
    with ExitStack() as ctx:
        def sb(name, shape, dt=F32):
            return ctx.enter_context(nc.sbuf_tensor("rw_" + name, shape, dt))

        def sem(name):
            return st.semaphore(nc, "rw_" + name)

        wk, wv, wr, wo, fr = (sb(n, [P, KC, D]) for n in ("wk", "wv", "wr", "wo", "fr"))
        fk = sb("fk", [P, KC, F])
        fv = sb("fv", [P, FC, D])
        x = sb("x", [P, U, TB, D])
        nrm = sb("nrm", [P, U, TB, D])
        h = sb("h", [P, U, KC, S + 1])
        dif = sb("dif", [P, U, KC, S])
        mix = sb("mix", [P, U, 3, KC, S])
        ex = sb("ex", [P, U, 4, KC, S])
        top = sb("top", [P, U, KC, S + 1])
        num = sb("num", [P, U, KC, S + 1])
        den = sb("den", [P, U, KC, S + 1])
        er = sb("er", [P, U, KC, S])
        e2bv = sb("e2bv", [P, U, KC, S])
        q = sb("q", [P, U, KC, S])
        y1 = sb("y1", [P, U, KC, S])
        y2 = sb("y2", [P, U, KC, S])
        rw = sb("rw", [P, U, KC, S])
        x2 = sb("x2", [P, U, TB, D])
        kf = sb("kf", [P, U, FC, S])
        es = sb("es", [P, U, TB, D])
        stats = sb("stats", [P, U, TB, 6])
        var = sb("var", [P, U, TB, 2])
        rstd = sb("rstd", [P, U, TB])
        ps = ctx.enter_context(nc.psum_tensor("rw_ps", [P, U, 4, 512], F32))

        def bank(u, n):
            return ps[:, u, n, :].rearrange("p (a b) -> p a b", a=2)

        w_loaded = sem("w_loaded")
        x_loaded = [sem(f"x_loaded{u}") for u in range(U)]
        var1, rstd1, eps1 = sem("var1_ready"), sem("rstd1_ready"), sem("eps1_added")
        var2, rstd2, eps2 = sem("var2_ready"), sem("rstd2_ready"), sem("eps2_added")
        var3, rstd3, eps3 = sem("var3_ready"), sem("rstd3_ready"), sem("eps3_added")
        norm1, norm2, x1_ready = sem("norm1_ready"), sem("norm2_ready"), sem("x1_ready")
        t1_ready, t2_ready = sem("t1_ready"), sem("t2_ready")
        h_ready, g_ready = sem("h_ready"), sem("g_ready")
        mix_ready, gmix_ready = sem("mix_ready"), sem("gmix_ready")
        kvr_ready = sem("kvr_ready")
        er_ready, args_ready, ex_ready = sem("er_ready"), sem("args_ready"), sem("ex_ready")
        rw_ready, o_ready = sem("rw_ready"), sem("o_ready")
        hid_ready, relu_ready, kf_ready = sem("hid_ready"), sem("relu_ready"), sem("kf_ready")
        f_ready, es_ready, kv_ready = sem("f_ready"), sem("es_ready"), sem("kv_ready")
        negr_ready, negf_ready = sem("negr_ready"), sem("negf_ready")
        edges_set = sem("edges_set")
        dve_steps = sem("dve_steps")
        block = ctx.enter_context(nc.Block())
        xv = d["x"].rearrange("(n p) c -> p n c", p=P)

        @block.sync
        def _(sp):
            for u in range(U):
                sp.dma_start(x[:, u], xv[:, TB * u:TB * u + TB, :]).then_inc(x_loaded[u], 16)
            for t, n in ((wk, "L0_attn_Wk"), (wv, "L0_attn_Wv"), (wr, "L0_attn_Wr"), (wo, "L0_attn_Wo"),
                         (fk, "L0_attn_Fk"), (fr, "L0_attn_Fr"), (fv, "L0_attn_Fv")):
                sp.dma_start(t[:], col(d[n])).then_inc(w_loaded, 16)
            for r in range(N, (E0 + 1) * REG0, ZERO_ROWS):
                sp.dma_start(st.ys0[r:r + ZERO_ROWS, :].rearrange("(n p) c -> p n c", p=P),
                             st.zero[:].unsqueeze(1).to_broadcast([P, ZERO_ROWS // P, D])).then_inc(st.ys0_zeroed, 16)
            with sp.Fori(0, STEPS - 1) as i:
                for u in range(U):
                    sp.wait_ge(x1_ready, U * i + u + 1)
                    sp.dma_start(x[:, u], xv[:, bass.ds(TB * U * (i + 1) + TB * u, TB), :]).then_inc(x_loaded[u], 16)

        @block.gpsimd
        def _(pool):
            with pool.Fori(0, STEPS) as i:
                for var_r, rstd_r, eps_r in ((var1, rstd1, eps1), (var2, rstd2, eps2), (var3, rstd3, eps3)):
                    for u in range(U):
                        pool_rstd(pool, st, var, rstd, u, var_r, rstd_r, eps_r, U * i + u + 1)

        @block.tensor
        def _(pe):
            pe.wait_ge(w_loaded, 16 * 7)

            def turn(u, dst):
                for t in range(TB):
                    for c in range(KC):
                        ins = pe.transpose(dst[:, c, t * P:t * P + P], nrm[:, u, t, c * P:c * P + P], st.ident[:])
                return ins

            with pe.Fori(0, STEPS) as i:
                for u in range(U):
                    pe.wait_ge(norm1, U * i + u + 1)
                    turn(u, bank(u, 0)).then_inc(t1_ready, 1)
                for u in range(U):
                    pe.wait_ge(mix_ready, U * i + u + 1)
                    for n, w in enumerate((wk, wv, wr)):
                        for m in range(KC):
                            for c in range(KC):
                                ins = pe.matmul(bank(u, 1 + n)[:, m, :], w[:, c, m * P:m * P + P], mix[:, u, n, c, :],
                                                start=(c == 0), stop=(c == KC - 1))
                    ins.then_inc(kvr_ready, 1)
                for u in range(U):
                    pe.wait_ge(rw_ready, U * i + u + 1)
                    for t in range(TB):
                        for c in range(KC):
                            ins = pe.matmul(bank(u, 0)[:, t, :], rw[:, u, c, t * P:t * P + P], wo[:, c, :],
                                            start=(c == 0), stop=(c == KC - 1))
                    ins.then_inc(o_ready, 1)
                for u in range(U):
                    pe.wait_ge(norm2, U * i + u + 1)
                    turn(u, bank(u, 1)).then_inc(t2_ready, 1)
                for u in range(U):
                    pe.wait_ge(gmix_ready, U * i + u + 1)
                    for m in range(FC):
                        for c in range(KC):
                            ins = pe.matmul(bank(u, m // 2)[:, m % 2, :], fk[:, c, m * P:m * P + P], mix[:, u, 0, c, :],
                                            start=(c == 0), stop=(c == KC - 1))
                    ins.then_inc(hid_ready, 1)
                for u in range(U):
                    pe.wait_ge(relu_ready, U * i + u + 1)
                    for t in range(TB):
                        for c in range(KC):
                            ins = pe.matmul(bank(u, 0)[:, t, :], mix[:, u, 1, c, t * P:t * P + P], fr[:, c, :],
                                            start=(c == 0), stop=(c == KC - 1))
                    ins.then_inc(f_ready, 1)
                for u in range(U):
                    pe.wait_ge(kf_ready, U * i + u + 1)
                    for t in range(TB):
                        for m in range(FC):
                            ins = pe.matmul(bank(u, 1)[:, t, :], kf[:, u, m, t * P:t * P + P], fv[:, m, :],
                                            start=(m == 0), stop=(m == FC - 1))
                    ins.then_inc(kv_ready, 1)

        @block.scalar
        def _(act):
            act.wait_ge(edges_set, 4)
            with act.Fori(0, STEPS) as i:
                for u in range(U):
                    act.wait_ge(t1_ready, U * i + u + 1)
                    for c in range(KC):
                        ins = act.activation(h[:, u, c, 1:S + 1], bank(u, 0)[:, c, :], ACT.Identity,
                                             bias=vec(st, "L0_attn_ln1_b", c), scale=vec(st, "L0_attn_ln1_g", c))
                    ins.then_inc(h_ready, 1)
                for u in range(U):
                    act.wait_ge(negr_ready, U * i + u + 1)
                    act.activation(er[:, u], er[:, u], ACT.Exp).then_inc(er_ready, 1)
                for u in range(U):
                    act.wait_ge(args_ready, U * i + u + 1)
                    act.activation(ex[:, u], ex[:, u], ACT.Exp).then_inc(ex_ready, 1)
                for u in range(U):
                    act.wait_ge(t2_ready, U * i + u + 1)
                    for c in range(KC):
                        ins = act.activation(h[:, u, c, 1:S + 1], bank(u, 1)[:, c, :], ACT.Identity,
                                             bias=vec(st, "L0_attn_ln2_b", c), scale=vec(st, "L0_attn_ln2_g", c))
                    ins.then_inc(g_ready, 1)
                for u in range(U):
                    act.wait_ge(hid_ready, U * i + u + 1)
                    act.activation(kf[:, u].rearrange("p a b -> p (a b)"),
                                   ps[:, u].rearrange("p a b -> p (a b)"), ACT.Relu).then_inc(relu_ready, 1)
                    act.wait_ge(relu_ready, U * i + u + 1)
                    act.activation(kf[:, u], kf[:, u], ACT.Square).then_inc(kf_ready, 1)
                for u in range(U):
                    act.wait_ge(negf_ready, U * i + u + 1)
                    act.activation(es[:, u], es[:, u], ACT.Exp).then_inc(es_ready, 1)

        @block.vector
        def _(dve):
            dve.memset(h[:, :, :, 0:1], 0.0).then_inc(edges_set, 1)
            dve.memset(top[:, :, :, 0:1], NEG).then_inc(edges_set, 1)
            dve.memset(num[:, :, :, 0:1], 0.0).then_inc(edges_set, 1)
            dve.memset(den[:, :, :, 0:1], 0.0).then_inc(edges_set, 1)
            dve.wait_ge(edges_set, 4)
            with dve.Fori(0, STEPS) as i:
                s = Steps(dve, dve_steps, i, U * 30)
                for u in range(U):
                    dve.wait_ge(x_loaded[u], 16 * i + 16)
                    dve_stats(dve, st, s, x[:, u], stats, var, u, var1)
                for u in range(U):
                    dve.wait_ge(rstd1, U * i + u + 1)
                    dve_normalize(dve, nrm[:, u], x[:, u], var, rstd, u).then_inc(norm1, 1)
                for u in range(U):
                    dve.wait_ge(h_ready, U * i + u + 1)
                    s.do(dve.tensor_tensor(dif[:, u], h[:, u, :, 1:S + 1], h[:, u, :, 0:S], ALU.subtract))
                    for n, name in enumerate(("L0_attn_tm_k", "L0_attn_tm_v", "L0_attn_tm_r")):
                        for c in range(KC):
                            ins = dve.scalar_tensor_tensor(mix[:, u, n, c, :], dif[:, u, c, :], vec(st, name, c),
                                                           h[:, u, c, 0:S], ALU.mult, ALU.add)
                    ins.then_inc(mix_ready, 1)
                for u in range(U):
                    k, ww = bank(u, 1), ex[:, u]
                    dve.wait_ge(kvr_ready, U * i + u + 1)
                    dve.tensor_scalar(er[:, u], bank(u, 3), -1.0, EXP_MAX, ALU.mult, ALU.min).then_inc(negr_ready, 1)
                    for c in range(KC):
                        s.mark(dve.tensor_tensor_scan(top[:, u, c, 1:S + 1], st.wdec[:, c, :], k[:, c, :], NEG,
                                                      ALU.add, ALU.max))
                    n_top = s.n
                    s.after(n_top)
                    for c in range(KC):
                        s.mark(dve.scalar_tensor_tensor(q[:, u, c, :], k[:, c, :], vec(st, "L0_attn_time_first", c),
                                                        top[:, u, c, 0:S], ALU.add, ALU.max))
                    n_q = s.n
                    for c in range(KC):
                        dve.scalar_tensor_tensor(ww[:, 2, c, :], top[:, u, c, 0:S], st.w[:, c:c + 1],
                                                 top[:, u, c, 1:S + 1], ALU.add, ALU.subtract)
                    dve.tensor_tensor(ww[:, 3], k, top[:, u, :, 1:S + 1], ALU.subtract)
                    s.after(n_q)
                    for c in range(KC):
                        dve.scalar_tensor_tensor(ww[:, 1, c, :], k[:, c, :], vec(st, "L0_attn_time_first", c),
                                                 q[:, u, c, :], ALU.add, ALU.subtract)
                    dve.tensor_tensor(ww[:, 0], top[:, u, :, 0:S], q[:, u], ALU.subtract).then_inc(args_ready, 1)
                for u in range(U):
                    v = bank(u, 2)
                    dve.wait_ge(ex_ready, U * i + u + 1)
                    n_ev = s.mark(dve.tensor_tensor(e2bv[:, u], ex[:, u, 3], v, ALU.mult))
                    for c in range(KC):
                        s.mark(dve.tensor_tensor_scan(den[:, u, c, 1:S + 1], ex[:, u, 2, c, :], ex[:, u, 3, c, :], 0.0,
                                                      ALU.mult, ALU.add))
                    n_den = s.n
                    s.after(n_ev)
                    for c in range(KC):
                        s.mark(dve.tensor_tensor_scan(num[:, u, c, 1:S + 1], ex[:, u, 2, c, :], e2bv[:, u, c, :], 0.0,
                                                      ALU.mult, ALU.add))
                    n_num = s.n
                    n_y2 = s.mark(dve.tensor_tensor(y2[:, u], ex[:, u, 1], v, ALU.mult))
                    s.after(n_den)
                    n_q2 = s.mark(dve.tensor_tensor(q[:, u], ex[:, u, 0], den[:, u, :, 0:S], ALU.mult))
                    s.after(n_num)
                    n_y1 = s.mark(dve.tensor_tensor(y1[:, u], ex[:, u, 0], num[:, u, :, 0:S], ALU.mult))
                    s.after(n_q2)
                    n_q3 = s.mark(dve.tensor_tensor(q[:, u], q[:, u], ex[:, u, 1], ALU.add))
                    s.after(n_y1)
                    n_y3 = s.mark(dve.tensor_tensor(y1[:, u], y1[:, u], y2[:, u], ALU.add))
                    s.after(n_q3)
                    dve.wait_ge(er_ready, U * i + u + 1)
                    s.do(dve.scalar_tensor_tensor(q[:, u], er[:, u], 1.0, q[:, u], ALU.add, ALU.mult))
                    s.do(dve.reciprocal(q[:, u], q[:, u]))
                    dve.tensor_tensor(rw[:, u], y1[:, u], q[:, u], ALU.mult).then_inc(rw_ready, 1)
                for u in range(U):
                    dve.wait_ge(o_ready, U * i + u + 1)
                    s.do(dve.tensor_tensor(x2[:, u], bank(u, 0), x[:, u], ALU.add))
                    dve_stats(dve, st, s, x2[:, u], stats, var, u, var2)
                for u in range(U):
                    dve.wait_ge(rstd2, U * i + u + 1)
                    dve_normalize(dve, nrm[:, u], x2[:, u], var, rstd, u).then_inc(norm2, 1)
                for u in range(U):
                    dve.wait_ge(g_ready, U * i + u + 1)
                    s.do(dve.tensor_tensor(dif[:, u], h[:, u, :, 1:S + 1], h[:, u, :, 0:S], ALU.subtract))
                    for n, name in enumerate(("L0_attn_fm_k", "L0_attn_fm_r")):
                        for c in range(KC):
                            ins = dve.scalar_tensor_tensor(mix[:, u, n, c, :], dif[:, u, c, :], vec(st, name, c),
                                                           h[:, u, c, 0:S], ALU.mult, ALU.add)
                    ins.then_inc(gmix_ready, 1)
                    s.mark(dve.tensor_tensor(x2[:, u], x2[:, u], x[:, u], ALU.add))
                for u in range(U):
                    dve.wait_ge(f_ready, U * i + u + 1)
                    dve.tensor_scalar(es[:, u], bank(u, 0), -1.0, EXP_MAX, ALU.mult, ALU.min).then_inc(negf_ready, 1)
                for u in range(U):
                    dve.wait_ge(es_ready, U * i + u + 1)
                    s.do(dve.tensor_scalar(es[:, u], es[:, u], 1.0, None, ALU.add))
                    s.do(dve.reciprocal(es[:, u], es[:, u]))
                    dve.wait_ge(kv_ready, U * i + u + 1)
                    s.do(dve.tensor_tensor(es[:, u], es[:, u], bank(u, 1), ALU.mult))
                    s.do(dve.tensor_tensor(x2[:, u], x2[:, u], es[:, u], ALU.add))
                    dve_stats(dve, st, s, x2[:, u], stats, var, u, var3)
                for u in range(U):
                    dve.wait_ge(rstd3, U * i + u + 1)
                    dve_normalize(dve, st.res[:, bass.ds(TB * U * i + TB * u, TB), :], x2[:, u], var, rstd,
                                  u).then_inc(x1_ready, 1)
                s.close()
            dve.wait_ge(x1_ready, B)


def xattn_stage(nc, st, d, layer):
    masked = layer == 0
    pre = "x0_" if masked else "x1_"
    wq_n, wk_n, wv_n, wo_n = (("L0_xattn_w_q", "L0_xattn_w_k", "L0_xattn_w_v", "L0_xattn_w_o") if masked else
                              ("L1_xattn_Wq", "L1_xattn_Wk", "L1_xattn_Wv", "L1_xattn_Wo"))
    bq_n, bk_n = ("L0_xattn_b_q", "L0_xattn_b_k") if masked else ("L1_xattn_bq", "L1_xattn_bk")
    bv_row, bo_row = (0, 1) if masked else (2, 3)
    experts, ecols, topk = (E0, E0P, K0) if masked else (E1, E1, K1)
    rows_x, macc, base = (st.xs0, st.macc0, st.base0) if masked else (st.xs1, st.macc1, st.base1)
    slot, gate = (st.slot0, st.gate0) if masked else (st.slot1, st.gate1)
    shared_row = 0 if masked else SHARED1
    last_row = (E0 + 1) * REG0 - 1 if masked else DUMP1 - 1
    with ExitStack() as ctx:
        def sb(name, shape, dt=F32):
            return ctx.enter_context(nc.sbuf_tensor(pre + name, shape, dt))

        def sem(name):
            return st.semaphore(nc, pre + name)

        wq, wk, wv = (sb(n, [P, KC, D]) for n in ("wq", "wk", "wv"))
        wo = sb("wo", [P, KC, D])
        wg = sb("wg", [P, KC, ecols])
        cx = sb("cx", [P, U, KC, S])
        xT = sb("xT", [P, U, KC, S])
        qT = sb("qT", [P, U, KC, S])
        kT = sb("kT", [P, U, KC, S])
        vp = sb("vp", [P, U, TB, HEADS, 32])
        qm = sb("qm", [P, U, KC, HPC, S])
        nmx = sb("nmx", [P, U, TB, P])
        nmT = sb("nmT", [P, U, S])
        pt = sb("pt", [P, U, TB, KC, HPC, S])
        rec = sb("rec", [P, U, TB, HEADS])
        o32 = qm[:, :, 0, 0:QUADS, :]
        aq = qm[:, :, 1, 0:TB, :].rearrange("p u t (h r) -> p u t h r", r=DH)
        aT = qT
        xin = sb("xin", [P, U, TB, D])
        xn = sb("xn", [P, U, TB, D])
        y = xn
        stats = sb("stats", [P, U, TB, 6])
        var = sb("var", [P, U, TB, 2])
        rstd = sb("rstd", [P, U, TB])
        lg = sb("lg", [P, U, TB, ecols])
        sc = sb("sc", [P, U, TB, ecols])
        mx8 = sb("mx8", [P, U, TB, 8])
        ix8 = sb("ix8", [P, U, TB, 8], U32)
        ixf = sb("ixf", [P, U, TB, 8])
        oh = sb("oh", [P, U, TB, topk, ecols])
        hit = sb("hit", [P, U, TB, ecols], BF16)
        pos = sb("pos", [P, U, TB, ecols])
        junk = sb("junk", [P, U, TB, topk, ecols])
        at = sb("at", [P, U, TB, topk])
        gt = sb("gt", [P, U, TB, topk])
        tmp = sb("tmp", [P, U, TB, topk])
        dst = sb("dst", [P, U, TB, topk], U32)
        if masked:
            mi = sb("mi", [P, 2, TB, S], I32)
            mb = sb("mb", [P, 2, TB, S], BF16)
        else:
            wg_bf = sb("wg_bf", [P, KC, ecols], BF16)
        ps = ctx.enter_context(nc.psum_tensor(pre + "ps", [P, U, 4, 512], F32))

        def bank(u, n):
            return ps[:, u, n, :].rearrange("p (a b) -> p a b", a=2)

        def heads(u):
            return ps[:, u].rearrange("p k (a b) -> p (k a) b", a=2)

        w_loaded = sem("w_loaded")
        cx_loaded = [sem(f"cx_loaded{u}") for u in range(U)]
        preset, mask_ready, mask_loaded = sem("preset"), sem("mask_ready"), sem("mask_loaded")
        t_ready, xT_ready, qkv_ready = sem("t_ready"), sem("xT_ready"), sem("qkv_ready")
        qk_ready, vp_ready, qm_ready = sem("qk_ready"), sem("vp_ready"), sem("qm_ready")
        s_ready, max_ready = sem("s_ready"), sem("max_ready")
        mt_ready, nmT_ready = sem("mt_ready"), sem("nmT_ready")
        st_ready, pt_ready = sem("st_ready"), sem("pt_ready")
        pv_ready, o32_ready, oq_ready = sem("pv_ready"), sem("o32_ready"), sem("oq_ready")
        aq_ready, at_ready, aT_ready = sem("aq_ready"), sem("at_ready"), sem("aT_ready")
        xin_ready = sem("xin_ready")
        y_ready = sem("y_ready")
        varr, rstdr, epsr, xn_ready = sem("var_ready"), sem("rstd_ready"), sem("eps_added"), sem("xn_ready")
        rt_ready, rT_ready, lg_ready = sem("rt_ready"), sem("rT_ready"), sem("lg_ready")
        earg_ready, e_ready = sem("earg_ready"), sem("e_ready")
        hit_ready, pos_ready, dst_ready = sem("hit_ready"), sem("pos_ready"), sem("dst_ready")
        kept = sem("kept")
        sent = [sem(f"rows_sent{u}") for u in range(U)]
        stored = [sem(f"rows_stored{u}") for u in range(U)]
        steps = sem("dve_steps")
        counted, tiles_ready = sem("counted"), sem("tiles_ready")
        block = ctx.enter_context(nc.Block())
        ctx_v = d["ctx"].rearrange("(k p) n -> p k n", p=P)
        shared_v = rows_x[shared_row:shared_row + N, :].rearrange("(n p) c -> p n c", p=P)

        @block.sync
        def _(sp):
            for u in range(U):
                sp.dma_start(cx[:, u], ctx_v[:, :, S * u:S * u + S]).then_inc(cx_loaded[u], 16)
            for t, n in ((wq, wq_n), (wk, wk_n), (wv, wv_n), (wo, wo_n)):
                sp.dma_start(t[:], col(d[n])).then_inc(w_loaded, 16)
            if masked:
                sp.dma_start(mi[:, 0], d["mask"].rearrange("(t p) k -> p t k", p=P)).then_inc(mask_loaded, 16)
                sp.dma_start(mi[:, 1], d["mask_t"].rearrange("(t p) k -> p t k", p=P)).then_inc(mask_loaded, 16)
                sp.wait_ge(preset, 3)
                sp.dma_start(wg[:, :, 0:experts], col(d["L0_ffn_router_w"])).then_inc(w_loaded, 16)
            else:
                sp.dma_start(wg_bf[:], col(d["L1_ffn_gate_w"])).then_inc(w_loaded, 16)
            with sp.Fori(0, STEPS - 1) as i:
                for u in range(U):
                    sp.wait_ge(qkv_ready, U * i + u + 1)
                    sp.dma_start(cx[:, u], ctx_v[:, :, bass.ds(S * U * (i + 1) + S * u, S)]).then_inc(cx_loaded[u], 16)

        @block.gpsimd
        def _(pool):
            with pool.Fori(0, STEPS) as i:
                for u in range(U):
                    pool.tensor_copy(xin[:, u], st.res[:, bass.ds(TB * U * i + TB * u, TB), :]).then_inc(xin_ready, 1)
                for u in range(U):
                    pool_rstd(pool, st, var, rstd, u, varr, rstdr, epsr, U * i + u + 1)
                for u in range(U):
                    pool.wait_ge(xn_ready, U * i + u + 1)
                    pool.sem_inc(st.pool_passed, 1)
                    pool.tensor_copy(st.res[:, bass.ds(TB * U * i + TB * u, TB), :], xn[:, u]).then_inc(kept, 1)
                    pool.dma_start(shared_v[:, bass.ds(TB * U * i + TB * u, TB), :], xn[:, u]).then_inc(stored[u], 16)
                for u in range(U):
                    pool.wait_ge(dst_ready, U * i + u + 1)
                    pool.sem_inc(st.pool_passed, 1)
                    pool.tensor_copy(slot[:, bass.ds(TB * U * i + TB * u, TB), :], dst[:, u]).then_inc(kept, 1)
                    pool.tensor_copy(gate[:, bass.ds(TB * U * i + TB * u, TB), :], gt[:, u]).then_inc(kept, 1)
                    for t in range(TB):
                        for j in range(topk):
                            pool.indirect_dma_start(
                                out=rows_x, out_offset=bass.IndirectOffsetOnAxis(ap=dst[:, u, t, j:j + 1], axis=0),
                                in_=xn[:, u, t, :], in_offset=None, bounds_check=last_row,
                                oob_is_err=False).then_inc(sent[u], 16)
                for u in range(U):
                    pool.wait_ge(sent[u], 16 * TB * topk * (i + 1))
                    pool.wait_ge(stored[u], 16 * (i + 1))
            pool.wait_ge(kept, 3 * B)

        @block.tensor
        def _(pe):
            pe.wait_ge(w_loaded, 16 * 5)
            pe.wait_ge(preset, 3)
            if masked:
                pe.wait_ge(mask_ready, 2 * TB)
            else:
                pe.wait_ge(mask_ready, 1)

            def turn(dst, src):
                for t in range(TB):
                    for c in range(KC):
                        ins = pe.transpose(dst[:, c, t * P:t * P + P], src[:, t, c * P:c * P + P], st.ident[:])
                return ins

            with pe.Fori(0, STEPS) as i:
                for u in range(U):
                    pe.wait_ge(xin_ready, U * i + u + 1)
                    turn(bank(u, 0), xin[:, u]).then_inc(t_ready, 1)
                for u in range(U):
                    pe.wait_ge(cx_loaded[u], 16 * i + 16)
                    pe.wait_ge(xT_ready, U * i + u + 1)
                    for n, w, a in ((1, wq, xT), (2, wk, cx)):
                        for m in range(KC):
                            for c in range(KC):
                                pe.matmul(bank(u, n)[:, m, :], w[:, c, m * P:m * P + P], a[:, u, c, :],
                                          start=(c == 0), stop=(c == KC - 1))
                    for t in range(TB):
                        for c in range(KC):
                            ins = pe.matmul(bank(u, 3)[:, t, :], cx[:, u, c, t * P:t * P + P], wv[:, c, :],
                                            start=(c == 0), stop=(c == KC - 1))
                    ins.then_inc(qkv_ready, 1)
                for g in range(KC * TB):
                    m, t = g // TB, g % TB
                    for u in range(U):
                        if g == 0:
                            pe.wait_ge(qm_ready, U * i + u + 1)
                        else:
                            pe.wait_ge(max_ready, U * KC * TB * i + U * (g - 1) + u + 1)
                        for k in range(HPC):
                            if masked:
                                pe.matmul(heads(u)[:, k, :], st.identb[:], mb[:, 0, t, :], start=True, stop=False)
                            ins = pe.matmul(heads(u)[:, k, :], qm[:, u, m, k, t * P:t * P + P], kT[:, u, m, :],
                                            start=not masked, stop=True)
                        ins.then_inc(s_ready, 1)
                for u in range(U):
                    pe.wait_ge(max_ready, U * KC * TB * i + U * (KC * TB - 1) + u + 1)
                    for t in range(TB):
                        ins = pe.transpose(bank(u, 0)[:, 0, t * P:t * P + P], nmx[:, u, t, :], st.ident[:])
                    ins.then_inc(mt_ready, 1)
                for g in range(KC * TB):
                    m, t = g // TB, g % TB
                    for u in range(U):
                        if g == 0:
                            pe.wait_ge(nmT_ready, U * i + u + 1)
                        else:
                            pe.wait_ge(pt_ready, U * KC * TB * i + U * (g - 1) + u + 1)
                        for k in range(HPC):
                            if masked:
                                pe.matmul(heads(u)[:, k, :], st.identb[:], mb[:, 1, t, :], start=True, stop=False)
                            pe.matmul(heads(u)[:, k, :], kT[:, u, m, t * P:t * P + P], qm[:, u, m, k, :],
                                      start=not masked, stop=False)
                            ins = pe.matmul(heads(u)[:, k, :], st.selrow[:, m * HPC + k, :], nmT[:, u, :],
                                            start=False, stop=True)
                        ins.then_inc(st_ready, 1)
                for u in range(U):
                    pe.wait_ge(pt_ready, U * KC * TB * i + U * (KC * TB - 1) + u + 1)
                    for qd in range(QUADS):
                        for t in range(TB):
                            for j in range(4):
                                hd = 4 * qd + j
                                ins = pe.matmul(bank(u, qd // 2)[32 * j:32 * j + 32, qd % 2, :], vp[:, u, t, hd, :],
                                                pt[:, u, t, hd // HPC, hd % HPC, :], start=(t == 0), stop=(t == TB - 1))
                    ins.then_inc(pv_ready, 1)
                for u in range(U):
                    pe.wait_ge(o32_ready, U * i + u + 1)
                    for t in range(TB):
                        for qd in range(QUADS):
                            ins = pe.transpose(ps[:, u, 2 + t, qd * P:qd * P + P], o32[:, u, qd, t * P:t * P + P], st.ident[:])
                    ins.then_inc(oq_ready, 1)
                for u in range(U):
                    pe.wait_ge(aq_ready, U * i + u + 1)
                    turn(bank(u, 0), aq[:, u].rearrange("p t h r -> p t (h r)")).then_inc(at_ready, 1)
                for u in range(U):
                    pe.wait_ge(aT_ready, U * i + u + 1)
                    for t in range(TB):
                        for c in range(KC):
                            ins = pe.matmul(bank(u, 1)[:, t, :], aT[:, u, c, t * P:t * P + P], wo[:, c, :],
                                            start=(c == 0), stop=(c == KC - 1))
                    ins.then_inc(y_ready, 1)
                for u in range(U):
                    pe.wait_ge(xn_ready, U * i + u + 1)
                    turn(bank(u, 2), xn[:, u]).then_inc(rt_ready, 1)
                for u in range(U):
                    pe.wait_ge(rT_ready, U * i + u + 1)
                    for t in range(TB):
                        for c in range(KC):
                            ins = pe.matmul(bank(u, 3)[:, t, 0:ecols], xT[:, u, c, t * P:t * P + P], wg[:, c, :],
                                            start=(c == 0), stop=(c == KC - 1))
                    ins.then_inc(lg_ready, 1)
                for u in range(U):
                    pe.wait_ge(hit_ready, U * i + u + 1)
                    for t in range(TB):
                        dst_ps = bank(u, 0)[:, t, 0:ecols]
                        pe.matmul(dst_ps, st.ones[:], macc[:, u, :], start=True, stop=False)
                        if t == 1:
                            pe.matmul(dst_ps, st.ones[:], hit[:, u, 0, :], start=False, stop=False)
                        ins = pe.matmul(dst_ps, st.lower[:], hit[:, u, t, :], start=False, stop=True)
                    ins.then_inc(pos_ready, 1)
            if masked:
                pe.wait_ge(counted, 1)
                pe.matmul(bank(0, 1)[:, 0, 0:E0P], st.ones[:], macc[:, 0, :], start=True, stop=True).then_inc(tiles_ready, 1)

        @block.scalar
        def _(act):
            with act.Fori(0, STEPS) as i:
                for u in range(U):
                    act.wait_ge(t_ready, U * i + u + 1)
                    act.activation(xT[:, u], bank(u, 0), ACT.Copy).then_inc(xT_ready, 1)
                for u in range(U):
                    act.wait_ge(qkv_ready, U * i + u + 1)
                    for c in range(KC):
                        act.activation(qT[:, u, c, :], bank(u, 1)[:, c, :], ACT.Identity, bias=vec(st, bq_n, c), scale=1.0)
                    for c in range(KC):
                        ins = act.activation(kT[:, u, c, :], bank(u, 2)[:, c, :], ACT.Identity, bias=vec(st, bk_n, c),
                                             scale=1.0)
                    ins.then_inc(qk_ready, 1)
                for u in range(U):
                    act.wait_ge(mt_ready, U * i + u + 1)
                    act.activation(nmT[:, u, :], bank(u, 0)[:, 0, :], ACT.Copy).then_inc(nmT_ready, 1)
                for g in range(KC * TB):
                    m, t = g // TB, g % TB
                    for u in range(U):
                        act.wait_ge(st_ready, U * KC * TB * i + U * g + u + 1)
                        act.activation(pt[:, u, t, m].rearrange("p k q -> p (k q)"),
                                       ps[:, u].rearrange("p k q -> p (k q)"), ACT.Exp, scale=SCALE).then_inc(pt_ready, 1)
                for u in range(U):
                    act.wait_ge(pv_ready, U * i + u + 1)
                    act.activation(o32[:, u].rearrange("p k q -> p (k q)"),
                                   ps[:, u, 0:2].rearrange("p k q -> p (k q)"), ACT.Copy).then_inc(o32_ready, 1)
                for u in range(U):
                    act.wait_ge(at_ready, U * i + u + 1)
                    act.activation(aT[:, u], bank(u, 0), ACT.Copy).then_inc(aT_ready, 1)
                for u in range(U):
                    act.wait_ge(rt_ready, U * i + u + 1)
                    act.activation(xT[:, u], bank(u, 2), ACT.Copy).then_inc(rT_ready, 1)
                for u in range(U):
                    act.wait_ge(earg_ready, U * i + u + 1)
                    if masked:
                        act.activation(tmp[:, u, :, 0:1], tmp[:, u, :, 0:1], ACT.Exp).then_inc(e_ready, 1)
                    else:
                        act.activation(sc[:, u], sc[:, u], ACT.Exp).then_inc(e_ready, 1)

        @block.vector
        def _(dve):
            dve.memset(vp[:, :, :, :, DH:32], 0.0).then_inc(preset, 1)
            dve.memset(nmx[:], 0.0).then_inc(preset, 1)
            dve.memset(wg[:], 0.0).then_inc(preset, 1)
            dve.wait_ge(preset, 3)
            dve.memset(vp[:, :, :, :, DH:DH + 1], 1.0).then_inc(preset, 1)
            if masked:
                dve.memset(lg[:], NEG).then_inc(preset, 1)
                dve.wait_ge(preset, 5)
                dve.wait_ge(mask_loaded, 32)
                for n in range(2):
                    for t in range(TB):
                        dve.tensor_scalar(mb[:, n, t, :], mi[:, n, t, :], 0, NEG, ALU.is_equal,
                                          ALU.mult).then_inc(mask_ready, 1)
            else:
                dve.wait_ge(preset, 4)
                dve.wait_ge(w_loaded, 16 * 5)
                dve.tensor_copy(wg[:], wg_bf[:]).then_inc(mask_ready, 1)
            with dve.Fori(0, STEPS) as i:
                s = Steps(dve, steps, i, U * DVE_STEPS[layer])
                for u in range(U):
                    dve.wait_ge(xin_ready, U * i + u + 1)
                    n_xb = s.mark(dve.tensor_tensor(y[:, u], xin[:, u],
                                                    st.rows[:, bo_row:bo_row + 1, :].to_broadcast([P, TB, D]), ALU.add))
                for u in range(U):
                    dve.wait_ge(qkv_ready, U * i + u + 1)
                    for t in range(TB):
                        ins = dve.tensor_tensor(vp[:, u, t, :, 0:DH], bank(u, 3)[:, t, :].rearrange("p (h r) -> p h r", r=DH),
                                                st.rows[:, bv_row, :].rearrange("p (h r) -> p h r", r=DH), ALU.add)
                    ins.then_inc(vp_ready, 1)
                    dve.wait_ge(qk_ready, U * i + u + 1)
                    for m in range(KC):
                        for k in range(HPC):
                            ins = dve.tensor_scalar(qm[:, u, m, k, :], qT[:, u, m, :], st.hmask[:, k:k + 1], None, ALU.mult)
                    ins.then_inc(qm_ready, 1)
                for g in range(KC * TB):
                    m, t = g // TB, g % TB
                    for u in range(U):
                        dve.wait_ge(s_ready, U * KC * TB * i + U * g + u + 1)
                        dve.tensor_reduce(nmx[:, u, t, m * HPC:m * HPC + HPC], heads(u), AX.X, ALU.max,
                                          negate=True).then_inc(max_ready, 1)
                for u in range(U):
                    oq = ps[:, u, 2:4].rearrange("p t (h r) -> p t h r", r=32)
                    dve.wait_ge(oq_ready, U * i + u + 1)
                    s.do(dve.reciprocal(rec[:, u], oq[:, :, :, DH]))
                    for t in range(TB):
                        ins = dve.tensor_tensor(aq[:, u, t], oq[:, t, :, 0:DH],
                                                rec[:, u, t].unsqueeze(2).to_broadcast([P, HEADS, DH]), ALU.mult)
                    ins.then_inc(aq_ready, 1)
                for u in range(U):
                    dve.wait_ge(y_ready, U * i + u + 1)
                    s.do(dve.tensor_tensor(y[:, u], y[:, u], bank(u, 1), ALU.add))
                    dve_stats(dve, st, s, y[:, u], stats, var, u, varr)
                for u in range(U):
                    dve.wait_ge(rstdr, U * i + u + 1)
                    dve_normalize(dve, xn[:, u], y[:, u], var, rstd, u).then_inc(xn_ready, 1)
                for u in range(U):
                    logits = bank(u, 3)[:, :, 0:experts]
                    dve.wait_ge(lg_ready, U * i + u + 1)
                    if masked:
                        s.do(dve.tensor_copy(lg[:, u, :, 0:experts], logits))
                    else:
                        dve.tensor_scalar(sc[:, u], logits, -1.0, EXP_MAX, ALU.mult, ALU.min).then_inc(earg_ready, 1)
                        dve.wait_ge(e_ready, U * i + u + 1)
                        s.do(dve.tensor_scalar(sc[:, u], sc[:, u], 1.0, None, ALU.add))
                        s.do(dve.reciprocal(sc[:, u], sc[:, u]))
                        s.do(dve.tensor_tensor(lg[:, u], sc[:, u],
                                               st.ebias[:].unsqueeze(1).to_broadcast([P, TB, E1]), ALU.add))
                    dve.sem_inc(st.dve_passed, 1)
                    for t in range(TB):
                        n_max = s.mark(dve.max(mx8[:, u, t, :], lg[:, u, t, :]))
                    s.after(n_max)
                    dve.sem_inc(st.dve_passed, 1)
                    for t in range(TB):
                        n_max = s.mark(dve.max_index(ix8[:, u, t, :], mx8[:, u, t, :], lg[:, u, t, :]))
                    s.after(n_max)
                    if masked:
                        dve.tensor_tensor(tmp[:, u, :, 0], mx8[:, u, :, 1], mx8[:, u, :, 0], ALU.subtract).then_inc(earg_ready, 1)
                    s.do(dve.tensor_copy(ixf[:, u], ix8[:, u]))
                    for t in range(TB):
                        for j in range(topk):
                            s.mark(dve.tensor_scalar(oh[:, u, t, j, :], st.iota[:, 0:ecols], ixf[:, u, t, j:j + 1], None,
                                                     ALU.is_equal))
                    s.after(s.n)
                    with nc.allow_low_precision(reason="zeros and ones are exact in bfloat16"):
                        for t in range(TB):
                            s.mark(dve.tensor_reduce(hit[:, u, t, :], oh[:, u, t].rearrange("p j e -> p e j"), AX.X,
                                                     ALU.add))
                    s.after(s.n)
                    if u == 1:
                        dve.wait_ge(pos_ready, U * i + 1)
                    s.do(dve.tensor_tensor(macc[:, 1 - u, :], macc[:, u, :], hit[:, u, 0, :], ALU.add))
                    s.do(dve.tensor_tensor(macc[:, 1 - u, :], macc[:, 1 - u, :], hit[:, u, 1, :], ALU.add))
                    dve.sem_inc(hit_ready, 1)
                    if masked:
                        dve.wait_ge(e_ready, U * i + u + 1)
                        s.do(dve.tensor_scalar(tmp[:, u, :, 1], tmp[:, u, :, 0], 1.0, None, ALU.add))
                        s.do(dve.reciprocal(gt[:, u, :, 0], tmp[:, u, :, 1]))
                        s.do(dve.tensor_tensor(gt[:, u, :, 1], gt[:, u, :, 0], tmp[:, u, :, 0], ALU.mult))
                    else:
                        for t in range(TB):
                            s.mark(dve.tensor_tensor(junk[:, u, t], oh[:, u, t],
                                                     sc[:, u, t, :].unsqueeze(1).to_broadcast([P, topk, ecols]), ALU.mult))
                        s.after(s.n)
                        s.do(dve.tensor_reduce(gt[:, u], junk[:, u], AX.X, ALU.add))
                        s.do(dve.tensor_reduce(tmp[:, u, :, 0], gt[:, u], AX.X, ALU.add))
                        s.do(dve.tensor_scalar(tmp[:, u, :, 0], tmp[:, u, :, 0], 1e-12, None, ALU.max))
                        s.do(dve.reciprocal(tmp[:, u, :, 1], tmp[:, u, :, 0]))
                        s.do(dve.tensor_tensor(gt[:, u], gt[:, u], tmp[:, u, :, 1:2].to_broadcast([P, TB, topk]), ALU.mult))
                    dve.wait_ge(pos_ready, U * i + u + 1)
                    place = bank(u, 0)[:, :, 0:ecols]
                    s.do(dve.tensor_tensor(pos[:, u], place, base[:].unsqueeze(1).to_broadcast([P, TB, ecols]), ALU.add))
                    if not masked:
                        s.do(dve.tensor_scalar(lg[:, u], place, CAP1 - 0.5, FAR, ALU.is_gt, ALU.mult))
                        s.do(dve.tensor_tensor(pos[:, u], pos[:, u], lg[:, u], ALU.add))
                    for t in range(TB):
                        s.mark(dve.tensor_tensor(junk[:, u, t], oh[:, u, t],
                                                 pos[:, u, t, :].unsqueeze(1).to_broadcast([P, topk, ecols]), ALU.mult))
                    s.after(s.n)
                    s.do(dve.tensor_reduce(at[:, u], junk[:, u], AX.X, ALU.add))
                    if not masked:
                        s.do(dve.tensor_scalar(at[:, u], at[:, u], float(DUMP1), None, ALU.min))
                        s.do(dve.tensor_scalar(tmp[:, u], at[:, u], DUMP1 - 0.5, None, ALU.is_lt))
                        s.do(dve.tensor_tensor(gt[:, u], gt[:, u], tmp[:, u], ALU.mult))
                    dve.tensor_copy(dst[:, u], at[:, u]).then_inc(dst_ready, 1)
                s.close()
            if masked:
                dve.wait_ge(pos_ready, B)
                dve.sem_inc(counted, 1)
                dve.wait_ge(tiles_ready, 1)
                dve.tensor_copy(st.count0[:], bank(0, 1)[:, 0, 0:E0P]).then_inc(counted, 1)
                dve.tensor_scalar(st.limits[:], st.iota[:, 1:TILES_SHARED], float(S), None, ALU.mult).then_inc(counted, 1)
                dve.wait_ge(counted, 3)
                dve.tensor_tensor(st.over[:], st.count0[:].unsqueeze(2).to_broadcast([P, E0P, TILES_SHARED - 1]),
                                  st.limits[:].unsqueeze(1).to_broadcast([P, E0P, TILES_SHARED - 1]),
                                  ALU.is_gt).then_inc(counted, 1)
                dve.wait_ge(counted, 4)
                dve.tensor_reduce(st.ntile[:], st.over[:], AX.X, ALU.add).then_inc(counted, 1)
                dve.wait_ge(counted, 5)
                dve.tensor_scalar(st.ntile[:], st.ntile[:], 1.0, None, ALU.add).then_inc(counted, 1)
                dve.wait_ge(counted, 6)
                dve.memset(st.first[:, 0:1], 0.0).then_inc(counted, 1)
                dve.memset(st.first[:, 1:2], float(TILES_SHARED)).then_inc(counted, 1)
                dve.tensor_tensor_scan(st.first[:, 2:2 + E0], st.ntile[:, 0:E0], st.zero[:, 0:E0], float(TILES_SHARED),
                                       ALU.add, ALU.add).then_inc(counted, 1)
                dve.wait_ge(counted, 9)
                dve.tensor_copy(st.tile0[:], st.first[:]).then_inc(counted, 1)
                dve.memset(st.tiles0[:, 0:1], TILES_SHARED).then_inc(counted, 1)
                dve.tensor_copy(st.tiles0[:, 1:1 + E0], st.ntile[:, 0:E0]).then_inc(counted, 1)
                dve.tensor_tensor(st.count0[:], st.count0[:], st.base0[:], ALU.add).then_inc(counted, 1)
                dve.wait_ge(counted, 13)
                dve.tensor_copy(st.end0[:], st.count0[:]).then_inc(counted, 1)
                dve.wait_ge(counted, 14)


def moe0_stage(nc, st, d):
    with ExitStack() as ctx:
        def sb(name, shape, dt=F32):
            return ctx.enter_context(nc.sbuf_tensor("m0_" + name, shape, dt))

        def sem(name):
            return st.semaphore(nc, "m0_" + name)

        wgt = sb("wgt", [P, 2, KC, F])
        wup = sb("wup", [P, 2, KC, F])
        wdn = sb("wdn", [P, 2, FC, D])
        x = sb("x", [P, TB, D])
        xT = sb("xT", [P, KC, S])
        sg = sb("sg", [P, 4, S])
        h = sb("h", [P, FC, S])
        y = sb("y", [P, TB, D])
        gu = ctx.enter_context(nc.psum_tensor("m0_gu", [P, 4, 2, S], F32))
        xp = ctx.enter_context(nc.psum_tensor("m0_xp", [P, KC, S], F32))
        yp = ctx.enter_context(nc.psum_tensor("m0_yp", [P, TB, 512], F32))
        w_loaded = [sem(f"w_loaded{b}") for b in range(2)]
        padded, x_loaded, t_ready, xT_ready = sem("rows_padded"), sem("x_loaded"), sem("t_ready"), sem("xT_ready")
        gu_ready, silu_ready, h_ready = sem("gu_ready"), sem("silu_ready"), sem("h_ready")
        down_done, y_ready, y_stored = sem("down_done"), sem("y_ready"), sem("y_stored")
        y_free = sem("y_free")
        block = ctx.enter_context(nc.Block())

        def tiles_of(eng, e):
            return (eng.value_load(st.tile0[0:1, bass.ds(e, 1)], min_val=0, max_val=MAX_TILES),
                    eng.value_load(st.tiles0[0:1, bass.ds(e, 1)], min_val=1, max_val=TILES_SHARED))

        def rows(dram, e, k):
            return dram[bass.ds(e * REG0 + k * S, S), :].rearrange("(n p) c -> p n c", p=P)

        def load_weights(eng, b, e):
            for w, n in ((wgt, "L0_ffn_w_gate"), (wup, "L0_ffn_w_up"), (wdn, "L0_ffn_w_down")):
                src = d[n].rearrange("e (k p) n -> p e k n", p=P)
                eng.dma_start(w[:, b], src[:, bass.ds(e, 1)].squeeze(1)).then_inc(w_loaded[b], 16)

        @block.sync
        def _(sp):
            for e in range(E0):
                end = sp.value_load(st.end0[0:1, e:e + 1], min_val=0, max_val=(E0 + 1) * REG0 - S)
                sp.dma_start(st.xs0[bass.ds(end, S), :].rearrange("(n p) c -> p n c", p=P),
                             st.zero[:].unsqueeze(1).to_broadcast([P, TB, D])).then_inc(padded, 16)
            sp.wait_ge(padded, 16 * E0)
            with sp.Fori(0, (E0 + 1) // 2) as q:
                for b in range(2):
                    e = 2 * q + b
                    first, count = tiles_of(sp, e)
                    with sp.Fori(0, count) as k:
                        t = first + k
                        sp.wait_ge(t_ready, t + 1)
                        sp.dma_start(x[:], rows(st.xs0, e, k)).then_inc(x_loaded, 16)

        @block.gpsimd
        def _(pool):
            pool.sem_inc(y_free, 1)
            pool.wait_ge(st.ys0_zeroed, 16 * ((E0 + 1) * REG0 - N) // ZERO_ROWS)
            with pool.Fori(0, (E0 + 1) // 2) as q:
                for b in range(2):
                    e = 2 * q + b
                    first, count = tiles_of(pool, e)
                    with pool.Fori(0, count) as k:
                        t = first + k
                        pool.wait_ge(y_ready, t + 2)
                        pool.sem_inc(st.pool_passed, 1)
                        pool.dma_start(rows(st.ys0, e, k), y[:]).then_inc(y_stored, 16)
                        pool.wait_ge(y_stored, 16 * t + 16)
                        pool.sem_inc(y_free, 1)

        @block.tensor
        def _(pe):
            pe.sem_inc(t_ready, 1)
            with pe.Fori(0, (E0 + 1) // 2) as q:
                for b in range(2):
                    e = 2 * q + b
                    first, count = tiles_of(pe, e)
                    pe.wait_ge(w_loaded[b], 16 * 3 * (q + 1))
                    pe.sem_inc(st.pe_passed, 1)
                    with pe.Fori(0, count) as k:
                        t = first + k
                        pe.wait_ge(x_loaded, 16 * t + 16)
                        for n in range(TB):
                            for c in range(KC):
                                ins = pe.transpose(xp[:, c, n * P:n * P + P], x[:, n, c * P:c * P + P], st.ident[:])
                        ins.then_inc(t_ready, 1)
                        pe.wait_ge(xT_ready, t + 1)

                        def down(m):
                            pe.wait_ge(h_ready, FC * t + m + 1)
                            if m == 0:
                                pe.wait_ge(y_ready, t + 1)
                            for n in range(TB):
                                ins = pe.matmul(yp[:, n, 0:D], h[:, m, n * P:n * P + P], wdn[:, b, m, :],
                                                start=(m == 0), stop=(m == FC - 1))
                            return ins

                        for m in range(FC):
                            if m >= 4:
                                pe.wait_ge(h_ready, FC * t + m - 3)
                            for n, w in enumerate((wgt, wup)):
                                for c in range(KC):
                                    ins = pe.matmul(gu[:, m % 4, n, :], w[:, b, c, m * P:m * P + P], xT[:, c, :],
                                                    start=(c == 0), stop=(c == KC - 1))
                            ins.then_inc(gu_ready, 1)
                            if m >= 2:
                                down(m - 2)
                        down(FC - 2)
                        down(FC - 1).then_inc(down_done, 1)

        @block.scalar
        def _(act):
            for b in range(2):
                load_weights(act, b, b)

            def pair(q, more):
                for b in range(2):
                    e = 2 * q + b
                    first, count = tiles_of(act, e)
                    with act.Fori(0, count) as k:
                        t = first + k
                        act.wait_ge(t_ready, t + 2)
                        act.activation(xT[:], xp[:], ACT.Copy).then_inc(xT_ready, 1)
                        for m in range(FC):
                            act.wait_ge(gu_ready, FC * t + m + 1)
                            act.activation(sg[:, m % 4, :], gu[:, m % 4, 0, :], ACT.Silu).then_inc(silu_ready, 1)
                    if more:
                        act.wait_ge(down_done, first + count)
                        load_weights(act, b, e + 2)

            with act.Fori(0, (E0 + 1) // 2 - 1) as q:
                pair(q, True)
            pair((E0 + 1) // 2 - 1, False)

        @block.vector
        def _(dve):
            dve.sem_inc(y_ready, 1)
            with dve.Fori(0, (E0 + 1) // 2) as q:
                for b in range(2):
                    e = 2 * q + b
                    first, count = tiles_of(dve, e)
                    with dve.Fori(0, count) as k:
                        t = first + k
                        for m in range(FC):
                            dve.wait_ge(silu_ready, FC * t + m + 1)
                            dve.tensor_tensor(h[:, m, :], sg[:, m % 4, :], gu[:, m % 4, 1, :], ALU.mult).then_inc(h_ready, 1)
                        dve.wait_ge(down_done, t + 1)
                        dve.wait_ge(y_free, t + 1)
                        dve.tensor_copy(y[:], yp[:, :, 0:D]).then_inc(y_ready, 1)


def attn1_stage(nc, st, d):
    with ExitStack() as ctx:
        def sb(name, shape, dt=F32):
            return ctx.enter_context(nc.sbuf_tensor("a1_" + name, shape, dt))

        def sem(name):
            return st.semaphore(nc, "a1_" + name)

        w = [sb(n, [P, KC, D]) for n in ("wq", "wk", "wv")]
        wp = sb("wp", [P, KC, D])
        qkv = sb("qkv", [P, 3, KC, N])
        sh = sb("sh", [P, U, TB, D])
        yr = sb("yr", [P, U, TB, K0, D])
        idx = sb("idx", [P, U, TB, K0], U32)
        xn = sb("xn", [P, U, TB, D])
        xT = sb("xT", [P, U, KC, S])
        bst = sb("bst", [P, 3, KC, B, 6])
        bnv = sb("bnv", [P, 3, KC, 2])
        bsc = sb("bsc", [P, 3, KC])
        bbi = sb("bbi", [P, 3, KC])
        sig = sb("sig", [P, U, 3, KC, S])
        vt = sb("vt", [P, U, TB, D])
        vvb = sb("vvb", [P, U, KC, P])
        oT = sb("oT", [P, U, KC, S])
        stats = sb("stats", [P, U, TB, 6])
        var = sb("var", [P, U, TB, 2])
        rstd = sb("rstd", [P, U, TB])
        ps = ctx.enter_context(nc.psum_tensor("a1_ps", [P, U, 4, 512], F32))

        def bank(u, n):
            return ps[:, u, n, :].rearrange("p (a b) -> p a b", a=2)

        w_loaded = sem("w_loaded")
        sh_loaded, yr_loaded = [sem(f"sh_loaded{u}") for u in range(U)], [sem(f"yr_loaded{u}") for u in range(U)]
        idx_ready, summed = sem("idx_ready"), sem("summed")
        varr, rstdr, epsr, xn_ready = sem("var_ready"), sem("rstd_ready"), sem("eps_added"), sem("xn_ready")
        var2, rstd2, eps2, out_ready = sem("var2_ready"), sem("rstd2_ready"), sem("eps2_added"), sem("out_ready")
        t_ready, xT_ready, proj_ready = sem("t_ready"), sem("xT_ready"), sem("proj_ready")
        kept, counted = sem("proj_kept"), sem("proj_counted")
        bn_steps, bn_eps, bn_rstd, bn_ready = sem("bn_steps"), sem("bn_eps_added"), sem("bn_rstd_ready"), sem("bn_ready")
        sig_ready, qk_ready, vt_ready, vtok_ready = sem("sig_ready"), sem("qk_ready"), sem("vt_ready"), sem("vtok_ready")
        vv_ready, vvb_ready = sem("vv_ready"), sem("vvb_ready")
        o_ready, oT_ready, y_ready = sem("o_ready"), sem("oT_ready"), sem("y_ready")
        steps, steps2 = sem("dve_steps"), sem("dve_steps2")
        block = ctx.enter_context(nc.Block())
        sh_v = st.ys0[0:N, :].rearrange("(n p) c -> p n c", p=P)

        @block.sync
        def _(sp):
            for u in range(U):
                sp.dma_start(sh[:, u], sh_v[:, TB * u:TB * u + TB, :]).then_inc(sh_loaded[u], 16)
            for t, n in zip(w + [wp], ("L1_attn_Wq", "L1_attn_Wk", "L1_attn_Wv", "L1_attn_Wp")):
                sp.dma_start(t[:], col(d[n])).then_inc(w_loaded, 16)
            with sp.Fori(0, STEPS - 1) as i:
                for u in range(U):
                    sp.wait_ge(xn_ready, U * i + u + 1)
                    sp.dma_start(sh[:, u], sh_v[:, bass.ds(TB * U * (i + 1) + TB * u, TB), :]).then_inc(sh_loaded[u], 16)

        @block.gpsimd
        def _(pool):
            def gather(i, u, start):
                pool.tensor_copy(idx[:, u], st.slot0[:, bass.ds(TB * U * i + TB * u, TB), :]).then_inc(idx_ready, 1)
                pool.wait_ge(idx_ready, start)
                pool.sem_inc(st.pool_passed, 1)
                for t in range(TB):
                    for j in range(K0):
                        pool.indirect_dma_start(
                            out=yr[:, u, t, j, :], out_offset=None, in_=st.ys0,
                            in_offset=bass.IndirectOffsetOnAxis(ap=idx[:, u, t, j:j + 1], axis=0)).then_inc(yr_loaded[u], 16)

            for u in range(U):
                gather(0, u, u + 1)
            with pool.Fori(0, STEPS - 1) as i:
                for u in range(U):
                    pool_rstd(pool, st, var, rstd, u, varr, rstdr, epsr, U * i + u + 1)
                for u in range(U):
                    pool.wait_ge(summed, U * i + u + 1)
                    pool.sem_inc(st.pool_passed, 1)
                    gather(i + 1, u, U * (i + 1) + u + 1)
            for u in range(U):
                pool_rstd(pool, st, var, rstd, u, varr, rstdr, epsr, U * (STEPS - 1) + u + 1)
            pool.wait_ge(bn_steps, 6)
            pool.tensor_tensor(bsc[:], bnv[:, :, :, 1], st.eps[:, 0:6].rearrange("p (a b) -> p a b", b=KC), ALU.add).then_inc(bn_eps, 1)
            pool.wait_ge(bn_eps, 1)
            pool.tensor_tensor(bsc[:], bsc[:], st.neghalf[:, 0:6].rearrange("p (a b) -> p a b", b=KC), ALU.pow).then_inc(bn_rstd, 1)
            with pool.Fori(0, STEPS) as i:
                for u in range(U):
                    pool_rstd(pool, st, var, rstd, u, var2, rstd2, eps2, U * i + u + 1)

        @block.tensor
        def _(pe):
            pe.wait_ge(w_loaded, 16 * 4)

            def turn(dst, src):
                for t in range(TB):
                    for c in range(KC):
                        ins = pe.transpose(dst[:, c, t * P:t * P + P], src[:, t, c * P:c * P + P], st.ident[:])
                return ins

            with pe.Fori(0, STEPS) as i:
                for u in range(U):
                    pe.wait_ge(xn_ready, U * i + u + 1)
                    turn(bank(u, 0), xn[:, u]).then_inc(t_ready, 1)
                for u in range(U):
                    pe.wait_ge(xT_ready, U * i + u + 1)
                    pe.wait_ge(kept, U * i + 1)
                    for n in range(3):
                        for m in range(KC):
                            for c in range(KC):
                                ins = pe.matmul(bank(u, 1 + n)[:, m, :], w[n][:, c, m * P:m * P + P], xT[:, u, c, :],
                                                start=(c == 0), stop=(c == KC - 1))
                    ins.then_inc(proj_ready, 1)
            pe.wait_ge(kept, B + 1)
            with pe.Fori(0, STEPS) as i:
                for u in range(U):
                    pe.wait_ge(sig_ready, U * i + u + 1)
                    for c in range(KC):
                        for t in range(TB):
                            ins = pe.transpose(bank(u, 0)[:, t, c * P:c * P + P], sig[:, u, 2, c, t * P:t * P + P], st.ident[:])
                    ins.then_inc(vt_ready, 1)
                for u in range(U):
                    pe.wait_ge(vtok_ready, U * i + u + 1)
                    for m in range(KC):
                        for t in range(TB):
                            v = vt[:, u, t, m * P:m * P + P]
                            ins = pe.matmul(bank(u, 1)[:, m, 0:P], v, v, start=(t == 0), stop=(t == TB - 1))
                    ins.then_inc(vv_ready, 1)
                for u in range(U):
                    pe.wait_ge(vvb_ready, U * i + u + 1)
                    pe.wait_ge(qk_ready, U * i + u + 1)
                    for m in range(KC):
                        ins = pe.matmul(bank(u, 2)[:, m, :], vvb[:, u, m, :], sig[:, u, 0, m, :], start=True, stop=True)
                    ins.then_inc(o_ready, 1)
                for u in range(U):
                    pe.wait_ge(oT_ready, U * i + u + 1)
                    for t in range(TB):
                        for c in range(KC):
                            ins = pe.matmul(bank(u, 3)[:, t, :], oT[:, u, c, t * P:t * P + P], wp[:, c, :],
                                            start=(c == 0), stop=(c == KC - 1))
                    ins.then_inc(y_ready, 1)

        @block.scalar
        def _(act):
            act.sem_inc(kept, 1)
            with act.Fori(0, STEPS) as i:
                for u in range(U):
                    act.wait_ge(t_ready, U * i + u + 1)
                    act.activation(xT[:, u], bank(u, 0), ACT.Copy).then_inc(xT_ready, 1)
                for u in range(U):
                    act.wait_ge(proj_ready, U * i + u + 1)
                    act.sem_inc(st.act_passed, 1)
                    for n in range(3):
                        ins = act.activation(qkv[:, n, :, bass.ds(S * U * i + S * u, S)], bank(u, 1 + n), ACT.Copy)
                    ins.then_inc(kept, 1)
            act.wait_ge(bn_ready, 1)
            act.wait_ge(kept, B + 1)
            with act.Fori(0, STEPS) as i:
                for u in range(U):
                    for n in (2, 0, 1):
                        for m in range(KC):
                            ins = act.activation(sig[:, u, n, m, :], qkv[:, n, m, bass.ds(S * U * i + S * u, S)], ACT.Sigmoid,
                                                 bias=bbi[:, n, m:m + 1], scale=bsc[:, n, m:m + 1])
                    ins.then_inc(sig_ready, 1)
                for u in range(U):
                    act.wait_ge(vt_ready, U * i + u + 1)
                    act.activation(vt[:, u], bank(u, 0), ACT.Copy).then_inc(vtok_ready, 1)
                for u in range(U):
                    act.wait_ge(o_ready, U * i + u + 1)
                    act.activation(oT[:, u], bank(u, 2), ACT.Copy).then_inc(oT_ready, 1)

        @block.vector
        def _(dve):
            with dve.Fori(0, STEPS) as i:
                s = Steps(dve, steps, i, U * 8)
                for u in range(U):
                    blk = TB * U * i + TB * u
                    dve.wait_ge(sh_loaded[u], 16 * (i + 1))
                    s.do(dve.tensor_tensor(sh[:, u], sh[:, u], st.res[:, bass.ds(blk, TB), :], ALU.add))
                    dve.wait_ge(yr_loaded[u], 16 * TB * K0 * (i + 1))
                    for j in range(K0):
                        for t in range(TB):
                            n_sum = s.mark(dve.scalar_tensor_tensor(sh[:, u, t, :], yr[:, u, t, j, :],
                                                                    st.gate0[:, bass.ds(blk + t, 1), j:j + 1].squeeze(1),
                                                                    sh[:, u, t, :], ALU.mult, ALU.add))
                        s.after(n_sum)
                    dve.sem_inc(summed, 1)
                    dve_stats(dve, st, s, sh[:, u], stats, var, u, varr)
                for u in range(U):
                    dve.wait_ge(rstdr, U * i + u + 1)
                    s.mark(dve_normalize(dve, xn[:, u], sh[:, u], var, rstd, u))
                    s.after(s.n)
                    dve.sem_inc(st.dve_passed, 1)
                    dve.tensor_copy(st.res[:, bass.ds(TB * U * i + TB * u, TB), :], xn[:, u]).then_inc(xn_ready, 1)
                for u in range(U):
                    dve.wait_ge(kept, U * i + u + 2)
                    dve.sem_inc(st.dve_passed, 1)
                    for n in range(3):
                        for m in range(KC):
                            ins = dve.bn_stats(bst[:, n, m, bass.ds(U * i + u, 1), :].squeeze(1), qkv[:, n, m, bass.ds(S * U * i + S * u, S)])
                    ins.then_inc(counted, 1)
                s.close()
            dve.wait_ge(counted, B)
            for n in range(3):
                for m in range(KC):
                    dve.bn_aggr(bnv[:, n, m, :], bst[:, n, m].rearrange("p b s -> p (b s)")).then_inc(bn_steps, 1)
            dve.wait_ge(bn_rstd, 1)
            g0, b0 = 2 * VECS.index("L1_attn_gq"), 2 * VECS.index("L1_attn_bq")
            g6 = st.vecs[:, g0:g0 + 6].rearrange("p (a b) -> p a b", b=KC)
            b6 = st.vecs[:, b0:b0 + 6].rearrange("p (a b) -> p a b", b=KC)
            dve.tensor_tensor(bsc[:], bsc[:], g6, ALU.mult).then_inc(bn_steps, 1)
            dve.wait_ge(bn_steps, 7)
            dve.tensor_tensor(bbi[:], bsc[:], bnv[:, :, :, 0], ALU.mult).then_inc(bn_steps, 1)
            dve.wait_ge(bn_steps, 8)
            dve.tensor_tensor(bbi[:], b6, bbi[:], ALU.subtract).then_inc(bn_steps, 1)
            dve.tensor_scalar(bsc[:], bsc[:], 4.0, None, ALU.mult).then_inc(bn_steps, 1)
            dve.wait_ge(bn_steps, 10)
            dve.tensor_scalar(bbi[:], bbi[:], -1.0, 4.0, ALU.add, ALU.mult).then_inc(bn_ready, 1)
            dve.sem_inc(out_ready, 1)
            with dve.Fori(0, STEPS) as i:
                s = Steps(dve, steps2, i, U * 4)
                for u in range(U):
                    dve.wait_ge(sig_ready, U * i + u + 1)
                    dve.tensor_tensor(sig[:, u, 0], sig[:, u, 0], sig[:, u, 1], ALU.mult).then_inc(qk_ready, 1)
                dve.wait_ge(out_ready, U * i + 1)
                for u in range(U):
                    s.mark(dve.tensor_tensor(xn[:, u], st.res[:, bass.ds(TB * U * i + TB * u, TB), :],
                                             st.rows[:, 4:5, :].to_broadcast([P, TB, D]), ALU.add))
                for u in range(U):
                    dve.wait_ge(vv_ready, U * i + u + 1)
                    dve.tensor_tensor(vvb[:, u], bank(u, 1)[:, :, 0:P],
                                      st.blk[:].unsqueeze(1).to_broadcast([P, KC, P]), ALU.mult).then_inc(vvb_ready, 1)
                for u in range(U):
                    dve.wait_ge(y_ready, U * i + u + 1)
                    s.after(s.n)
                    s.do(dve.tensor_tensor(xn[:, u], xn[:, u], bank(u, 3), ALU.add))
                    dve_stats(dve, st, s, xn[:, u], stats, var, u, var2)
                for u in range(U):
                    dve.wait_ge(rstd2, U * i + u + 1)
                    dve_normalize(dve, st.res[:, bass.ds(TB * U * i + TB * u, TB), :], xn[:, u], var, rstd,
                                  u).then_inc(out_ready, 1)
                s.close()
            dve.wait_ge(out_ready, B + 1)


def moe1_stage(nc, st, d):
    with ExitStack() as ctx:
        def sb(name, shape, dt=F32):
            return ctx.enter_context(nc.sbuf_tensor("m1_" + name, shape, dt))

        def sem(name):
            return st.semaphore(nc, "m1_" + name)

        w1_all = sb("w1_all", [P, TILES1, KC, I1], BF16)
        w3_all = sb("w3_all", [P, TILES1, KC, I1], BF16)
        w2_all = sb("w2_all", [P, TILES1, D], BF16)
        w1, w3 = sb("w1", [P, U, KC, I1]), sb("w3", [P, U, KC, I1])
        w2 = sb("w2", [P, U, D])
        x = sb("x", [P, U, TB, D])
        xT = sb("xT", [P, U, KC, S])
        sg = sb("sg", [P, U, S])
        h = sb("h", [P, U, S])
        y = sb("y", [P, U, TB, D])
        ps = ctx.enter_context(nc.psum_tensor("m1_ps", [P, U, 4, 512], F32))

        def bank(u, n):
            return ps[:, u, n, :].rearrange("p (a b) -> p a b", a=2)

        w_loaded, w_ready = sem("w_loaded"), sem("w_ready")
        x_loaded, y_stored = [sem(f"x_loaded{u}") for u in range(U)], [sem(f"y_stored{u}") for u in range(U)]
        t_ready, xT_ready, gu_ready = sem("t_ready"), sem("xT_ready"), sem("gu_ready")
        silu_ready, h_ready, down_done, y_ready = sem("silu_ready"), sem("h_ready"), sem("down_done"), sem("y_ready")
        block = ctx.enter_context(nc.Block())

        @block.sync
        def _(sp):
            def rows(dram, i, u):
                return dram[bass.ds(S * (U * i + u), S), :].rearrange("(n p) c -> p n c", p=P)

            for u in range(U):
                sp.sem_inc(y_stored[u], 1)
                sp.dma_start(x[:, u], rows(st.xs1, 0, u)).then_inc(x_loaded[u], 16)
            w1v = d["L1_ffn_W1"].rearrange("e (k p) n -> p e k n", p=P)
            w3v = d["L1_ffn_W3"].rearrange("e (k p) n -> p e k n", p=P)
            w2v = d["L1_ffn_W2"].rearrange("e p n -> p e n")
            for k in range(KC):
                sp.dma_start(w1_all[:, 0:E1, k, :], w1v[:, 0:E1, k, :]).then_inc(w_loaded, 16)
                sp.dma_start(w3_all[:, 0:E1, k, :], w3v[:, 0:E1, k, :]).then_inc(w_loaded, 16)
                sp.dma_start(w1_all[:, E1:, k, :], w1v[:, E1:, k, :].to_broadcast([P, TILES_SHARED, I1])).then_inc(w_loaded, 16)
                sp.dma_start(w3_all[:, E1:, k, :], w3v[:, E1:, k, :].to_broadcast([P, TILES_SHARED, I1])).then_inc(w_loaded, 16)
            sp.dma_start(w2_all[:, 0:E1, :], w2v[:, 0:E1, :]).then_inc(w_loaded, 16)
            sp.dma_start(w2_all[:, E1:, :], w2v[:, E1:, :].to_broadcast([P, TILES_SHARED, D])).then_inc(w_loaded, 16)

            def store(i):
                for u in range(U):
                    sp.wait_ge(y_ready, U * i + u + 2)
                    sp.dma_start(rows(st.ys1, i, u), y[:, u]).then_inc(y_stored[u], 16)

            with sp.Fori(0, TILES1 // U - 1) as i:
                for u in range(U):
                    sp.wait_ge(t_ready, U * i + u + 1)
                    sp.dma_start(x[:, u], rows(st.xs1, i + 1, u)).then_inc(x_loaded[u], 16)
                store(i)
            store(TILES1 // U - 1)
            for u in range(U):
                sp.wait_ge(y_stored[u], 16 * TILES1 // U + 1)

        @block.gpsimd
        def _(pool):
            pool.wait_ge(w_loaded, 16 * (4 * KC + 2))

            def widen(i, u):
                t = U * i + u
                pool.tensor_copy(w1[:, u], w1_all[:, bass.ds(t, 1)].squeeze(1)).then_inc(w_ready, 1)
                pool.tensor_copy(w3[:, u], w3_all[:, bass.ds(t, 1)].squeeze(1)).then_inc(w_ready, 1)
                pool.tensor_copy(w2[:, u], w2_all[:, bass.ds(t, 1)].squeeze(1)).then_inc(w_ready, 1)

            for u in range(U):
                widen(0, u)
            with pool.Fori(0, TILES1 // U - 1) as i:
                for u in range(U):
                    pool.wait_ge(down_done, U * i + u + 1)
                    pool.sem_inc(st.pool_passed, 1)
                    widen(i + 1, u)

        @block.tensor
        def _(pe):
            with pe.Fori(0, TILES1 // U) as i:
                for u in range(U):
                    pe.wait_ge(x_loaded[u], 16 * (i + 1))
                    for t in range(TB):
                        for c in range(KC):
                            ins = pe.transpose(bank(u, 0)[:, c, t * P:t * P + P], x[:, u, t, c * P:c * P + P], st.ident[:])
                    ins.then_inc(t_ready, 1)
                for u in range(U):
                    pe.wait_ge(xT_ready, U * i + u + 1)
                    pe.wait_ge(w_ready, 3 * (U * i + u + 1))
                    for n, w in enumerate((w1, w3)):
                        for c in range(KC):
                            ins = pe.matmul(bank(u, 1)[:, n, :], w[:, u, c, :], xT[:, u, c, :], start=(c == 0), stop=(c == KC - 1))
                    ins.then_inc(gu_ready, 1)
                for u in range(U):
                    pe.wait_ge(h_ready, U * i + u + 1)
                    pe.wait_ge(y_ready, U * i + 1)
                    for t in range(TB):
                        ins = pe.matmul(bank(u, 2)[:, t, :], h[:, u, t * P:t * P + P], w2[:, u, :], start=True, stop=True)
                    ins.then_inc(down_done, 1)

        @block.scalar
        def _(act):
            with act.Fori(0, TILES1 // U) as i:
                for u in range(U):
                    act.wait_ge(t_ready, U * i + u + 1)
                    act.activation(xT[:, u], bank(u, 0), ACT.Copy).then_inc(xT_ready, 1)
                for u in range(U):
                    act.wait_ge(gu_ready, U * i + u + 1)
                    act.activation(sg[:, u, :], bank(u, 1)[:, 0, :], ACT.Silu).then_inc(silu_ready, 1)

        @block.vector
        def _(dve):
            dve.sem_inc(y_ready, 1)
            with dve.Fori(0, TILES1 // U) as i:
                for u in range(U):
                    dve.wait_ge(silu_ready, U * i + u + 1)
                    dve.tensor_tensor(h[:, u, :], sg[:, u, :], bank(u, 1)[:, 1, :], ALU.mult).then_inc(h_ready, 1)
                for u in range(U):
                    dve.wait_ge(down_done, U * i + u + 1)
                    dve.wait_ge(y_stored[u], 16 * i + 1)
                    dve.tensor_copy(y[:, u], bank(u, 2)).then_inc(y_ready, 1)


def output_stage(nc, st, d, out):
    with ExitStack() as ctx:
        def sb(name, shape, dt=F32):
            return ctx.enter_context(nc.sbuf_tensor("out_" + name, shape, dt))

        def sem(name):
            return st.semaphore(nc, "out_" + name)

        sh = sb("sh", [P, U, TB, D])
        yr = sb("yr", [P, U, TB, K1, D])
        idx = sb("idx", [P, U, TB, K1], U32)
        xn = sb("xn", [P, U, TB, D])
        stats = sb("stats", [P, U, TB, 6])
        var = sb("var", [P, U, TB, 2])
        rstd = sb("rstd", [P, U, TB])
        sh_loaded, yr_loaded = [sem(f"sh_loaded{u}") for u in range(U)], [sem(f"yr_loaded{u}") for u in range(U)]
        stored = [sem(f"stored{u}") for u in range(U)]
        idx_ready, summed, steps = sem("idx_ready"), sem("summed"), sem("dve_steps")
        varr, rstdr, epsr, xn_ready = sem("var_ready"), sem("rstd_ready"), sem("eps_added"), sem("xn_ready")
        block = ctx.enter_context(nc.Block())
        sh_v = st.ys1[SHARED1:SHARED1 + N, :].rearrange("(n p) c -> p n c", p=P)
        out_v = out.rearrange("(n p) c -> p n c", p=P)

        @block.sync
        def _(sp):
            for u in range(U):
                sp.dma_start(sh[:, u], sh_v[:, TB * u:TB * u + TB, :]).then_inc(sh_loaded[u], 16)
            with sp.Fori(0, STEPS - 1) as i:
                for u in range(U):
                    sp.wait_ge(xn_ready, U * i + u + 1)
                    sp.dma_start(sh[:, u], sh_v[:, bass.ds(TB * U * (i + 1) + TB * u, TB), :]).then_inc(sh_loaded[u], 16)

        @block.scalar
        def _(act):
            for u in range(U):
                act.sem_inc(stored[u], 1)
            with act.Fori(0, STEPS) as i:
                for u in range(U):
                    act.wait_ge(xn_ready, U * i + u + 1)
                    act.dma_start(out_v[:, bass.ds(TB * U * i + TB * u, TB), :], xn[:, u]).then_inc(stored[u], 16)
            for u in range(U):
                act.wait_ge(stored[u], 16 * STEPS + 1)

        @block.gpsimd
        def _(pool):
            def gather(i, u, count):
                pool.tensor_copy(idx[:, u], st.slot1[:, bass.ds(TB * U * i + TB * u, TB), :]).then_inc(idx_ready, 1)
                pool.wait_ge(idx_ready, count)
                pool.sem_inc(st.pool_passed, 1)
                for t in range(TB):
                    for j in range(K1):
                        pool.indirect_dma_start(
                            out=yr[:, u, t, j, :], out_offset=None, in_=st.ys1,
                            in_offset=bass.IndirectOffsetOnAxis(ap=idx[:, u, t, j:j + 1], axis=0)).then_inc(yr_loaded[u], 16)

            for u in range(U):
                gather(0, u, u + 1)
            with pool.Fori(0, STEPS - 1) as i:
                for u in range(U):
                    pool_rstd(pool, st, var, rstd, u, varr, rstdr, epsr, U * i + u + 1)
                for u in range(U):
                    pool.wait_ge(summed, U * i + u + 1)
                    pool.sem_inc(st.pool_passed, 1)
                    gather(i + 1, u, U * (i + 1) + u + 1)
            for u in range(U):
                pool_rstd(pool, st, var, rstd, u, varr, rstdr, epsr, U * (STEPS - 1) + u + 1)

        @block.vector
        def _(dve):
            with dve.Fori(0, STEPS) as i:
                s = Steps(dve, steps, i, U * (3 + TB * K1))
                for u in range(U):
                    blk = TB * U * i + TB * u
                    dve.wait_ge(sh_loaded[u], 16 * (i + 1))
                    s.do(dve.tensor_tensor(sh[:, u], sh[:, u], st.res[:, bass.ds(blk, TB), :], ALU.add))
                    dve.wait_ge(yr_loaded[u], 16 * TB * K1 * (i + 1))
                    for j in range(K1):
                        for t in range(TB):
                            n_sum = s.mark(dve.scalar_tensor_tensor(sh[:, u, t, :], yr[:, u, t, j, :],
                                                                    st.gate1[:, bass.ds(blk + t, 1), j:j + 1].squeeze(1),
                                                                    sh[:, u, t, :], ALU.mult, ALU.add))
                        s.after(n_sum)
                    dve.sem_inc(summed, 1)
                    dve_stats(dve, st, s, sh[:, u], stats, var, u, varr)
                for u in range(U):
                    dve.wait_ge(rstdr, U * i + u + 1)
                    dve.wait_ge(stored[u], 16 * i + 1)
                    dve_normalize(dve, xn[:, u], sh[:, u], var, rstd, u).then_inc(xn_ready, 1)
                s.close()


def xattn0_stage(nc, st, d):
    xattn_stage(nc, st, d, 0)


def xattn1_stage(nc, st, d):
    xattn_stage(nc, st, d, 1)


STAGES = [setup_stage, rwkv_stage, xattn0_stage, moe0_stage, attn1_stage, xattn1_stage, moe1_stage]


def decoder(nc, d, out):
    st = Store()
    with ExitStack() as ctx:
        def sb(name, shape, dt=F32):
            return ctx.enter_context(nc.sbuf_tensor(name, shape, dt))

        def dram(name, shape):
            return nc.dram_tensor(name, shape, F32, kind="Internal").ap()

        st.res = sb("res", [P, NBLK, D])
        st.vecs = sb("vecs", [P, KC * len(VECS)])
        st.rows = sb("rows", [P, len(ROWS), D])
        st.ebias = sb("ebias", [P, E1])
        st.zero = sb("zero", [P, D])
        st.ident = sb("ident", [P, P])
        st.identb = sb("identb", [P, P], BF16)
        st.lower = sb("lower", [P, P], BF16)
        st.ones = sb("ones", [P, P], BF16)
        st.hmask = sb("hmask", [P, HPC])
        st.selrow = sb("selrow", [P, HEADS, P])
        st.eps = sb("eps", [P, 8])
        st.dve_passed = ctx.enter_context(nc.semaphore("dve_passed"))
        st.act_passed = ctx.enter_context(nc.semaphore("act_passed"))
        st.pe_passed = ctx.enter_context(nc.semaphore("pe_passed"))
        st.ys0_zeroed = ctx.enter_context(nc.semaphore("ys0_zeroed"))
        st.pool_passed = ctx.enter_context(nc.semaphore("pool_passed"))
        st.consts_ready = ctx.enter_context(nc.semaphore("consts_ready"))
        st.blk = sb("blk", [P, P])
        st.neghalf = sb("neghalf", [P, 8])
        st.iota = sb("iota", [P, E1])
        st.base0 = sb("base0", [P, E0P])
        st.base1 = sb("base1", [P, E1])
        st.w = sb("w", [P, KC])
        st.wdec = sb("wdec", [P, KC, S])
        st.macc0 = sb("macc0", [P, U, E0P], BF16)
        st.macc1 = sb("macc1", [P, U, E1], BF16)
        st.slot0 = sb("slot0", [P, NBLK, K0], U32)
        st.gate0 = sb("gate0", [P, NBLK, K0])
        st.slot1 = sb("slot1", [P, NBLK, K1], U32)
        st.gate1 = sb("gate1", [P, NBLK, K1])
        st.count0 = sb("count0", [P, E0P])
        st.limits = sb("limits", [P, TILES_SHARED - 1])
        st.over = sb("over", [P, E0P, TILES_SHARED - 1])
        st.ntile = sb("ntile", [P, E0P])
        st.first = sb("first", [P, E0 + 2])
        st.tile0 = sb("tile0", [P, E0 + 2], I32)
        st.tiles0 = sb("tiles0", [P, E0 + 1], I32)
        st.end0 = sb("end0", [P, E0P], I32)
        st.xs0, st.ys0 = dram("xs0", [(E0 + 1) * REG0, D]), dram("ys0", [(E0 + 1) * REG0, D])
        st.xs1, st.ys1 = dram("xs1", [ROWS1, D]), dram("ys1", [ROWS1, D])

        for stage in STAGES:
            stage(nc, st, d)
            st.end_stage(nc)
        output_stage(nc, st, d, out)


_T = ["L0_attn_Wk", "L0_attn_Wv", "L0_attn_Wr", "L0_attn_Wo", "L0_attn_Fk", "L0_attn_Fr", "L0_attn_Fv",
      "L0_xattn_w_q", "L0_xattn_w_k", "L0_xattn_w_v", "L0_ffn_router_w",
      "L1_attn_Wq", "L1_attn_Wk", "L1_attn_Wv", "L1_attn_Wp",
      "L1_xattn_Wq", "L1_xattn_Wk", "L1_xattn_Wv", "L1_ffn_gate_w", "L0_xattn_w_o", "L1_xattn_Wo"]


def kernel(**inputs):
    import numpy as _np
    import concourse.bacc as _bacc
    from concourse import mybir as _mybir
    from concourse.bass_utils import run_bass_kernel_spmd as _run

    a = {k: _np.asarray(v) for k, v in inputs.items()}
    arrays = {n: _np.ascontiguousarray(a[n].T) for n in _T}
    arrays["x"] = a["x"].reshape(N, D)
    arrays["ctx"] = _np.ascontiguousarray(a["ctx_1024"].reshape(N, D).T)
    mask = a["mask_1x1xSxS2_ik0"].reshape(S, S)
    arrays["mask"] = _np.ascontiguousarray(mask)
    arrays["mask_t"] = _np.ascontiguousarray(mask.T)
    arrays["vecs"] = _np.ascontiguousarray(_np.stack([a[n] for n in VECS]).reshape(len(VECS), KC, P)
                                           .transpose(2, 0, 1).reshape(P, -1))
    arrays["rows"] = _np.stack([a[n] for n in ROWS])
    arrays["L1_ffn_bias"] = a["L1_ffn_bias"]
    for n, m in (("L0_ffn_w_gate", "L0_ffn_sw_gate"), ("L0_ffn_w_up", "L0_ffn_sw_up"), ("L0_ffn_w_down", "L0_ffn_sw_down")):
        arrays[n] = _np.concatenate([a[m], a[n]])
    for n, m in (("L1_ffn_W1", "L1_ffn_sw1"), ("L1_ffn_W3", "L1_ffn_sw3"), ("L1_ffn_W2", "L1_ffn_sw2")):
        arrays[n] = _np.concatenate([a[n], a[m].T[None]])

    nc = _bacc.Bacc("TRN2", target_bir_lowering=False, num_devices=1)
    d = {n: nc.dram_tensor("in_" + n, v.shape, _mybir.dt.from_np(v.dtype), kind="ExternalInput").ap()
         for n, v in arrays.items()}
    out = nc.dram_tensor("out", (N, D), F32, kind="ExternalOutput").ap()
    decoder(nc, d, out)
    r = _run(nc, [{"in_" + n: v for n, v in arrays.items()}], core_ids=[0])
    return r.results[0]["out"].reshape(B, S, D)
```

```python
from contextlib import ExitStack

import numpy as np

import concourse.bass as bass
from concourse import mybir

F32 = mybir.dt.float32
BF16 = mybir.dt.bfloat16
F32R = mybir.dt.float32r
I32 = mybir.dt.int32
U32 = mybir.dt.uint32
ALU = mybir.AluOpType
ACT = mybir.ActivationFunctionType
AX = mybir.AxisListType

P = 128
B, S, D = 16, 256, 256
N = B * S
KC = D // P
TB = S // P
U = 2
STEPS = B // U
NBLK = N // P
HEADS, DH = 16, 16
HPC = P // DH
QUADS = HEADS // 4
F = 1024
FC = F // P
E0, K0 = 7, 2
E0P = 8
TILES_SHARED = N // S
E1, K1, I1 = 32, 4, 128
CAP1 = 2 * (2 * 512) * K1 // E1
SHARED1 = E1 * CAP1
DUMP1 = SHARED1 + N
ROWS1 = DUMP1 + S
TILES1 = (SHARED1 + N) // S
TILES0_MIN = N * K0 // S
TILES0_MAX = TILES0_MIN + E0
EPS = 1e-5
NEG = -1e30
EXP_MAX = 80.0
SCALE = 1.0 / DH ** 0.5
FAR = float(1 << 17)
DVE_STEPS = [25 + HEADS, 41 + HEADS]

VECS = ["L0_attn_ln1_g", "L0_attn_ln1_b", "L0_attn_ln2_g", "L0_attn_ln2_b", "L0_attn_tm_k", "L0_attn_tm_v",
        "L0_attn_tm_r", "L0_attn_time_decay", "L0_attn_time_first", "L0_attn_fm_k", "L0_attn_fm_r",
        "L0_xattn_b_q", "L0_xattn_b_k", "L1_xattn_bq", "L1_xattn_bk",
        "L1_attn_gq", "L1_attn_gk", "L1_attn_gv", "L1_attn_bq", "L1_attn_bk", "L1_attn_bv"]
ROWS = ["L0_xattn_b_v", "L0_xattn_b_o", "L1_xattn_bv", "L1_xattn_bo", "L1_attn_bp"]


class Steps:

    def __init__(self, eng, sem, i, per):
        self.eng, self.sem, self.base, self.n, self.per = eng, sem, i * per, 0, per

    def mark(self, ins):
        self.n += 1
        ins.then_inc(self.sem, 1)
        return self.n

    def after(self, n):
        self.eng.wait_ge(self.sem, self.base + n)

    def do(self, ins):
        self.after(self.mark(ins))

    def close(self):
        assert self.n == self.per, (self.n, self.per)


class Store:

    def __init__(self):
        self.stage_sems = []

    def semaphore(self, nc, name):
        self.stage_sems.append(nc.alloc_semaphore(name=name))
        return self.stage_sems[-1]

    def end_stage(self, nc):
        nc.clear_and_free_semaphores(self.stage_sems)
        nc.all_engine_barrier()
        self.stage_sems = []


def vec(st, name, c):
    n = 2 * VECS.index(name) + c
    return st.vecs[:, n:n + 1]


def col(w):
    return w.rearrange("(k p) n -> p k n", p=P)


def setup_stage(nc, st, d):
    with ExitStack() as ctx:
        selrow = ctx.enter_context(nc.sbuf_tensor("setup_selrow", [P, HEADS, P], F32))
        loaded = st.semaphore(nc, "consts_loaded")
        zeroed = st.semaphore(nc, "consts_zeroed")
        shaped = st.semaphore(nc, "consts_shaped")
        padded = st.semaphore(nc, "slots_zeroed")
        decay = st.semaphore(nc, "decay_ready")
        block = ctx.enter_context(nc.Block())

        @block.sync
        def _(sp):
            sp.dma_start(st.vecs[:], d["vecs"]).then_inc(loaded, 16)
            sp.dma_start(st.rows[:], d["rows"].partition_broadcast(P)).then_inc(loaded, 16)
            sp.dma_start(st.ebias[:], d["L1_ffn_bias"].partition_broadcast(P)).then_inc(loaded, 16)
            sp.wait_ge(loaded, 48)
            sp.wait_ge(zeroed, 1)
            for r in range(0, SHARED1, 8 * P):
                n = min(8 * P, SHARED1 - r)
                sp.dma_start(st.xs1[r:r + n, :].rearrange("(n p) c -> p n c", p=P),
                             st.zero[:].unsqueeze(1).to_broadcast([P, n // P, D])).then_inc(padded, 16)
            sp.dma_start(st.ys1[DUMP1:ROWS1, :].rearrange("(n p) c -> p n c", p=P),
                         st.zero[:].unsqueeze(1).to_broadcast([P, TB, D])).then_inc(padded, 16)
            first, n = TILES0_MIN * S, E0 * TB
            sp.dma_start(st.ys0[first:first + E0 * S, :].rearrange("(n p) c -> p n c", p=P),
                         st.zero[:].unsqueeze(1).to_broadcast([P, n, D])).then_inc(padded, 16)
            sp.wait_ge(padded, 16 * (-(-SHARED1 // (8 * P)) + 2))

        @block.gpsimd
        def _(pool):
            pool.memset(st.zero[:], 0.0).then_inc(zeroed, 1)
            pool.memset(st.ident[:], 0.0).then_inc(zeroed, 1)
            pool.memset(st.lower[:], 1.0).then_inc(zeroed, 1)
            pool.memset(st.ones[:], 1.0).then_inc(zeroed, 1)
            pool.memset(st.hmask[:], 1.0).then_inc(zeroed, 1)
            pool.memset(selrow[:], 1.0).then_inc(zeroed, 1)
            pool.memset(st.eps[:], EPS).then_inc(zeroed, 1)
            pool.memset(st.blk[:], SCALE).then_inc(zeroed, 1)
            pool.memset(st.neghalf[:], -0.5).then_inc(zeroed, 1)
            pool.iota(st.iota[:], pattern=[[1, E1]], base=0, channel_multiplier=0,
                      allow_small_or_imprecise_dtypes=True).then_inc(zeroed, 1)
            pool.iota(st.base1[:], pattern=[[CAP1, E1]], base=0, channel_multiplier=0,
                      allow_small_or_imprecise_dtypes=True).then_inc(zeroed, 1)
            pool.wait_ge(zeroed, 11)
            pool.affine_select(out=st.ident[:], in_=st.ident[:], compare_op=ALU.not_equal, fill=1.0, base=0,
                               pattern=[[-1, P]], channel_multiplier=1).then_inc(shaped, 1)
            pool.affine_select(out=st.lower[:], in_=st.lower[:], compare_op=ALU.is_gt, fill=0.0, base=0,
                               pattern=[[1, P]], channel_multiplier=-1).then_inc(shaped, 1)
            pool.affine_select(out=st.hmask[:], in_=st.hmask[:], compare_op=ALU.is_ge, fill=0.0, base=0,
                               pattern=[[-DH, HPC]], channel_multiplier=1).then_inc(shaped, 1)
            pool.wait_ge(shaped, 3)
            pool.affine_select(out=st.hmask[:], in_=st.hmask[:], compare_op=ALU.is_ge, fill=0.0, base=DH - 1,
                               pattern=[[DH, HPC]], channel_multiplier=-1).then_inc(shaped, 1)
            pool.affine_select(out=selrow[:], in_=selrow[:], compare_op=ALU.is_equal, fill=0.0, base=0,
                               pattern=[[-1, HEADS], [0, P]], channel_multiplier=1).then_inc(shaped, 1)
            blk = st.blk[:].rearrange("p (h r) -> p h r", r=DH)
            pool.affine_select(out=blk, in_=blk, compare_op=ALU.is_ge, fill=0.0, base=0,
                               pattern=[[-DH, HPC], [0, DH]], channel_multiplier=1).then_inc(shaped, 1)
            pool.wait_ge(shaped, 6)
            pool.affine_select(out=blk, in_=blk, compare_op=ALU.is_ge, fill=0.0, base=DH - 1,
                               pattern=[[DH, HPC], [0, DH]], channel_multiplier=-1).then_inc(shaped, 1)
            pool.tensor_copy(st.identb[:], st.ident[:]).then_inc(shaped, 1)
            pool.wait_ge(shaped, 8)
            pool.tensor_copy(st.selrow[:], selrow[:]).then_inc(shaped, 1)
            pool.wait_ge(shaped, 9)
            pool.memset(st.eps[:], EPS).then_inc(st.consts_ready, 1)

        @block.scalar
        def _(act):
            act.wait_ge(loaded, 48)
            n = 2 * VECS.index("L0_attn_time_decay")
            act.activation(st.w[:], st.vecs[:, n:n + KC], ACT.Exp).then_inc(decay, 1)

        @block.vector
        def _(dve):
            dve.memset(st.macc0[:], 0.0).then_inc(decay, 1)
            dve.memset(st.macc1[:], 0.0).then_inc(decay, 1)
            dve.wait_ge(decay, 3)
            dve.wait_ge(zeroed, 11)
            dve.tensor_scalar(st.w[:], st.w[:], -1.0, None, ALU.mult).then_inc(decay, 1)
            dve.wait_ge(decay, 4)


def pool_rstd(pool, st, var, rstd, u, var_ready, rstd_ready, eps_added, count):
    pool.wait_ge(var_ready, count)
    pool.tensor_tensor(rstd[:, u, :], var[:, u, :, 1], st.eps[:, 0:TB], ALU.add).then_inc(eps_added, 1)
    pool.wait_ge(eps_added, count)
    pool.tensor_tensor(rstd[:, u, :], rstd[:, u, :], st.neghalf[:, 0:TB], ALU.pow).then_inc(rstd_ready, 1)


def dve_stats(dve, st, steps, x, stats, var, u, var_ready):
    for t in range(TB):
        n = steps.mark(dve.bn_stats(stats[:, u, t, :], x[:, t, :]))
    steps.after(n)
    dve.sem_inc(st.dve_passed, 1)
    dve.bn_aggr(var[:, u, 0, :], stats[:, u, 0, :])
    dve.bn_aggr(var[:, u, 1, :], stats[:, u, 1, :]).then_inc(var_ready, 1)


def dve_normalize(dve, out, x, var, rstd, u):
    for t in range(TB):
        ins = dve.tensor_scalar(out[:, t, :], x[:, t, :], var[:, u, t, 0:1], rstd[:, u, t:t + 1],
                                ALU.subtract, ALU.mult)
    return ins


def rwkv_stage(nc, st, d):
    with ExitStack() as ctx:
        def sb(name, shape, dt=F32):
            return ctx.enter_context(nc.sbuf_tensor("rw_" + name, shape, dt))

        def sem(name):
            return st.semaphore(nc, "rw_" + name)

        wk, wv, wr, wo, fr = (sb(n, [P, KC, D]) for n in ("wk", "wv", "wr", "wo", "fr"))
        fk = sb("fk", [P, KC, F])
        fv = sb("fv", [P, FC, D])
        x = sb("x", [P, U, TB, D])
        nrm = sb("nrm", [P, U, TB, D])
        h = sb("h", [P, U, KC, S + 1])
        dif = sb("dif", [P, U, KC, S])
        mix = sb("mix", [P, U, 3, KC, S])
        ex = sb("ex", [P, U, 4, KC, S])
        top = sb("top", [P, U, KC, S + 1])
        num = sb("num", [P, U, KC, S + 1])
        den = sb("den", [P, U, KC, S + 1])
        er = sb("er", [P, U, KC, S])
        e2bv = sb("e2bv", [P, U, KC, S])
        q = sb("q", [P, U, KC, S])
        y1 = sb("y1", [P, U, KC, S])
        y2 = sb("y2", [P, U, KC, S])
        rw = sb("rw", [P, U, KC, S])
        x2 = sb("x2", [P, U, TB, D])
        kf = sb("kf", [P, U, FC, S])
        es = sb("es", [P, U, TB, D])
        wdec = sb("wdec", [P, KC, S])
        stats = sb("stats", [P, U, TB, 6])
        var = sb("var", [P, U, TB, 2])
        rstd = sb("rstd", [P, U, TB])
        ps = ctx.enter_context(nc.psum_tensor("rw_ps", [P, U, 4, 512], F32))

        def bank(u, n):
            return ps[:, u, n, :].rearrange("p (a b) -> p a b", a=2)

        w_loaded = sem("w_loaded")
        x_loaded = [sem(f"x_loaded{u}") for u in range(U)]
        var1, rstd1, eps1 = sem("var1_ready"), sem("rstd1_ready"), sem("eps1_added")
        var2, rstd2, eps2 = sem("var2_ready"), sem("rstd2_ready"), sem("eps2_added")
        var3, rstd3, eps3 = sem("var3_ready"), sem("rstd3_ready"), sem("eps3_added")
        norm1, norm2, x1_ready = sem("norm1_ready"), sem("norm2_ready"), sem("x1_ready")
        t1_ready, t2_ready = sem("t1_ready"), sem("t2_ready")
        h_ready, g_ready = sem("h_ready"), sem("g_ready")
        mix_ready, gmix_ready = sem("mix_ready"), sem("gmix_ready")
        kvr_ready = sem("kvr_ready")
        er_ready, args_ready, ex_ready = sem("er_ready"), sem("args_ready"), sem("ex_ready")
        rw_ready, o_ready = sem("rw_ready"), sem("o_ready")
        hid_ready, relu_ready, kf_ready = sem("hid_ready"), sem("relu_ready"), sem("kf_ready")
        f_ready, es_ready, kv_ready = sem("f_ready"), sem("es_ready"), sem("kv_ready")
        negr_ready, negf_ready = sem("negr_ready"), sem("negf_ready")
        edges_set = sem("edges_set")
        dve_steps = sem("dve_steps")
        block = ctx.enter_context(nc.Block())
        xv = d["x"].rearrange("(n p) c -> p n c", p=P)

        @block.sync
        def _(sp):
            for u in range(U):
                sp.dma_start(x[:, u], xv[:, TB * u:TB * u + TB, :]).then_inc(x_loaded[u], 16)
            for t, n in ((wk, "L0_attn_Wk"), (wv, "L0_attn_Wv"), (wr, "L0_attn_Wr"), (wo, "L0_attn_Wo"),
                         (fk, "L0_attn_Fk"), (fr, "L0_attn_Fr"), (fv, "L0_attn_Fv")):
                sp.dma_start(t[:], col(d[n])).then_inc(w_loaded, 16)
            with sp.Fori(0, STEPS - 1) as i:
                for u in range(U):
                    sp.wait_ge(x1_ready, U * i + u + 1)
                    sp.dma_start(x[:, u], xv[:, bass.ds(TB * U * (i + 1) + TB * u, TB), :]).then_inc(x_loaded[u], 16)

        @block.gpsimd
        def _(pool):
            with pool.Fori(0, STEPS) as i:
                for var_r, rstd_r, eps_r in ((var1, rstd1, eps1), (var2, rstd2, eps2), (var3, rstd3, eps3)):
                    for u in range(U):
                        pool_rstd(pool, st, var, rstd, u, var_r, rstd_r, eps_r, U * i + u + 1)

        @block.tensor
        def _(pe):
            pe.wait_ge(w_loaded, 16 * 7)

            def turn(u, dst):
                for t in range(TB):
                    for c in range(KC):
                        ins = pe.transpose(dst[:, c, t * P:t * P + P], nrm[:, u, t, c * P:c * P + P], st.ident[:])
                return ins

            with pe.Fori(0, STEPS) as i:
                for u in range(U):
                    pe.wait_ge(norm1, U * i + u + 1)
                    turn(u, bank(u, 0)).then_inc(t1_ready, 1)
                for u in range(U):
                    pe.wait_ge(mix_ready, U * i + u + 1)
                    for n, w in enumerate((wk, wv, wr)):
                        for m in range(KC):
                            for c in range(KC):
                                ins = pe.matmul(bank(u, 1 + n)[:, m, :], w[:, c, m * P:m * P + P], mix[:, u, n, c, :],
                                                start=(c == 0), stop=(c == KC - 1))
                    ins.then_inc(kvr_ready, 1)
                for u in range(U):
                    pe.wait_ge(rw_ready, U * i + u + 1)
                    for t in range(TB):
                        for c in range(KC):
                            ins = pe.matmul(bank(u, 0)[:, t, :], rw[:, u, c, t * P:t * P + P], wo[:, c, :],
                                            start=(c == 0), stop=(c == KC - 1))
                    ins.then_inc(o_ready, 1)
                for u in range(U):
                    pe.wait_ge(norm2, U * i + u + 1)
                    turn(u, bank(u, 1)).then_inc(t2_ready, 1)
                for u in range(U):
                    pe.wait_ge(gmix_ready, U * i + u + 1)
                    for m in range(FC):
                        for c in range(KC):
                            ins = pe.matmul(bank(u, m // 2)[:, m % 2, :], fk[:, c, m * P:m * P + P], mix[:, u, 0, c, :],
                                            start=(c == 0), stop=(c == KC - 1))
                    ins.then_inc(hid_ready, 1)
                for u in range(U):
                    pe.wait_ge(relu_ready, U * i + u + 1)
                    for t in range(TB):
                        for c in range(KC):
                            ins = pe.matmul(bank(u, 0)[:, t, :], mix[:, u, 1, c, t * P:t * P + P], fr[:, c, :],
                                            start=(c == 0), stop=(c == KC - 1))
                    ins.then_inc(f_ready, 1)
                for u in range(U):
                    pe.wait_ge(kf_ready, U * i + u + 1)
                    for t in range(TB):
                        for m in range(FC):
                            ins = pe.matmul(bank(u, 1)[:, t, :], kf[:, u, m, t * P:t * P + P], fv[:, m, :],
                                            start=(m == 0), stop=(m == FC - 1))
                    ins.then_inc(kv_ready, 1)

        @block.scalar
        def _(act):
            act.wait_ge(edges_set, 4)
            with act.Fori(0, STEPS) as i:
                for u in range(U):
                    act.wait_ge(t1_ready, U * i + u + 1)
                    for c in range(KC):
                        ins = act.activation(h[:, u, c, 1:S + 1], bank(u, 0)[:, c, :], ACT.Identity,
                                             bias=vec(st, "L0_attn_ln1_b", c), scale=vec(st, "L0_attn_ln1_g", c))
                    ins.then_inc(h_ready, 1)
                for u in range(U):
                    act.wait_ge(negr_ready, U * i + u + 1)
                    act.activation(er[:, u], er[:, u], ACT.Exp).then_inc(er_ready, 1)
                for u in range(U):
                    act.wait_ge(args_ready, U * i + u + 1)
                    act.activation(ex[:, u], ex[:, u], ACT.Exp).then_inc(ex_ready, 1)
                for u in range(U):
                    act.wait_ge(t2_ready, U * i + u + 1)
                    for c in range(KC):
                        ins = act.activation(h[:, u, c, 1:S + 1], bank(u, 1)[:, c, :], ACT.Identity,
                                             bias=vec(st, "L0_attn_ln2_b", c), scale=vec(st, "L0_attn_ln2_g", c))
                    ins.then_inc(g_ready, 1)
                for u in range(U):
                    act.wait_ge(hid_ready, U * i + u + 1)
                    act.activation(kf[:, u].rearrange("p a b -> p (a b)"),
                                   ps[:, u].rearrange("p a b -> p (a b)"), ACT.Relu).then_inc(relu_ready, 1)
                    act.wait_ge(relu_ready, U * i + u + 1)
                    act.activation(kf[:, u], kf[:, u], ACT.Square).then_inc(kf_ready, 1)
                for u in range(U):
                    act.wait_ge(negf_ready, U * i + u + 1)
                    act.activation(es[:, u], es[:, u], ACT.Exp).then_inc(es_ready, 1)

        @block.vector
        def _(dve):
            dve.memset(h[:, :, :, 0:1], 0.0).then_inc(edges_set, 1)
            dve.memset(top[:, :, :, 0:1], NEG).then_inc(edges_set, 1)
            dve.memset(num[:, :, :, 0:1], 0.0).then_inc(edges_set, 1)
            dve.memset(den[:, :, :, 0:1], 0.0).then_inc(edges_set, 1)
            for c in range(KC):
                dve.tensor_scalar(wdec[:, c, :], st.zero[:, 0:S], st.w[:, c:c + 1], None, ALU.add).then_inc(edges_set, 1)
            dve.wait_ge(edges_set, 4 + KC)
            with dve.Fori(0, STEPS) as i:
                s = Steps(dve, dve_steps, i, U * 30)
                for u in range(U):
                    dve.wait_ge(x_loaded[u], 16 * i + 16)
                    dve_stats(dve, st, s, x[:, u], stats, var, u, var1)
                for u in range(U):
                    dve.wait_ge(rstd1, U * i + u + 1)
                    dve_normalize(dve, nrm[:, u], x[:, u], var, rstd, u).then_inc(norm1, 1)
                for u in range(U):
                    dve.wait_ge(h_ready, U * i + u + 1)
                    s.do(dve.tensor_tensor(dif[:, u], h[:, u, :, 1:S + 1], h[:, u, :, 0:S], ALU.subtract))
                    for n, name in enumerate(("L0_attn_tm_k", "L0_attn_tm_v", "L0_attn_tm_r")):
                        for c in range(KC):
                            ins = dve.scalar_tensor_tensor(mix[:, u, n, c, :], dif[:, u, c, :], vec(st, name, c),
                                                           h[:, u, c, 0:S], ALU.mult, ALU.add)
                    ins.then_inc(mix_ready, 1)
                for u in range(U):
                    k, ww = bank(u, 1), ex[:, u]
                    dve.wait_ge(kvr_ready, U * i + u + 1)
                    dve.tensor_scalar(er[:, u], bank(u, 3), -1.0, EXP_MAX, ALU.mult, ALU.min).then_inc(negr_ready, 1)
                    for c in range(KC):
                        s.mark(dve.tensor_tensor_scan(top[:, u, c, 1:S + 1], wdec[:, c, :], k[:, c, :], NEG,
                                                      ALU.add, ALU.max))
                    n_top = s.n
                    s.after(n_top)
                    for c in range(KC):
                        s.mark(dve.scalar_tensor_tensor(q[:, u, c, :], k[:, c, :], vec(st, "L0_attn_time_first", c),
                                                        top[:, u, c, 0:S], ALU.add, ALU.max))
                    n_q = s.n
                    for c in range(KC):
                        dve.scalar_tensor_tensor(ww[:, 2, c, :], top[:, u, c, 0:S], st.w[:, c:c + 1],
                                                 top[:, u, c, 1:S + 1], ALU.add, ALU.subtract)
                    dve.tensor_tensor(ww[:, 3], k, top[:, u, :, 1:S + 1], ALU.subtract)
                    s.after(n_q)
                    for c in range(KC):
                        dve.scalar_tensor_tensor(ww[:, 1, c, :], k[:, c, :], vec(st, "L0_attn_time_first", c),
                                                 q[:, u, c, :], ALU.add, ALU.subtract)
                    dve.tensor_tensor(ww[:, 0], top[:, u, :, 0:S], q[:, u], ALU.subtract).then_inc(args_ready, 1)
                for u in range(U):
                    v = bank(u, 2)
                    dve.wait_ge(ex_ready, U * i + u + 1)
                    n_ev = s.mark(dve.tensor_tensor(e2bv[:, u], ex[:, u, 3], v, ALU.mult))
                    for c in range(KC):
                        s.mark(dve.tensor_tensor_scan(den[:, u, c, 1:S + 1], ex[:, u, 2, c, :], ex[:, u, 3, c, :], 0.0,
                                                      ALU.mult, ALU.add))
                    n_den = s.n
                    s.after(n_ev)
                    for c in range(KC):
                        s.mark(dve.tensor_tensor_scan(num[:, u, c, 1:S + 1], ex[:, u, 2, c, :], e2bv[:, u, c, :], 0.0,
                                                      ALU.mult, ALU.add))
                    n_num = s.n
                    n_y2 = s.mark(dve.tensor_tensor(y2[:, u], ex[:, u, 1], v, ALU.mult))
                    s.after(n_den)
                    n_q2 = s.mark(dve.tensor_tensor(q[:, u], ex[:, u, 0], den[:, u, :, 0:S], ALU.mult))
                    s.after(n_num)
                    n_y1 = s.mark(dve.tensor_tensor(y1[:, u], ex[:, u, 0], num[:, u, :, 0:S], ALU.mult))
                    s.after(n_q2)
                    n_q3 = s.mark(dve.tensor_tensor(q[:, u], q[:, u], ex[:, u, 1], ALU.add))
                    s.after(n_y1)
                    n_y3 = s.mark(dve.tensor_tensor(y1[:, u], y1[:, u], y2[:, u], ALU.add))
                    s.after(n_q3)
                    dve.wait_ge(er_ready, U * i + u + 1)
                    s.do(dve.scalar_tensor_tensor(q[:, u], er[:, u], 1.0, q[:, u], ALU.add, ALU.mult))
                    s.do(dve.reciprocal(q[:, u], q[:, u]))
                    dve.tensor_tensor(rw[:, u], y1[:, u], q[:, u], ALU.mult).then_inc(rw_ready, 1)
                for u in range(U):
                    dve.wait_ge(o_ready, U * i + u + 1)
                    s.do(dve.tensor_tensor(x2[:, u], bank(u, 0), x[:, u], ALU.add))
                    dve_stats(dve, st, s, x2[:, u], stats, var, u, var2)
                for u in range(U):
                    dve.wait_ge(rstd2, U * i + u + 1)
                    dve_normalize(dve, nrm[:, u], x2[:, u], var, rstd, u).then_inc(norm2, 1)
                for u in range(U):
                    dve.wait_ge(g_ready, U * i + u + 1)
                    s.do(dve.tensor_tensor(dif[:, u], h[:, u, :, 1:S + 1], h[:, u, :, 0:S], ALU.subtract))
                    for n, name in enumerate(("L0_attn_fm_k", "L0_attn_fm_r")):
                        for c in range(KC):
                            ins = dve.scalar_tensor_tensor(mix[:, u, n, c, :], dif[:, u, c, :], vec(st, name, c),
                                                           h[:, u, c, 0:S], ALU.mult, ALU.add)
                    ins.then_inc(gmix_ready, 1)
                    s.mark(dve.tensor_tensor(x2[:, u], x2[:, u], x[:, u], ALU.add))
                for u in range(U):
                    dve.wait_ge(f_ready, U * i + u + 1)
                    dve.tensor_scalar(es[:, u], bank(u, 0), -1.0, EXP_MAX, ALU.mult, ALU.min).then_inc(negf_ready, 1)
                for u in range(U):
                    dve.wait_ge(es_ready, U * i + u + 1)
                    s.do(dve.tensor_scalar(es[:, u], es[:, u], 1.0, None, ALU.add))
                    s.do(dve.reciprocal(es[:, u], es[:, u]))
                    dve.wait_ge(kv_ready, U * i + u + 1)
                    s.do(dve.tensor_tensor(es[:, u], es[:, u], bank(u, 1), ALU.mult))
                    s.do(dve.tensor_tensor(x2[:, u], x2[:, u], es[:, u], ALU.add))
                    dve_stats(dve, st, s, x2[:, u], stats, var, u, var3)
                for u in range(U):
                    dve.wait_ge(rstd3, U * i + u + 1)
                    dve_normalize(dve, st.res[:, bass.ds(TB * U * i + TB * u, TB), :], x2[:, u], var, rstd,
                                  u).then_inc(x1_ready, 1)
                s.close()
            dve.wait_ge(x1_ready, B)


def xattn_stage(nc, st, d, layer):
    masked = layer == 0
    pre = "x0_" if masked else "x1_"
    wq_n, wk_n, wv_n, wo_n = (("L0_xattn_w_q", "L0_xattn_w_k", "L0_xattn_w_v", "L0_xattn_w_o") if masked else
                              ("L1_xattn_Wq", "L1_xattn_Wk", "L1_xattn_Wv", "L1_xattn_Wo"))
    bq_n, bk_n = ("L0_xattn_b_q", "L0_xattn_b_k") if masked else ("L1_xattn_bq", "L1_xattn_bk")
    bv_row, bo_row = (0, 1) if masked else (2, 3)
    experts, ecols, topk = (E0, E0P, K0) if masked else (E1, E1, K1)
    macc = st.macc0 if masked else st.macc1
    with ExitStack() as ctx:
        def sb(name, shape, dt=F32):
            return ctx.enter_context(nc.sbuf_tensor(pre + name, shape, dt))

        def sem(name):
            return st.semaphore(nc, pre + name)

        wq, wk, wv = (sb(n, [P, KC, D]) for n in ("wq", "wk", "wv"))
        wo = sb("wo", [P, KC, D])
        wg = sb("wg", [P, KC, ecols])
        cx = sb("cx", [P, U, KC, S])
        xT = sb("xT", [P, U, KC, S])
        qT = sb("qT", [P, U, KC, S])
        kT = sb("kT", [P, U, KC, S])
        kh, kl = sb("kh", [P, U, KC, S], F32R), sb("kl", [P, U, KC, S], F32R)
        vp = sb("vp", [P, U, TB, HEADS, 32])
        qmh, qml = sb("qmh", [P, U, KC, HPC, S], F32R), sb("qml", [P, U, KC, HPC, S], F32R)
        nmx = sb("nmx", [P, U, TB, P])
        nmT = sb("nmT", [P, U, S], F32R)
        pt = sb("pt", [P, U, TB, HPC, S])
        o32 = sb("o32", [P, U, QUADS, S])
        aq = qT.rearrange("p u t (h r) -> p u t h r", r=DH)
        rec = sb("rec", [P, U, TB, HEADS])
        aT = kT
        xin = sb("xin", [P, U, TB, D])
        xn = y = xin
        stats = sb("stats", [P, U, TB, 6])
        var = sb("var", [P, U, TB, 2])
        rstd = sb("rstd", [P, U, TB])
        lg = sb("lg", [P, U, TB, ecols])
        sc = sb("sc", [P, U, TB, ecols])
        mx8 = sb("mx8", [P, U, TB, 8])
        ix8 = sb("ix8", [P, U, TB, 8], U32)
        ixf = sb("ixf", [P, U, TB, 8])
        hit = sb("hit", [P, U, TB, ecols], BF16)
        pos = sb("pos", [P, U, TB, ecols])
        o_flat = o32.rearrange("p u k s -> p u (k s)")
        oh = o_flat[:, :, 0:TB * topk * ecols].rearrange("p u (t j e) -> p u t j e", t=TB, j=topk)
        junk = o_flat[:, :, 2 * S:2 * S + TB * topk * ecols].rearrange("p u (t j e) -> p u t j e", t=TB, j=topk)
        at = sb("at", [P, U, TB, topk])
        gt = sb("gt", [P, U, TB, topk])
        tmp = sb("tmp", [P, U, TB, topk])
        dst = sb("dst", [P, U, TB, topk], U32)
        if masked:
            count, tiles, first = sb("count", [P, E0P]), sb("tiles", [P, E0P]), sb("first", [P, E0P])
            limits, over = sb("limits", [P, TILES_SHARED - 1]), sb("over", [P, E0P, TILES_SHARED - 1])
            mi = o32.bitcast(I32).rearrange("p u (t h) s -> p (u t) h s", t=QUADS // TB)
            mb = sb("mb", [P, 2, TB, S], BF16)
        else:
            wg_bf = sb("wg_bf", [P, KC, ecols], BF16)
        ps = ctx.enter_context(nc.psum_tensor(pre + "ps", [P, U, 4, 512], F32))

        def bank(u, n):
            return ps[:, u, n, :].rearrange("p (a b) -> p a b", a=2)

        def heads(u):
            return ps[:, u].rearrange("p k (a b) -> p (k a) b", a=2)

        w_loaded = sem("w_loaded")
        cx_loaded = [sem(f"cx_loaded{u}") for u in range(U)]
        preset, mask_ready, mask_loaded = sem("preset"), sem("mask_ready"), sem("mask_loaded")
        t_ready, xT_ready, qkv_ready = sem("t_ready"), sem("xT_ready"), sem("qkv_ready")
        kh_ready = sem("kh_ready")
        qk_ready, vp_ready, qm_ready = sem("qk_ready"), sem("vp_ready"), sem("qm_ready")
        s_ready, max_ready = sem("s_ready"), sem("max_ready")
        mt_ready, nmT_ready = sem("mt_ready"), sem("nmT_ready")
        st_ready, pt_ready = sem("st_ready"), sem("pt_ready")
        pv_ready, o32_ready, oq_ready = sem("pv_ready"), sem("o32_ready"), sem("oq_ready")
        aq_ready, at_ready, aT_ready = sem("aq_ready"), sem("at_ready"), sem("aT_ready")
        xin_ready = sem("xin_ready")
        y_ready = sem("y_ready")
        varr, rstdr, epsr, xn_ready = sem("var_ready"), sem("rstd_ready"), sem("eps_added"), sem("xn_ready")
        rt_ready, rT_ready, lg_ready = sem("rt_ready"), sem("rT_ready"), sem("lg_ready")
        earg_ready, e_ready = sem("earg_ready"), sem("e_ready")
        hit_ready, pos_ready, dst_ready = sem("hit_ready"), sem("pos_ready"), sem("dst_ready")
        kept = sem("kept")
        sent = [sem(f"rows_sent{u}") for u in range(U)]
        stored = [sem(f"rows_stored{u}") for u in range(U)]
        steps = sem("dve_steps")
        counted, tiles_ready = sem("counted"), sem("tiles_ready")
        block = ctx.enter_context(nc.Block())
        ctx_v = d["ctx"].rearrange("(k p) n -> p k n", p=P)
        shared_v = st.xs1[SHARED1:SHARED1 + N, :].rearrange("(n p) c -> p n c", p=P)

        @block.sync
        def _(sp):
            for u in range(U):
                sp.dma_start(cx[:, u], ctx_v[:, :, S * u:S * u + S]).then_inc(cx_loaded[u], 16)
            for t, n in ((wq, wq_n), (wk, wk_n), (wv, wv_n), (wo, wo_n)):
                sp.dma_start(t[:], col(d[n])).then_inc(w_loaded, 16)
            if masked:
                sp.dma_start(mi[:, 0], d["mask"].rearrange("(t p) k -> p t k", p=P)).then_inc(mask_loaded, 16)
                sp.dma_start(mi[:, 1], d["mask_t"].rearrange("(t p) k -> p t k", p=P)).then_inc(mask_loaded, 16)
                sp.wait_ge(preset, 3)
                sp.dma_start(wg[:, :, 0:experts], col(d["L0_ffn_router_w"])).then_inc(w_loaded, 16)
            else:
                sp.dma_start(wg_bf[:], col(d["L1_ffn_gate_w"])).then_inc(w_loaded, 16)
            with sp.Fori(0, STEPS - 1) as i:
                for u in range(U):
                    sp.wait_ge(qkv_ready, U * i + u + 1)
                    sp.dma_start(cx[:, u], ctx_v[:, :, bass.ds(S * U * (i + 1) + S * u, S)]).then_inc(cx_loaded[u], 16)

        @block.gpsimd
        def _(pool):
            with pool.Fori(0, STEPS) as i:
                for u in range(U):
                    pool.tensor_copy(xin[:, u], st.res[:, bass.ds(TB * U * i + TB * u, TB), :]).then_inc(xin_ready, 1)
                for u in range(U):
                    pool_rstd(pool, st, var, rstd, u, varr, rstdr, epsr, U * i + u + 1)
                for u in range(U):
                    pool.wait_ge(xn_ready, U * i + u + 1)
                    pool.sem_inc(st.pool_passed, 1)
                    pool.tensor_copy(st.res[:, bass.ds(TB * U * i + TB * u, TB), :], xn[:, u]).then_inc(kept, 1)
                    if not masked:
                        pool.dma_start(shared_v[:, bass.ds(TB * U * i + TB * u, TB), :], xn[:, u]).then_inc(stored[u], 16)
                for u in range(U):
                    here = bass.ds(TB * U * i + TB * u, TB)
                    pool.wait_ge(dst_ready, U * i + u + 1)
                    pool.sem_inc(st.pool_passed, 1)
                    if masked:
                        pool.tensor_copy(st.expert0[:, here, :], ixf[:, u, :, 0:K0]).then_inc(kept, 1)
                        pool.tensor_copy(st.rank0[:, here, :], at[:, u]).then_inc(kept, 1)
                        pool.tensor_copy(st.gate0[:, here, :], gt[:, u]).then_inc(kept, 1)
                    else:
                        pool.tensor_copy(st.slot1[:, here, :], dst[:, u]).then_inc(kept, 1)
                        pool.tensor_copy(st.gate1[:, here, :], gt[:, u]).then_inc(kept, 1)
                        for t in range(TB):
                            for j in range(topk):
                                pool.indirect_dma_start(
                                    out=st.xs1, out_offset=bass.IndirectOffsetOnAxis(ap=dst[:, u, t, j:j + 1], axis=0),
                                    in_=xn[:, u, t, :], in_offset=None, bounds_check=DUMP1 - 1,
                                    oob_is_err=False).then_inc(sent[u], 16)
                if not masked:
                    for u in range(U):
                        pool.wait_ge(sent[u], 16 * TB * topk * (i + 1))
                        pool.wait_ge(stored[u], 16 * (i + 1))
                pool.wait_ge(kept, (4 if masked else 3) * U * (i + 1))
                pool.sem_inc(st.pool_passed, 1)

        @block.tensor
        def _(pe):
            pe.wait_ge(w_loaded, 16 * 5)
            pe.wait_ge(preset, 3)
            if masked:
                pe.wait_ge(mask_ready, 2 * TB)
            else:
                pe.wait_ge(mask_ready, 1)

            def turn(dst, src):
                for t in range(TB):
                    for c in range(KC):
                        ins = pe.transpose(dst[:, c, t * P:t * P + P], src[:, t, c * P:c * P + P], st.ident[:])
                return ins

            with pe.Fori(0, STEPS) as i:
                for u in range(U):
                    pe.wait_ge(xin_ready, U * i + u + 1)
                    turn(bank(u, 0), xin[:, u]).then_inc(t_ready, 1)
                for u in range(U):
                    pe.wait_ge(cx_loaded[u], 16 * i + 16)
                    pe.wait_ge(xT_ready, U * i + u + 1)
                    for n, w, a in ((1, wq, xT), (2, wk, cx)):
                        for m in range(KC):
                            for c in range(KC):
                                pe.matmul(bank(u, n)[:, m, :], w[:, c, m * P:m * P + P], a[:, u, c, :],
                                          start=(c == 0), stop=(c == KC - 1))
                    for t in range(TB):
                        for c in range(KC):
                            ins = pe.matmul(bank(u, 3)[:, t, :], cx[:, u, c, t * P:t * P + P], wv[:, c, :],
                                            start=(c == 0), stop=(c == KC - 1))
                    ins.then_inc(qkv_ready, 1)
                for g in range(KC * TB):
                    m, t = g // TB, g % TB
                    for u in range(U):
                        if g == 0:
                            pe.wait_ge(qm_ready, U * i + u + 1)
                        else:
                            pe.wait_ge(max_ready, U * KC * TB * i + U * (g - 1) + u + 1)
                        for k in range(HPC):
                            if masked:
                                pe.matmul(heads(u)[:, k, :], st.identb[:], mb[:, 0, t, :], start=True, stop=False)
                            ins = pe.matmul(heads(u)[:, k, :], qmh[:, u, m, k, t * P:t * P + P], kh[:, u, m, :],
                                            start=not masked, stop=True)
                        ins.then_inc(s_ready, 1)
                for u in range(U):
                    pe.wait_ge(max_ready, U * KC * TB * i + U * (KC * TB - 1) + u + 1)
                    for t in range(TB):
                        ins = pe.transpose(bank(u, 0)[:, 0, t * P:t * P + P], nmx[:, u, t, :], st.ident[:])
                    ins.then_inc(mt_ready, 1)
                for m in range(KC):
                    for t in range(TB):
                        g = m * TB + t
                        for u in range(U):
                            if g == 0:
                                pe.wait_ge(nmT_ready, U * i + u + 1)
                            elif t == 0:
                                pe.wait_ge(o32_ready, U * KC * i + U * (m - 1) + u + 1)
                            else:
                                pe.wait_ge(pt_ready, U * KC * TB * i + U * (g - 1) + u + 1)
                            for k in range(HPC):
                                if masked:
                                    pe.matmul(heads(u)[:, k, :], st.identb[:], mb[:, 1, t, :], start=True, stop=False)
                                for n, (kp, qp) in enumerate(((kh, qmh), (kh, qml), (kl, qmh))):
                                    pe.matmul(heads(u)[:, k, :], kp[:, u, m, t * P:t * P + P], qp[:, u, m, k, :],
                                              start=not masked and n == 0, stop=False)
                                ins = pe.matmul(heads(u)[:, k, :], st.selrow[:, m * HPC + k, :], nmT[:, u, :],
                                                start=False, stop=True)
                            ins.then_inc(st_ready, 1)
                    for u in range(U):
                        pe.wait_ge(pt_ready, U * KC * TB * i + U * (m * TB + TB - 1) + u + 1)
                        for qd in range(QUADS // KC):
                            for t in range(TB):
                                for j in range(4):
                                    ins = pe.matmul(bank(u, 0)[32 * j:32 * j + 32, qd, :],
                                                    vp[:, u, t, m * HPC + 4 * qd + j, :], pt[:, u, t, 4 * qd + j, :],
                                                    start=(t == 0), stop=(t == TB - 1))
                        ins.then_inc(pv_ready, 1)
                for u in range(U):
                    pe.wait_ge(o32_ready, U * KC * i + U * (KC - 1) + u + 1)
                    for t in range(TB):
                        for qd in range(QUADS):
                            ins = pe.transpose(ps[:, u, 2 + t, qd * P:qd * P + P], o32[:, u, qd, t * P:t * P + P], st.ident[:])
                    ins.then_inc(oq_ready, 1)
                for u in range(U):
                    pe.wait_ge(aq_ready, U * i + u + 1)
                    turn(bank(u, 0), aq[:, u].rearrange("p t h r -> p t (h r)")).then_inc(at_ready, 1)
                for u in range(U):
                    pe.wait_ge(aT_ready, U * i + u + 1)
                    for t in range(TB):
                        for c in range(KC):
                            ins = pe.matmul(bank(u, 1)[:, t, :], aT[:, u, c, t * P:t * P + P], wo[:, c, :],
                                            start=(c == 0), stop=(c == KC - 1))
                    ins.then_inc(y_ready, 1)
                for u in range(U):
                    pe.wait_ge(xn_ready, U * i + u + 1)
                    turn(bank(u, 2), xn[:, u]).then_inc(rt_ready, 1)
                for u in range(U):
                    pe.wait_ge(rT_ready, U * i + u + 1)
                    for t in range(TB):
                        for c in range(KC):
                            ins = pe.matmul(bank(u, 3)[:, t, 0:ecols], xT[:, u, c, t * P:t * P + P], wg[:, c, :],
                                            start=(c == 0), stop=(c == KC - 1))
                    ins.then_inc(lg_ready, 1)
                for u in range(U):
                    pe.wait_ge(hit_ready, U * i + u + 1)
                    for t in range(TB):
                        dst_ps = bank(u, 0)[:, t, 0:ecols]
                        pe.matmul(dst_ps, st.ones[:], macc[:, u, :], start=True, stop=False)
                        if t == 1:
                            pe.matmul(dst_ps, st.ones[:], hit[:, u, 0, :], start=False, stop=False)
                        ins = pe.matmul(dst_ps, st.lower[:], hit[:, u, t, :], start=False, stop=True)
                    ins.then_inc(pos_ready, 1)
            if masked:
                pe.wait_ge(counted, 1)
                pe.matmul(bank(0, 1)[:, 0, 0:E0P], st.ones[:], macc[:, 0, :], start=True, stop=True).then_inc(tiles_ready, 1)

        @block.scalar
        def _(act):
            with act.Fori(0, STEPS) as i:
                for u in range(U):
                    act.wait_ge(t_ready, U * i + u + 1)
                    act.activation(xT[:, u], bank(u, 0), ACT.Copy).then_inc(xT_ready, 1)
                for u in range(U):
                    act.wait_ge(qkv_ready, U * i + u + 1)
                    for c in range(KC):
                        act.activation(qT[:, u, c, :], bank(u, 1)[:, c, :], ACT.Identity, bias=vec(st, bq_n, c), scale=1.0)
                    for c in range(KC):
                        ins = act.activation(kT[:, u, c, :], bank(u, 2)[:, c, :], ACT.Identity, bias=vec(st, bk_n, c),
                                             scale=1.0)
                    ins.then_inc(qk_ready, 1)
                    act.wait_ge(qk_ready, U * i + u + 1)
                    act.activation(kh[:, u], kT[:, u], ACT.Copy).then_inc(kh_ready, 1)
                for u in range(U):
                    act.wait_ge(mt_ready, U * i + u + 1)
                    act.activation(nmT[:, u, :], bank(u, 0)[:, 0, :], ACT.Copy).then_inc(nmT_ready, 1)
                for m in range(KC):
                    for t in range(TB):
                        for u in range(U):
                            act.wait_ge(st_ready, U * KC * TB * i + U * (m * TB + t) + u + 1)
                            act.activation(pt[:, u, t].rearrange("p k q -> p (k q)"),
                                           ps[:, u].rearrange("p k q -> p (k q)"), ACT.Exp, scale=SCALE).then_inc(pt_ready, 1)
                    for u in range(U):
                        act.wait_ge(pv_ready, U * KC * i + U * m + u + 1)
                        act.activation(o32[:, u, m * TB:m * TB + TB].rearrange("p k q -> p (k q)"),
                                       ps[:, u, 0], ACT.Copy).then_inc(o32_ready, 1)
                for u in range(U):
                    act.wait_ge(at_ready, U * i + u + 1)
                    act.activation(aT[:, u], bank(u, 0), ACT.Copy).then_inc(aT_ready, 1)
                for u in range(U):
                    act.wait_ge(rt_ready, U * i + u + 1)
                    act.activation(xT[:, u], bank(u, 2), ACT.Copy).then_inc(rT_ready, 1)
                for u in range(U):
                    act.wait_ge(earg_ready, U * i + u + 1)
                    if masked:
                        act.activation(tmp[:, u, :, 0:1], tmp[:, u, :, 0:1], ACT.Exp).then_inc(e_ready, 1)
                    else:
                        act.activation(sc[:, u], sc[:, u], ACT.Exp).then_inc(e_ready, 1)

        @block.vector
        def _(dve):
            dve.memset(vp[:, :, :, :, DH:32], 0.0).then_inc(preset, 1)
            dve.memset(nmx[:], 0.0).then_inc(preset, 1)
            dve.memset(wg[:], 0.0).then_inc(preset, 1)
            dve.wait_ge(preset, 3)
            dve.memset(vp[:, :, :, :, DH:DH + 1], 1.0).then_inc(preset, 1)
            if masked:
                dve.memset(lg[:], NEG).then_inc(preset, 1)
                dve.wait_ge(preset, 5)
                dve.wait_ge(mask_loaded, 32)
                for n in range(2):
                    for t in range(TB):
                        dve.tensor_scalar(mb[:, n, t, :], mi[:, n, t, :], 0, NEG, ALU.is_equal,
                                          ALU.mult).then_inc(mask_ready, 1)
            else:
                dve.wait_ge(preset, 4)
                dve.wait_ge(w_loaded, 16 * 5)
                dve.tensor_copy(wg[:], wg_bf[:]).then_inc(mask_ready, 1)
            with dve.Fori(0, STEPS) as i:
                s = Steps(dve, steps, i, U * DVE_STEPS[layer])
                for u in range(U):
                    dve.wait_ge(t_ready, U * i + u + 1)
                    n_xb = s.mark(dve.tensor_tensor(y[:, u], xin[:, u],
                                                    st.rows[:, bo_row:bo_row + 1, :].to_broadcast([P, TB, D]), ALU.add))
                for u in range(U):
                    dve.wait_ge(qkv_ready, U * i + u + 1)
                    for t in range(TB):
                        ins = dve.tensor_tensor(vp[:, u, t, :, 0:DH], bank(u, 3)[:, t, :].rearrange("p (h r) -> p h r", r=DH),
                                                st.rows[:, bv_row, :].rearrange("p (h r) -> p h r", r=DH), ALU.add)
                    ins.then_inc(vp_ready, 1)
                    dve.wait_ge(qk_ready, U * i + u + 1)
                    for m in range(KC):
                        for k in range(HPC):
                            s.mark(dve.tensor_scalar(qmh[:, u, m, k, :], qT[:, u, m, :], st.hmask[:, k:k + 1], None, ALU.mult))
                    s.after(s.n)
                    for m in range(KC):
                        for k in range(HPC):
                            dve.scalar_tensor_tensor(qml[:, u, m, k, :], qT[:, u, m, :], st.hmask[:, k:k + 1],
                                                     qmh[:, u, m, k, :].bitcast(F32), ALU.mult, ALU.subtract)
                    dve.wait_ge(kh_ready, U * i + u + 1)
                    dve.tensor_tensor(kl[:, u], kT[:, u], kh[:, u].bitcast(F32), ALU.subtract).then_inc(qm_ready, 1)
                for g in range(KC * TB):
                    m, t = g // TB, g % TB
                    for u in range(U):
                        dve.wait_ge(s_ready, U * KC * TB * i + U * g + u + 1)
                        dve.tensor_reduce(nmx[:, u, t, m * HPC:m * HPC + HPC], heads(u), AX.X, ALU.max,
                                          negate=True).then_inc(max_ready, 1)
                for u in range(U):
                    oq = ps[:, u, 2:4].rearrange("p t (h r) -> p t h r", r=32)
                    dve.wait_ge(oq_ready, U * i + u + 1)
                    s.do(dve.reciprocal(rec[:, u], oq[:, :, :, DH]))
                    for t in range(TB):
                        ins = dve.tensor_tensor(aq[:, u, t], oq[:, t, :, 0:DH],
                                                rec[:, u, t].unsqueeze(2).to_broadcast([P, HEADS, DH]), ALU.mult)
                    ins.then_inc(aq_ready, 1)
                for u in range(U):
                    dve.wait_ge(y_ready, U * i + u + 1)
                    s.do(dve.tensor_tensor(y[:, u], y[:, u], bank(u, 1), ALU.add))
                    dve_stats(dve, st, s, y[:, u], stats, var, u, varr)
                for u in range(U):
                    dve.wait_ge(rstdr, U * i + u + 1)
                    dve_normalize(dve, xn[:, u], y[:, u], var, rstd, u).then_inc(xn_ready, 1)
                for u in range(U):
                    logits = bank(u, 3)[:, :, 0:experts]
                    dve.wait_ge(lg_ready, U * i + u + 1)
                    if masked:
                        s.do(dve.tensor_copy(lg[:, u, :, 0:experts], logits))
                    else:
                        dve.tensor_scalar(sc[:, u], logits, -1.0, EXP_MAX, ALU.mult, ALU.min).then_inc(earg_ready, 1)
                        dve.wait_ge(e_ready, U * i + u + 1)
                        s.do(dve.tensor_scalar(sc[:, u], sc[:, u], 1.0, None, ALU.add))
                        s.do(dve.reciprocal(sc[:, u], sc[:, u]))
                        s.do(dve.tensor_tensor(lg[:, u], sc[:, u],
                                               st.ebias[:].unsqueeze(1).to_broadcast([P, TB, E1]), ALU.add))
                    dve.sem_inc(st.dve_passed, 1)
                    for t in range(TB):
                        n_max = s.mark(dve.max(mx8[:, u, t, :], lg[:, u, t, :]))
                    s.after(n_max)
                    dve.sem_inc(st.dve_passed, 1)
                    for t in range(TB):
                        n_max = s.mark(dve.max_index(ix8[:, u, t, :], mx8[:, u, t, :], lg[:, u, t, :]))
                    s.after(n_max)
                    if masked:
                        dve.tensor_tensor(tmp[:, u, :, 0], mx8[:, u, :, 1], mx8[:, u, :, 0], ALU.subtract).then_inc(earg_ready, 1)
                    s.do(dve.tensor_copy(ixf[:, u], ix8[:, u]))
                    for t in range(TB):
                        for j in range(topk):
                            s.mark(dve.tensor_scalar(oh[:, u, t, j, :], st.iota[:, 0:ecols], ixf[:, u, t, j:j + 1], None,
                                                     ALU.is_equal))
                    s.after(s.n)
                    with nc.allow_low_precision(reason="zeros and ones are exact in bfloat16"):
                        for t in range(TB):
                            s.mark(dve.tensor_reduce(hit[:, u, t, :], oh[:, u, t].rearrange("p j e -> p e j"), AX.X,
                                                     ALU.add))
                    s.after(s.n)
                    if u == 1:
                        dve.wait_ge(pos_ready, U * i + 1)
                    s.do(dve.tensor_tensor(macc[:, 1 - u, :], macc[:, u, :], hit[:, u, 0, :], ALU.add))
                    s.do(dve.tensor_tensor(macc[:, 1 - u, :], macc[:, 1 - u, :], hit[:, u, 1, :], ALU.add))
                    dve.sem_inc(hit_ready, 1)
                    if masked:
                        dve.wait_ge(e_ready, U * i + u + 1)
                        s.do(dve.tensor_scalar(tmp[:, u, :, 1], tmp[:, u, :, 0], 1.0, None, ALU.add))
                        s.do(dve.reciprocal(gt[:, u, :, 0], tmp[:, u, :, 1]))
                        s.do(dve.tensor_tensor(gt[:, u, :, 1], gt[:, u, :, 0], tmp[:, u, :, 0], ALU.mult))
                    else:
                        for t in range(TB):
                            s.mark(dve.tensor_tensor(junk[:, u, t], oh[:, u, t],
                                                     sc[:, u, t, :].unsqueeze(1).to_broadcast([P, topk, ecols]), ALU.mult))
                        s.after(s.n)
                        s.do(dve.tensor_reduce(gt[:, u], junk[:, u], AX.X, ALU.add))
                        s.do(dve.tensor_reduce(tmp[:, u, :, 0], gt[:, u], AX.X, ALU.add))
                        s.do(dve.tensor_scalar(tmp[:, u, :, 0], tmp[:, u, :, 0], 1e-12, None, ALU.max))
                        s.do(dve.reciprocal(tmp[:, u, :, 1], tmp[:, u, :, 0]))
                        s.do(dve.tensor_tensor(gt[:, u], gt[:, u], tmp[:, u, :, 1:2].to_broadcast([P, TB, topk]), ALU.mult))
                    dve.wait_ge(pos_ready, U * i + u + 1)
                    place = bank(u, 0)[:, :, 0:ecols]
                    if masked:
                        s.do(dve.tensor_copy(pos[:, u], place))
                    else:
                        s.do(dve.tensor_tensor(pos[:, u], place, st.base1[:].unsqueeze(1).to_broadcast([P, TB, E1]), ALU.add))
                    if not masked:
                        s.do(dve.tensor_scalar(lg[:, u], place, CAP1 - 0.5, FAR, ALU.is_gt, ALU.mult))
                        s.do(dve.tensor_tensor(pos[:, u], pos[:, u], lg[:, u], ALU.add))
                    for t in range(TB):
                        s.mark(dve.tensor_tensor(junk[:, u, t], oh[:, u, t],
                                                 pos[:, u, t, :].unsqueeze(1).to_broadcast([P, topk, ecols]), ALU.mult))
                    s.after(s.n)
                    if masked:
                        dve.tensor_reduce(at[:, u], junk[:, u], AX.X, ALU.add).then_inc(dst_ready, 1)
                    else:
                        s.do(dve.tensor_reduce(at[:, u], junk[:, u], AX.X, ALU.add))
                        s.do(dve.tensor_scalar(at[:, u], at[:, u], float(DUMP1), None, ALU.min))
                        s.do(dve.tensor_scalar(tmp[:, u], at[:, u], DUMP1 - 0.5, None, ALU.is_lt))
                        s.do(dve.tensor_tensor(gt[:, u], gt[:, u], tmp[:, u], ALU.mult))
                        dve.tensor_copy(dst[:, u], at[:, u]).then_inc(dst_ready, 1)
                s.close()
            if masked:
                dve.wait_ge(pos_ready, B)
                dve.sem_inc(counted, 1)
                dve.wait_ge(tiles_ready, 1)
                dve.tensor_copy(count[:], bank(0, 1)[:, 0, 0:E0P]).then_inc(counted, 1)
                dve.tensor_scalar(limits[:], st.iota[:, 1:TILES_SHARED], float(S), None, ALU.mult).then_inc(counted, 1)
                dve.wait_ge(counted, 3)
                dve.tensor_tensor(over[:], count[:].unsqueeze(2).to_broadcast([P, E0P, TILES_SHARED - 1]),
                                  limits[:].unsqueeze(1).to_broadcast([P, E0P, TILES_SHARED - 1]),
                                  ALU.is_gt).then_inc(counted, 1)
                dve.wait_ge(counted, 4)
                dve.tensor_reduce(tiles[:], over[:], AX.X, ALU.add).then_inc(counted, 1)
                dve.wait_ge(counted, 5)
                dve.tensor_scalar(tiles[:], tiles[:], 1.0, None, ALU.add).then_inc(counted, 1)
                dve.memset(first[:, 0:1], 0.0).then_inc(counted, 1)
                dve.wait_ge(counted, 7)
                dve.tensor_tensor_scan(first[:, 1:1 + E0], tiles[:, 0:E0], st.zero[:, 0:E0], 0.0,
                                       ALU.add, ALU.add).then_inc(counted, 1)
                dve.wait_ge(counted, 8)
                dve.tensor_copy(st.tile0[:], first[:]).then_inc(counted, 1)
                dve.tensor_copy(st.tiles0[:], tiles[:, 0:E0]).then_inc(counted, 1)
                dve.tensor_scalar(first[:], first[:], float(S), None, ALU.mult).then_inc(counted, 1)
                dve.wait_ge(counted, 11)
                dve.tensor_tensor(count[:], count[:], first[:], ALU.add).then_inc(counted, 1)
                dve.wait_ge(counted, 12)
                dve.tensor_copy(st.end0[:], count[:, 0:E0]).then_inc(counted, 1)
                dve.wait_ge(kept, 4 * B)
                pick = pt.rearrange("p u t h s -> p (u t h s)")[:, 0:NBLK * K0 * E0P].rearrange("p (n e) -> p n e", e=E0P)
                dve.tensor_tensor(pick, st.expert0[:].rearrange("p n j -> p (n j)").unsqueeze(2).to_broadcast([P, NBLK * K0, E0P]),
                                  st.iota[:, 0:E0P].unsqueeze(1).to_broadcast([P, NBLK * K0, E0P]),
                                  ALU.is_equal).then_inc(counted, 1)
                dve.wait_ge(counted, 14)
                dve.tensor_tensor(pick, pick, first[:].unsqueeze(1).to_broadcast([P, NBLK * K0, E0P]), ALU.mult).then_inc(counted, 1)
                dve.wait_ge(counted, 15)
                dve.tensor_reduce(st.expert0[:].rearrange("p n j -> p (n j)"), pick, AX.X, ALU.add).then_inc(counted, 1)
                dve.wait_ge(counted, 16)
                dve.tensor_tensor(st.rank0[:], st.rank0[:], st.expert0[:], ALU.add).then_inc(counted, 1)
                dve.wait_ge(counted, 17)
                dve.tensor_copy(st.slot0[:], st.rank0[:]).then_inc(counted, 1)
                dve.wait_ge(counted, 18)


def moe0_stage(nc, st, d):
    with ExitStack() as ctx:
        def sb(name, shape, dt=F32):
            return ctx.enter_context(nc.sbuf_tensor("m0_" + name, shape, dt))

        def sem(name):
            return st.semaphore(nc, "m0_" + name)

        raw = sb("raw", [P, 3, FC * D])
        w_hi, w_lo = sb("w_hi", [P, 2, 3, FC * D], F32R), sb("w_lo", [P, 2, 3, FC * D], F32R)
        x = sb("x", [P, TB, D])
        idx = sb("idx", [P, TB, K0], U32)
        x_hi, x_lo = sb("x_hi", [P, KC, S], F32R), sb("x_lo", [P, KC, S], F32R)
        sg = sb("sg", [P, 4, S])
        h = sb("h", [P, 4, S])
        h_hi, h_lo = sb("h_hi", [P, FC, S], F32R), sb("h_lo", [P, FC, S], F32R)
        y = sb("y", [P, TB, D])
        gu = ctx.enter_context(nc.psum_tensor("m0_gu", [P, 4, 2, S], F32))
        xp = ctx.enter_context(nc.psum_tensor("m0_xp", [P, KC, S], F32))
        yp = ctx.enter_context(nc.psum_tensor("m0_yp", [P, TB, 512], F32))
        raw_loaded, first_hi, first_lo = sem("raw_loaded"), sem("first_hi_ready"), sem("first_lo_ready")
        hi_ready, w_ready = sem("w_hi_ready"), sem("w_ready")
        padded, idx_ready, scattered = sem("slots_padded"), sem("idx_ready"), sem("rows_scattered")
        x_ready, t_ready, xh_ready, xl_ready = sem("x_ready"), sem("t_ready"), sem("xh_ready"), sem("xl_ready")
        gu_ready, silu_ready, h_ready = sem("gu_ready"), sem("silu_ready"), sem("h_ready")
        down_done, y_taken, y_stored = sem("down_done"), sem("y_taken"), sem("y_stored")
        steps = sem("dve_steps")
        block = ctx.enter_context(nc.Block())
        names = ("L0_ffn_w_gate", "L0_ffn_w_up", "L0_ffn_w_down")

        def tiles_of(eng, e):
            return (eng.value_load(st.tile0[0:1, bass.ds(e, 1)], min_val=0, max_val=TILES0_MAX),
                    eng.value_load(st.tiles0[0:1, bass.ds(e, 1)], min_val=1, max_val=TILES_SHARED))

        def all_tiles(eng):
            return eng.value_load(st.tile0[0:1, E0:E0 + 1], min_val=TILES0_MIN, max_val=TILES0_MAX)

        def rows(dram, row):
            return dram[bass.ds(row, S), :].rearrange("(n p) c -> p n c", p=P)

        def load_raw(eng, w):
            for n, name in enumerate(names):
                src = d[name].rearrange("e (k p) n -> p e k n", p=P)
                eng.dma_start(raw[:, n].rearrange("p (k n) -> p k n", k=src.shape[2]),
                              src[:, bass.ds(w, 1)].squeeze(1)).then_inc(raw_loaded, 16)

        def over_experts(eng, body):
            with eng.Fori(0, E0 // 2) as q:
                body(2 * q, 1, True)
                body(2 * q + 1, 0, True)
            body(E0 - 1, 1, False)

        @block.sync
        def _(sp):
            for e in range(E0):
                end = sp.value_load(st.end0[0:1, e:e + 1], min_val=0, max_val=TILES0_MAX * S)
                sp.dma_start(rows(st.xs0, end), st.zero[:].unsqueeze(1).to_broadcast([P, TB, D])).then_inc(padded, 16)
                sp.wait_ge(padded, 16 * (e + 1))
            total = all_tiles(sp)
            sp.dma_start(rows(st.xs0, total * S), st.zero[:].unsqueeze(1).to_broadcast([P, TB, D])).then_inc(padded, 16)
            sp.sem_inc(y_stored, 1)
            sp.wait_ge(t_ready, TILES_SHARED)
            sp.wait_ge(scattered, 16 * TB * K0 * TILES_SHARED)
            sp.dma_start(x[:], rows(st.xs0, 0)).then_inc(x_ready, 16)
            with sp.Fori(0, total) as j:
                sp.wait_ge(t_ready, TILES_SHARED + j + 1)
                sp.dma_start(x[:], rows(st.xs0, (j + 1) * S)).then_inc(x_ready, 16)
                sp.wait_ge(y_taken, TILES_SHARED + j + 2)
                sp.dma_start(rows(st.ys0, j * S), y[:]).then_inc(y_stored, 16)
            sp.wait_ge(y_stored, 16 * total + 1)
            sp.sem_inc(st.sp_passed, 1)

        @block.gpsimd
        def _(pool):
            def split(e, b, free):
                if free is not None:
                    pool.wait_ge(down_done, free)
                pool.wait_ge(raw_loaded, 16 * 3 * (e + 2))
                pool.sem_inc(st.pool_passed, 1)
                for n in range(3):
                    pool.tensor_copy(w_hi[:, b, n], raw[:, n]).then_inc(hi_ready, 1)
                for n in range(3):
                    pool.wait_ge(hi_ready, 3 * e + n + 1)
                    pool.tensor_tensor(w_lo[:, b, n], raw[:, n], w_hi[:, b, n].bitcast(F32), ALU.subtract).then_inc(w_ready, 1)

            def send(t):
                pool.tensor_copy(x[:], st.res[:, bass.ds(TB * t, TB), :]).then_inc(x_ready, 16)
                pool.tensor_copy(idx[:], st.slot0[:, bass.ds(TB * t, TB), :]).then_inc(idx_ready, 1)
                pool.wait_ge(idx_ready, t + 1)
                pool.wait_ge(x_ready, 16 * (t + 1))
                pool.sem_inc(st.pool_passed, 1)
                for n in range(TB):
                    for j in range(K0):
                        pool.indirect_dma_start(
                            out=st.xs0, out_offset=bass.IndirectOffsetOnAxis(ap=idx[:, n, j:j + 1], axis=0),
                            in_=x[:, n, :], in_offset=None).then_inc(scattered, 16)
                pool.wait_ge(scattered, 16 * TB * K0 * (t + 1))

            pool.wait_ge(padded, 16 * (E0 + 1))
            send(0)
            split(0, 1, None)
            with pool.Fori(1, TILES_SHARED) as t:
                pool.wait_ge(t_ready, t)
                pool.sem_inc(st.pool_passed, 1)
                send(t)

            def next_weights(e, b, more):
                if more:
                    first = pool.value_load(st.tile0[0:1, bass.ds(e, 1)], min_val=0, max_val=TILES0_MAX)
                    split(e + 1, 1 - b, TILES_SHARED + first)

            over_experts(pool, next_weights)

        @block.tensor
        def _(pe):
            def transpose(t):
                pe.wait_ge(x_ready, 16 * (t + 1))
                for n in range(TB):
                    for c in range(KC):
                        ins = pe.transpose(xp[:, c, n * P:n * P + P], x[:, n, c * P:c * P + P], st.ident[:])
                ins.then_inc(t_ready, 1)

            def tile(t, b):
                wh = [w_hi[:, b, n].rearrange("p (c f) -> p c f", f=f) for n, f in enumerate((F, F, D))]
                wl = [w_lo[:, b, n].rearrange("p (c f) -> p c f", f=f) for n, f in enumerate((F, F, D))]

                def down(m):
                    pe.wait_ge(h_ready, FC * t + m + 1)
                    if m == 0:
                        pe.wait_ge(y_taken, t + 1)
                    for n in range(TB):
                        for k, (hp, wp) in enumerate(((h_hi, wh), (h_hi, wl), (h_lo, wh))):
                            ins = pe.matmul(yp[:, n, 0:D], hp[:, m, n * P:n * P + P], wp[2][:, m, :],
                                            start=(m == 0 and k == 0), stop=(m == FC - 1 and k == 2))
                    return ins

                pe.wait_ge(xl_ready, t + 1)
                for m in range(FC):
                    if m >= 4:
                        pe.wait_ge(h_ready, FC * t + m - 3)
                    for n in range(2):
                        for c in range(KC):
                            for k, (wp, xp_) in enumerate(((wh, x_hi), (wl, x_hi), (wh, x_lo))):
                                ins = pe.matmul(gu[:, m % 4, n, :], wp[n][:, c, m * P:m * P + P], xp_[:, c, :],
                                                start=(c == 0 and k == 0), stop=(c == KC - 1 and k == 2))
                    ins.then_inc(gu_ready, 1)
                    if m >= 2:
                        down(m - 2)
                transpose(t + 1)
                down(FC - 2)
                down(FC - 1).then_inc(down_done, 1)

            transpose(0)
            pe.wait_ge(first_lo, 3)
            with pe.Fori(0, TILES_SHARED) as t:
                tile(t, 0)

            def expert(e, b, more):
                first, count = tiles_of(pe, e)
                pe.wait_ge(w_ready, 3 * (e + 1))
                pe.sem_inc(st.pe_passed, 1)
                with pe.Fori(0, count) as k:
                    tile(TILES_SHARED + first + k, b)

            over_experts(pe, expert)

        @block.scalar
        def _(act):
            load_raw(act, 0)
            act.wait_ge(raw_loaded, 16 * 3)
            for n in range(3):
                act.activation(w_hi[:, 0, n], raw[:, n], ACT.Copy).then_inc(first_hi, 1)

            def part(t):
                act.wait_ge(t_ready, t + 1)
                act.activation(x_hi[:], xp[:], ACT.Copy).then_inc(xh_ready, 1)

            def tile(t):
                for m in range(FC):
                    act.wait_ge(gu_ready, FC * t + m + 1)
                    act.activation(sg[:, m % 4, :], gu[:, m % 4, 0, :], ACT.Silu).then_inc(silu_ready, 1)
                part(t + 1)

            part(0)
            act.wait_ge(first_lo, 3)
            load_raw(act, 1)
            with act.Fori(0, TILES_SHARED) as t:
                tile(t)

            def expert(e, b, more):
                first, count = tiles_of(act, e)
                if more:
                    act.wait_ge(w_ready, 3 * (e + 1))
                    act.sem_inc(st.act_passed, 1)
                    load_raw(act, e + 2)
                with act.Fori(0, count) as k:
                    tile(TILES_SHARED + first + k)

            over_experts(act, expert)

        @block.vector
        def _(dve):
            dve.sem_inc(y_taken, 1)

            def part(t):
                dve.wait_ge(xh_ready, t + 1)
                dve.tensor_tensor(x_lo[:], xp[:], x_hi[:].bitcast(F32), ALU.subtract).then_inc(xl_ready, 1)

            def hidden(t):
                s = Steps(dve, steps, t, 2 * FC)
                for m in range(FC):
                    dve.wait_ge(silu_ready, FC * t + m + 1)
                    s.do(dve.tensor_tensor(h[:, m % 4, :], sg[:, m % 4, :], gu[:, m % 4, 1, :], ALU.mult))
                    s.do(dve.tensor_copy(h_hi[:, m, :], h[:, m % 4, :]))
                    dve.tensor_tensor(h_lo[:, m, :], h[:, m % 4, :], h_hi[:, m, :].bitcast(F32), ALU.subtract).then_inc(h_ready, 1)
                s.close()
                part(t + 1)
                dve.wait_ge(down_done, t + 1)

            for n in range(3):
                dve.wait_ge(first_hi, n + 1)
                dve.tensor_tensor(w_lo[:, 0, n], raw[:, n], w_hi[:, 0, n].bitcast(F32), ALU.subtract).then_inc(first_lo, 1)
            part(0)
            with dve.Fori(0, TILES_SHARED) as t:
                hidden(t)
                here = st.res[:, bass.ds(TB * t, TB), :]
                dve.tensor_tensor(here, here, yp[:, :, 0:D], ALU.add).then_inc(y_taken, 1)

            def expert(e, b, more):
                first, count = tiles_of(dve, e)
                with dve.Fori(0, count) as k:
                    hidden(TILES_SHARED + first + k)
                    dve.wait_ge(y_stored, 16 * (first + k) + 1)
                    dve.tensor_copy(y[:], yp[:, :, 0:D]).then_inc(y_taken, 1)

            over_experts(dve, expert)


def attn1_stage(nc, st, d):
    with ExitStack() as ctx:
        def sb(name, shape, dt=F32):
            return ctx.enter_context(nc.sbuf_tensor("a1_" + name, shape, dt))

        def sem(name):
            return st.semaphore(nc, "a1_" + name)

        w = [sb(n, [P, KC, D]) for n in ("wq", "wk", "wv")]
        wp = sb("wp", [P, KC, D])
        qkv = sb("qkv", [P, 3, KC, N])
        acc = sb("acc", [P, U, TB, D])
        yr = sb("yr", [P, U, TB, K0, D])
        idx = sb("idx", [P, U, TB, K0], U32)
        xn = sb("xn", [P, U, TB, D])
        xT = sb("xT", [P, U, KC, S])
        bst = sb("bst", [P, 3, KC, B, 6])
        bnv = sb("bnv", [P, 3, KC, 2])
        bsc = sb("bsc", [P, 3, KC])
        bbi = sb("bbi", [P, 3, KC])
        sig = sb("sig", [P, U, 3, KC, S])
        vt = sb("vt", [P, U, TB, D])
        vvb = sb("vvb", [P, U, KC, P])
        oT = sb("oT", [P, U, KC, S])
        stats = sb("stats", [P, U, TB, 6])
        var = sb("var", [P, U, TB, 2])
        rstd = sb("rstd", [P, U, TB])
        ps = ctx.enter_context(nc.psum_tensor("a1_ps", [P, U, 4, 512], F32))

        def bank(u, n):
            return ps[:, u, n, :].rearrange("p (a b) -> p a b", a=2)

        w_loaded = sem("w_loaded")
        yr_loaded = [sem(f"yr_loaded{u}") for u in range(U)]
        idx_ready, summed = sem("idx_ready"), sem("summed")
        varr, rstdr, epsr, xn_ready = sem("var_ready"), sem("rstd_ready"), sem("eps_added"), sem("xn_ready")
        var2, rstd2, eps2, out_ready = sem("var2_ready"), sem("rstd2_ready"), sem("eps2_added"), sem("out_ready")
        t_ready, xT_ready, proj_ready = sem("t_ready"), sem("xT_ready"), sem("proj_ready")
        kept, counted = sem("proj_kept"), sem("proj_counted")
        bn_steps, bn_eps, bn_rstd, bn_ready = sem("bn_steps"), sem("bn_eps_added"), sem("bn_rstd_ready"), sem("bn_ready")
        sig_ready, qk_ready, vt_ready, vtok_ready = sem("sig_ready"), sem("qk_ready"), sem("vt_ready"), sem("vtok_ready")
        vv_ready, vvb_ready = sem("vv_ready"), sem("vvb_ready")
        o_ready, oT_ready, y_ready = sem("o_ready"), sem("oT_ready"), sem("y_ready")
        steps, steps2 = sem("dve_steps"), sem("dve_steps2")
        block = ctx.enter_context(nc.Block())

        @block.sync
        def _(sp):
            for t, n in zip(w + [wp], ("L1_attn_Wq", "L1_attn_Wk", "L1_attn_Wv", "L1_attn_Wp")):
                sp.dma_start(t[:], col(d[n])).then_inc(w_loaded, 16)

        @block.gpsimd
        def _(pool):
            def gather(i, u, start):
                pool.tensor_copy(idx[:, u], st.slot0[:, bass.ds(TB * U * i + TB * u, TB), :]).then_inc(idx_ready, 1)
                pool.wait_ge(idx_ready, start)
                pool.sem_inc(st.pool_passed, 1)
                for t in range(TB):
                    for j in range(K0):
                        pool.indirect_dma_start(
                            out=yr[:, u, t, j, :], out_offset=None, in_=st.ys0,
                            in_offset=bass.IndirectOffsetOnAxis(ap=idx[:, u, t, j:j + 1], axis=0)).then_inc(yr_loaded[u], 16)

            for u in range(U):
                gather(0, u, u + 1)
            with pool.Fori(0, STEPS - 1) as i:
                for u in range(U):
                    pool_rstd(pool, st, var, rstd, u, varr, rstdr, epsr, U * i + u + 1)
                for u in range(U):
                    pool.wait_ge(summed, U * i + u + 1)
                    pool.sem_inc(st.pool_passed, 1)
                    gather(i + 1, u, U * (i + 1) + u + 1)
            for u in range(U):
                pool_rstd(pool, st, var, rstd, u, varr, rstdr, epsr, U * (STEPS - 1) + u + 1)
            pool.wait_ge(bn_steps, 6)
            pool.tensor_tensor(bsc[:], bnv[:, :, :, 1], st.eps[:, 0:6].rearrange("p (a b) -> p a b", b=KC), ALU.add).then_inc(bn_eps, 1)
            pool.wait_ge(bn_eps, 1)
            pool.tensor_tensor(bsc[:], bsc[:], st.neghalf[:, 0:6].rearrange("p (a b) -> p a b", b=KC), ALU.pow).then_inc(bn_rstd, 1)
            with pool.Fori(0, STEPS) as i:
                for u in range(U):
                    pool_rstd(pool, st, var, rstd, u, var2, rstd2, eps2, U * i + u + 1)

        @block.tensor
        def _(pe):
            pe.wait_ge(w_loaded, 16 * 4)

            def turn(dst, src):
                for t in range(TB):
                    for c in range(KC):
                        ins = pe.transpose(dst[:, c, t * P:t * P + P], src[:, t, c * P:c * P + P], st.ident[:])
                return ins

            with pe.Fori(0, STEPS) as i:
                for u in range(U):
                    pe.wait_ge(xn_ready, U * i + u + 1)
                    turn(bank(u, 0), xn[:, u]).then_inc(t_ready, 1)
                for u in range(U):
                    pe.wait_ge(xT_ready, U * i + u + 1)
                    pe.wait_ge(kept, U * i + 1)
                    for n in range(3):
                        for m in range(KC):
                            for c in range(KC):
                                ins = pe.matmul(bank(u, 1 + n)[:, m, :], w[n][:, c, m * P:m * P + P], xT[:, u, c, :],
                                                start=(c == 0), stop=(c == KC - 1))
                    ins.then_inc(proj_ready, 1)
            pe.wait_ge(kept, B + 1)
            with pe.Fori(0, STEPS) as i:
                for u in range(U):
                    pe.wait_ge(sig_ready, U * i + u + 1)
                    for c in range(KC):
                        for t in range(TB):
                            ins = pe.transpose(bank(u, 0)[:, t, c * P:c * P + P], sig[:, u, 2, c, t * P:t * P + P], st.ident[:])
                    ins.then_inc(vt_ready, 1)
                for u in range(U):
                    pe.wait_ge(vtok_ready, U * i + u + 1)
                    for m in range(KC):
                        for t in range(TB):
                            v = vt[:, u, t, m * P:m * P + P]
                            ins = pe.matmul(bank(u, 1)[:, m, 0:P], v, v, start=(t == 0), stop=(t == TB - 1))
                    ins.then_inc(vv_ready, 1)
                for u in range(U):
                    pe.wait_ge(vvb_ready, U * i + u + 1)
                    pe.wait_ge(qk_ready, U * i + u + 1)
                    for m in range(KC):
                        ins = pe.matmul(bank(u, 2)[:, m, :], vvb[:, u, m, :], sig[:, u, 0, m, :], start=True, stop=True)
                    ins.then_inc(o_ready, 1)
                for u in range(U):
                    pe.wait_ge(oT_ready, U * i + u + 1)
                    for t in range(TB):
                        for c in range(KC):
                            ins = pe.matmul(bank(u, 3)[:, t, :], oT[:, u, c, t * P:t * P + P], wp[:, c, :],
                                            start=(c == 0), stop=(c == KC - 1))
                    ins.then_inc(y_ready, 1)

        @block.scalar
        def _(act):
            act.sem_inc(kept, 1)
            with act.Fori(0, STEPS) as i:
                for u in range(U):
                    act.wait_ge(t_ready, U * i + u + 1)
                    act.activation(xT[:, u], bank(u, 0), ACT.Copy).then_inc(xT_ready, 1)
                for u in range(U):
                    act.wait_ge(proj_ready, U * i + u + 1)
                    act.sem_inc(st.act_passed, 1)
                    for n in range(3):
                        ins = act.activation(qkv[:, n, :, bass.ds(S * U * i + S * u, S)], bank(u, 1 + n), ACT.Copy)
                    ins.then_inc(kept, 1)
            act.wait_ge(bn_ready, 1)
            act.wait_ge(kept, B + 1)
            with act.Fori(0, STEPS) as i:
                for u in range(U):
                    for n in (2, 0, 1):
                        for m in range(KC):
                            ins = act.activation(sig[:, u, n, m, :], qkv[:, n, m, bass.ds(S * U * i + S * u, S)], ACT.Sigmoid,
                                                 bias=bbi[:, n, m:m + 1], scale=bsc[:, n, m:m + 1])
                    ins.then_inc(sig_ready, 1)
                for u in range(U):
                    act.wait_ge(vt_ready, U * i + u + 1)
                    act.activation(vt[:, u], bank(u, 0), ACT.Copy).then_inc(vtok_ready, 1)
                for u in range(U):
                    act.wait_ge(o_ready, U * i + u + 1)
                    act.activation(oT[:, u], bank(u, 2), ACT.Copy).then_inc(oT_ready, 1)

        @block.vector
        def _(dve):
            with dve.Fori(0, STEPS) as i:
                s = Steps(dve, steps, i, U * 7)
                for u in range(U):
                    blk = TB * U * i + TB * u
                    dve.wait_ge(yr_loaded[u], 16 * TB * K0 * (i + 1))
                    for j in range(K0):
                        for t in range(TB):
                            before = acc[:, u, t, :] if j else st.res[:, bass.ds(blk + t, 1), :].squeeze(1)
                            n_sum = s.mark(dve.scalar_tensor_tensor(acc[:, u, t, :], yr[:, u, t, j, :],
                                                                    st.gate0[:, bass.ds(blk + t, 1), j:j + 1].squeeze(1),
                                                                    before, ALU.mult, ALU.add))
                        s.after(n_sum)
                    dve.sem_inc(summed, 1)
                    dve_stats(dve, st, s, acc[:, u], stats, var, u, varr)
                for u in range(U):
                    dve.wait_ge(rstdr, U * i + u + 1)
                    s.mark(dve_normalize(dve, xn[:, u], acc[:, u], var, rstd, u))
                    s.after(s.n)
                    dve.sem_inc(st.dve_passed, 1)
                    dve.tensor_copy(st.res[:, bass.ds(TB * U * i + TB * u, TB), :], xn[:, u]).then_inc(xn_ready, 1)
                for u in range(U):
                    dve.wait_ge(kept, U * i + u + 2)
                    dve.sem_inc(st.dve_passed, 1)
                    for n in range(3):
                        for m in range(KC):
                            ins = dve.bn_stats(bst[:, n, m, bass.ds(U * i + u, 1), :].squeeze(1), qkv[:, n, m, bass.ds(S * U * i + S * u, S)])
                    ins.then_inc(counted, 1)
                s.close()
            dve.wait_ge(counted, B)
            for n in range(3):
                for m in range(KC):
                    dve.bn_aggr(bnv[:, n, m, :], bst[:, n, m].rearrange("p b s -> p (b s)")).then_inc(bn_steps, 1)
            dve.wait_ge(bn_rstd, 1)
            g0, b0 = 2 * VECS.index("L1_attn_gq"), 2 * VECS.index("L1_attn_bq")
            g6 = st.vecs[:, g0:g0 + 6].rearrange("p (a b) -> p a b", b=KC)
            b6 = st.vecs[:, b0:b0 + 6].rearrange("p (a b) -> p a b", b=KC)
            dve.tensor_tensor(bsc[:], bsc[:], g6, ALU.mult).then_inc(bn_steps, 1)
            dve.wait_ge(bn_steps, 7)
            dve.tensor_tensor(bbi[:], bsc[:], bnv[:, :, :, 0], ALU.mult).then_inc(bn_steps, 1)
            dve.wait_ge(bn_steps, 8)
            dve.tensor_tensor(bbi[:], b6, bbi[:], ALU.subtract).then_inc(bn_steps, 1)
            dve.tensor_scalar(bsc[:], bsc[:], 4.0, None, ALU.mult).then_inc(bn_steps, 1)
            dve.wait_ge(bn_steps, 10)
            dve.tensor_scalar(bbi[:], bbi[:], -1.0, 4.0, ALU.add, ALU.mult).then_inc(bn_ready, 1)
            dve.sem_inc(out_ready, 1)
            with dve.Fori(0, STEPS) as i:
                s = Steps(dve, steps2, i, U * 4)
                for u in range(U):
                    dve.wait_ge(sig_ready, U * i + u + 1)
                    dve.tensor_tensor(sig[:, u, 0], sig[:, u, 0], sig[:, u, 1], ALU.mult).then_inc(qk_ready, 1)
                dve.wait_ge(out_ready, U * i + 1)
                for u in range(U):
                    s.mark(dve.tensor_tensor(xn[:, u], st.res[:, bass.ds(TB * U * i + TB * u, TB), :],
                                             st.rows[:, 4:5, :].to_broadcast([P, TB, D]), ALU.add))
                for u in range(U):
                    dve.wait_ge(vv_ready, U * i + u + 1)
                    dve.tensor_tensor(vvb[:, u], bank(u, 1)[:, :, 0:P],
                                      st.blk[:].unsqueeze(1).to_broadcast([P, KC, P]), ALU.mult).then_inc(vvb_ready, 1)
                for u in range(U):
                    dve.wait_ge(y_ready, U * i + u + 1)
                    s.after(s.n)
                    s.do(dve.tensor_tensor(xn[:, u], xn[:, u], bank(u, 3), ALU.add))
                    dve_stats(dve, st, s, xn[:, u], stats, var, u, var2)
                for u in range(U):
                    dve.wait_ge(rstd2, U * i + u + 1)
                    dve_normalize(dve, st.res[:, bass.ds(TB * U * i + TB * u, TB), :], xn[:, u], var, rstd,
                                  u).then_inc(out_ready, 1)
                s.close()
            dve.wait_ge(out_ready, B + 1)


def moe1_stage(nc, st, d):
    with ExitStack() as ctx:
        def sb(name, shape, dt=F32):
            return ctx.enter_context(nc.sbuf_tensor("m1_" + name, shape, dt))

        def sem(name):
            return st.semaphore(nc, "m1_" + name)

        w1_all = sb("w1_all", [P, TILES1, KC, I1], BF16)
        w3_all = sb("w3_all", [P, TILES1, KC, I1], BF16)
        w2_all = sb("w2_all", [P, TILES1, D], BF16)
        w1, w3 = sb("w1", [P, U, KC, I1]), sb("w3", [P, U, KC, I1])
        w2 = sb("w2", [P, U, D])
        x = sb("x", [P, U, TB, D])
        xT = sb("xT", [P, U, KC, S])
        sg = sb("sg", [P, U, S])
        h = sb("h", [P, U, S])
        y = sb("y", [P, U, TB, D])
        ps = ctx.enter_context(nc.psum_tensor("m1_ps", [P, U, 4, 512], F32))

        def bank(u, n):
            return ps[:, u, n, :].rearrange("p (a b) -> p a b", a=2)

        w_loaded, w_ready = sem("w_loaded"), sem("w_ready")
        x_loaded, y_stored = [sem(f"x_loaded{u}") for u in range(U)], [sem(f"y_stored{u}") for u in range(U)]
        t_ready, xT_ready, gu_ready = sem("t_ready"), sem("xT_ready"), sem("gu_ready")
        silu_ready, h_ready, down_done, y_ready = sem("silu_ready"), sem("h_ready"), sem("down_done"), sem("y_ready")
        block = ctx.enter_context(nc.Block())

        @block.sync
        def _(sp):
            def rows(dram, i, u):
                return dram[bass.ds(S * (U * i + u), S), :].rearrange("(n p) c -> p n c", p=P)

            for u in range(U):
                sp.sem_inc(y_stored[u], 1)
                sp.dma_start(x[:, u], rows(st.xs1, 0, u)).then_inc(x_loaded[u], 16)
            w1v = d["L1_ffn_W1"].rearrange("e (k p) n -> p e k n", p=P)
            w3v = d["L1_ffn_W3"].rearrange("e (k p) n -> p e k n", p=P)
            w2v = d["L1_ffn_W2"].rearrange("e p n -> p e n")
            for k in range(KC):
                sp.dma_start(w1_all[:, 0:E1, k, :], w1v[:, 0:E1, k, :]).then_inc(w_loaded, 16)
                sp.dma_start(w3_all[:, 0:E1, k, :], w3v[:, 0:E1, k, :]).then_inc(w_loaded, 16)
                sp.dma_start(w1_all[:, E1:, k, :], w1v[:, E1:, k, :].to_broadcast([P, TILES_SHARED, I1])).then_inc(w_loaded, 16)
                sp.dma_start(w3_all[:, E1:, k, :], w3v[:, E1:, k, :].to_broadcast([P, TILES_SHARED, I1])).then_inc(w_loaded, 16)
            sp.dma_start(w2_all[:, 0:E1, :], w2v[:, 0:E1, :]).then_inc(w_loaded, 16)
            sp.dma_start(w2_all[:, E1:, :], w2v[:, E1:, :].to_broadcast([P, TILES_SHARED, D])).then_inc(w_loaded, 16)

            def store(i):
                for u in range(U):
                    sp.wait_ge(y_ready, U * i + u + 2)
                    sp.dma_start(rows(st.ys1, i, u), y[:, u]).then_inc(y_stored[u], 16)

            with sp.Fori(0, TILES1 // U - 1) as i:
                for u in range(U):
                    sp.wait_ge(t_ready, U * i + u + 1)
                    sp.dma_start(x[:, u], rows(st.xs1, i + 1, u)).then_inc(x_loaded[u], 16)
                store(i)
            store(TILES1 // U - 1)
            for u in range(U):
                sp.wait_ge(y_stored[u], 16 * TILES1 // U + 1)

        @block.gpsimd
        def _(pool):
            pool.wait_ge(w_loaded, 16 * (4 * KC + 2))

            def widen(i, u):
                t = U * i + u
                pool.tensor_copy(w1[:, u], w1_all[:, bass.ds(t, 1)].squeeze(1)).then_inc(w_ready, 1)
                pool.tensor_copy(w3[:, u], w3_all[:, bass.ds(t, 1)].squeeze(1)).then_inc(w_ready, 1)
                pool.tensor_copy(w2[:, u], w2_all[:, bass.ds(t, 1)].squeeze(1)).then_inc(w_ready, 1)

            for u in range(U):
                widen(0, u)
            with pool.Fori(0, TILES1 // U - 1) as i:
                for u in range(U):
                    pool.wait_ge(down_done, U * i + u + 1)
                    pool.sem_inc(st.pool_passed, 1)
                    widen(i + 1, u)

        @block.tensor
        def _(pe):
            with pe.Fori(0, TILES1 // U) as i:
                for u in range(U):
                    pe.wait_ge(x_loaded[u], 16 * (i + 1))
                    for t in range(TB):
                        for c in range(KC):
                            ins = pe.transpose(bank(u, 0)[:, c, t * P:t * P + P], x[:, u, t, c * P:c * P + P], st.ident[:])
                    ins.then_inc(t_ready, 1)
                for u in range(U):
                    pe.wait_ge(xT_ready, U * i + u + 1)
                    pe.wait_ge(w_ready, 3 * (U * i + u + 1))
                    for n, w in enumerate((w1, w3)):
                        for c in range(KC):
                            ins = pe.matmul(bank(u, 1)[:, n, :], w[:, u, c, :], xT[:, u, c, :], start=(c == 0), stop=(c == KC - 1))
                    ins.then_inc(gu_ready, 1)
                for u in range(U):
                    pe.wait_ge(h_ready, U * i + u + 1)
                    pe.wait_ge(y_ready, U * i + 1)
                    for t in range(TB):
                        ins = pe.matmul(bank(u, 2)[:, t, :], h[:, u, t * P:t * P + P], w2[:, u, :], start=True, stop=True)
                    ins.then_inc(down_done, 1)

        @block.scalar
        def _(act):
            with act.Fori(0, TILES1 // U) as i:
                for u in range(U):
                    act.wait_ge(t_ready, U * i + u + 1)
                    act.activation(xT[:, u], bank(u, 0), ACT.Copy).then_inc(xT_ready, 1)
                for u in range(U):
                    act.wait_ge(gu_ready, U * i + u + 1)
                    act.activation(sg[:, u, :], bank(u, 1)[:, 0, :], ACT.Silu).then_inc(silu_ready, 1)

        @block.vector
        def _(dve):
            dve.sem_inc(y_ready, 1)
            with dve.Fori(0, TILES1 // U) as i:
                for u in range(U):
                    dve.wait_ge(silu_ready, U * i + u + 1)
                    dve.tensor_tensor(h[:, u, :], sg[:, u, :], bank(u, 1)[:, 1, :], ALU.mult).then_inc(h_ready, 1)
                for u in range(U):
                    dve.wait_ge(down_done, U * i + u + 1)
                    dve.wait_ge(y_stored[u], 16 * i + 1)
                    dve.tensor_copy(y[:, u], bank(u, 2)).then_inc(y_ready, 1)


def output_stage(nc, st, d, out):
    with ExitStack() as ctx:
        def sb(name, shape, dt=F32):
            return ctx.enter_context(nc.sbuf_tensor("out_" + name, shape, dt))

        def sem(name):
            return st.semaphore(nc, "out_" + name)

        sh = sb("sh", [P, U, TB, D])
        yr = sb("yr", [P, U, TB, K1, D])
        idx = sb("idx", [P, U, TB, K1], U32)
        xn = sb("xn", [P, U, TB, D])
        stats = sb("stats", [P, U, TB, 6])
        var = sb("var", [P, U, TB, 2])
        rstd = sb("rstd", [P, U, TB])
        sh_loaded, yr_loaded = [sem(f"sh_loaded{u}") for u in range(U)], [sem(f"yr_loaded{u}") for u in range(U)]
        stored = [sem(f"stored{u}") for u in range(U)]
        idx_ready, summed, steps = sem("idx_ready"), sem("summed"), sem("dve_steps")
        varr, rstdr, epsr, xn_ready = sem("var_ready"), sem("rstd_ready"), sem("eps_added"), sem("xn_ready")
        block = ctx.enter_context(nc.Block())
        sh_v = st.ys1[SHARED1:SHARED1 + N, :].rearrange("(n p) c -> p n c", p=P)
        out_v = out.rearrange("(n p) c -> p n c", p=P)

        @block.sync
        def _(sp):
            for u in range(U):
                sp.dma_start(sh[:, u], sh_v[:, TB * u:TB * u + TB, :]).then_inc(sh_loaded[u], 16)
            with sp.Fori(0, STEPS - 1) as i:
                for u in range(U):
                    sp.wait_ge(xn_ready, U * i + u + 1)
                    sp.dma_start(sh[:, u], sh_v[:, bass.ds(TB * U * (i + 1) + TB * u, TB), :]).then_inc(sh_loaded[u], 16)

        @block.scalar
        def _(act):
            for u in range(U):
                act.sem_inc(stored[u], 1)
            with act.Fori(0, STEPS) as i:
                for u in range(U):
                    act.wait_ge(xn_ready, U * i + u + 1)
                    act.dma_start(out_v[:, bass.ds(TB * U * i + TB * u, TB), :], xn[:, u]).then_inc(stored[u], 16)
            for u in range(U):
                act.wait_ge(stored[u], 16 * STEPS + 1)

        @block.gpsimd
        def _(pool):
            def gather(i, u, count):
                pool.tensor_copy(idx[:, u], st.slot1[:, bass.ds(TB * U * i + TB * u, TB), :]).then_inc(idx_ready, 1)
                pool.wait_ge(idx_ready, count)
                pool.sem_inc(st.pool_passed, 1)
                for t in range(TB):
                    for j in range(K1):
                        pool.indirect_dma_start(
                            out=yr[:, u, t, j, :], out_offset=None, in_=st.ys1,
                            in_offset=bass.IndirectOffsetOnAxis(ap=idx[:, u, t, j:j + 1], axis=0)).then_inc(yr_loaded[u], 16)

            for u in range(U):
                gather(0, u, u + 1)
            with pool.Fori(0, STEPS - 1) as i:
                for u in range(U):
                    pool_rstd(pool, st, var, rstd, u, varr, rstdr, epsr, U * i + u + 1)
                for u in range(U):
                    pool.wait_ge(summed, U * i + u + 1)
                    pool.sem_inc(st.pool_passed, 1)
                    gather(i + 1, u, U * (i + 1) + u + 1)
            for u in range(U):
                pool_rstd(pool, st, var, rstd, u, varr, rstdr, epsr, U * (STEPS - 1) + u + 1)

        @block.vector
        def _(dve):
            with dve.Fori(0, STEPS) as i:
                s = Steps(dve, steps, i, U * (3 + TB * K1))
                for u in range(U):
                    blk = TB * U * i + TB * u
                    dve.wait_ge(sh_loaded[u], 16 * (i + 1))
                    s.do(dve.tensor_tensor(sh[:, u], sh[:, u], st.res[:, bass.ds(blk, TB), :], ALU.add))
                    dve.wait_ge(yr_loaded[u], 16 * TB * K1 * (i + 1))
                    for j in range(K1):
                        for t in range(TB):
                            n_sum = s.mark(dve.scalar_tensor_tensor(sh[:, u, t, :], yr[:, u, t, j, :],
                                                                    st.gate1[:, bass.ds(blk + t, 1), j:j + 1].squeeze(1),
                                                                    sh[:, u, t, :], ALU.mult, ALU.add))
                        s.after(n_sum)
                    dve.sem_inc(summed, 1)
                    dve_stats(dve, st, s, sh[:, u], stats, var, u, varr)
                for u in range(U):
                    dve.wait_ge(rstdr, U * i + u + 1)
                    dve.wait_ge(stored[u], 16 * i + 1)
                    dve_normalize(dve, xn[:, u], sh[:, u], var, rstd, u).then_inc(xn_ready, 1)
                s.close()


def xattn0_stage(nc, st, d):
    xattn_stage(nc, st, d, 0)


def xattn1_stage(nc, st, d):
    xattn_stage(nc, st, d, 1)


STAGES = [setup_stage, rwkv_stage, xattn0_stage, moe0_stage, attn1_stage, xattn1_stage, moe1_stage]


def decoder(nc, d, out):
    st = Store()
    with ExitStack() as ctx:
        def sb(name, shape, dt=F32):
            return ctx.enter_context(nc.sbuf_tensor(name, shape, dt))

        def dram(name, shape):
            return nc.dram_tensor(name, shape, F32, kind="Internal").ap()

        st.res = sb("res", [P, NBLK, D])
        st.vecs = sb("vecs", [P, KC * len(VECS)])
        st.rows = sb("rows", [P, len(ROWS), D])
        st.ebias = sb("ebias", [P, E1])
        st.zero = sb("zero", [P, D])
        st.ident = sb("ident", [P, P])
        st.identb = sb("identb", [P, P], BF16)
        st.lower = sb("lower", [P, P], BF16)
        st.ones = sb("ones", [P, P], BF16)
        st.hmask = sb("hmask", [P, HPC])
        st.selrow = sb("selrow", [P, HEADS, P], F32R)
        st.eps = sb("eps", [P, 8])
        st.dve_passed = ctx.enter_context(nc.semaphore("dve_passed"))
        st.act_passed = ctx.enter_context(nc.semaphore("act_passed"))
        st.sp_passed = ctx.enter_context(nc.semaphore("sp_passed"))
        st.pe_passed = ctx.enter_context(nc.semaphore("pe_passed"))
        st.pool_passed = ctx.enter_context(nc.semaphore("pool_passed"))
        st.consts_ready = ctx.enter_context(nc.semaphore("consts_ready"))
        st.blk = sb("blk", [P, P])
        st.neghalf = sb("neghalf", [P, 8])
        st.iota = sb("iota", [P, E1])
        st.base1 = sb("base1", [P, E1])
        st.w = sb("w", [P, KC])
        st.macc0 = sb("macc0", [P, U, E0P], BF16)
        st.macc1 = sb("macc1", [P, U, E1], BF16)
        st.slot0 = sb("slot0", [P, NBLK, K0], U32)
        st.gate0 = sb("gate0", [P, NBLK, K0])
        st.slot1 = sb("slot1", [P, NBLK, K1], U32)
        st.gate1 = sb("gate1", [P, NBLK, K1])
        st.expert0 = sb("expert0", [P, NBLK, K0])
        st.rank0 = sb("rank0", [P, NBLK, K0])
        st.tile0 = sb("tile0", [P, E0P], I32)
        st.tiles0 = sb("tiles0", [P, E0], I32)
        st.end0 = sb("end0", [P, E0], I32)
        st.xs0, st.ys0 = dram("xs0", [(TILES0_MAX + 1) * S, D]), dram("ys0", [TILES0_MAX * S, D])
        st.xs1, st.ys1 = dram("xs1", [ROWS1, D]), dram("ys1", [ROWS1, D])

        for stage in STAGES:
            stage(nc, st, d)
            st.end_stage(nc)
        output_stage(nc, st, d, out)


_T = ["L0_attn_Wk", "L0_attn_Wv", "L0_attn_Wr", "L0_attn_Wo", "L0_attn_Fk", "L0_attn_Fr", "L0_attn_Fv",
      "L0_xattn_w_q", "L0_xattn_w_k", "L0_xattn_w_v", "L0_ffn_router_w",
      "L1_attn_Wq", "L1_attn_Wk", "L1_attn_Wv", "L1_attn_Wp",
      "L1_xattn_Wq", "L1_xattn_Wk", "L1_xattn_Wv", "L1_ffn_gate_w", "L0_xattn_w_o", "L1_xattn_Wo"]


def kernel(**inputs):
    import numpy as _np
    import concourse.bacc as _bacc
    from concourse import mybir as _mybir
    from concourse.bass_utils import run_bass_kernel_spmd as _run

    a = {k: _np.asarray(v) for k, v in inputs.items()}
    arrays = {n: _np.ascontiguousarray(a[n].T) for n in _T}
    arrays["x"] = a["x"].reshape(N, D)
    arrays["ctx"] = _np.ascontiguousarray(a["ctx_1024"].reshape(N, D).T)
    mask = a["mask_1x1xSxS2_ik0"].reshape(S, S)
    arrays["mask"] = _np.ascontiguousarray(mask)
    arrays["mask_t"] = _np.ascontiguousarray(mask.T)
    arrays["vecs"] = _np.ascontiguousarray(_np.stack([a[n] for n in VECS]).reshape(len(VECS), KC, P)
                                           .transpose(2, 0, 1).reshape(P, -1))
    arrays["rows"] = _np.stack([a[n] for n in ROWS])
    arrays["L1_ffn_bias"] = a["L1_ffn_bias"]
    for n, m in (("L0_ffn_w_gate", "L0_ffn_sw_gate"), ("L0_ffn_w_up", "L0_ffn_sw_up"), ("L0_ffn_w_down", "L0_ffn_sw_down")):
        arrays[n] = _np.concatenate([a[m], a[n]])
    for n, m in (("L1_ffn_W1", "L1_ffn_sw1"), ("L1_ffn_W3", "L1_ffn_sw3"), ("L1_ffn_W2", "L1_ffn_sw2")):
        arrays[n] = _np.concatenate([a[n], a[m].T[None]])

    nc = _bacc.Bacc("TRN2", target_bir_lowering=False, num_devices=1)
    d = {n: nc.dram_tensor("in_" + n, v.shape, _mybir.dt.from_np(v.dtype), kind="ExternalInput").ap()
         for n, v in arrays.items()}
    out = nc.dram_tensor("out", (N, D), F32, kind="ExternalOutput").ap()
    decoder(nc, d, out)
    r = _run(nc, [{"in_" + n: v for n, v in arrays.items()}], core_ids=[0])
    return r.results[0]["out"].reshape(B, S, D)
```

```python
from contextlib import ExitStack

import numpy as np

import concourse.bass as bass
from concourse import mybir

F32 = mybir.dt.float32
BF16 = mybir.dt.bfloat16
F32R = mybir.dt.float32r
I32 = mybir.dt.int32
U32 = mybir.dt.uint32
ALU = mybir.AluOpType
ACT = mybir.ActivationFunctionType
AX = mybir.AxisListType

P = 128
B, S, D = 16, 256, 256
N = B * S
KC = D // P
TB = S // P
U = 2
STEPS = B // U
NBLK = N // P
HEADS, DH = 16, 16
HPC = P // DH
QUADS = HEADS // 4
F = 1024
FC = F // P
E0, K0 = 7, 2
E0P = 8
TILES_SHARED = N // S
E1, K1, I1 = 32, 4, 128
CAP1 = 2 * (2 * 512) * K1 // E1
SHARED1 = E1 * CAP1
DUMP1 = SHARED1 + N
ROWS1 = DUMP1 + S
TILES1 = (SHARED1 + N) // S
TILES0_MIN = N * K0 // S
TILES0_MAX = TILES0_MIN + E0
EPS = 1e-5
NEG = -1e30
EXP_MAX = 80.0
SCALE = 1.0 / DH ** 0.5
FAR = float(1 << 17)
DVE_STEPS = [25, 41]
BLEND_STEPS, TIME_STEPS, CHANNEL_STEPS = 3, 16, 9

VECS = ["L0_attn_ln1_g", "L0_attn_ln1_b", "L0_attn_ln2_g", "L0_attn_ln2_b", "L0_attn_tm_k", "L0_attn_tm_v",
        "L0_attn_tm_r", "L0_attn_time_decay", "L0_attn_time_first", "L0_attn_fm_k", "L0_attn_fm_r",
        "L0_xattn_b_q", "L0_xattn_b_k", "L1_xattn_bq", "L1_xattn_bk",
        "L1_attn_gq", "L1_attn_gk", "L1_attn_gv", "L1_attn_bq", "L1_attn_bk", "L1_attn_bv"]
ROWS = ["L0_xattn_b_v", "L0_xattn_b_o", "L1_xattn_bv", "L1_xattn_bo", "L1_attn_bp"]


class Steps:

    def __init__(self, eng, sem, i, per):
        self.eng, self.sem, self.base, self.n, self.per = eng, sem, i * per, 0, per

    def mark(self, ins):
        self.n += 1
        ins.then_inc(self.sem, 1)
        return self.n

    def after(self, n):
        self.eng.wait_ge(self.sem, self.base + n)

    def do(self, ins):
        self.after(self.mark(ins))

    def close(self):
        assert self.n == self.per, (self.n, self.per)


class Store:

    def __init__(self):
        self.stage_sems = []

    def semaphore(self, nc, name):
        self.stage_sems.append(nc.alloc_semaphore(name=name))
        return self.stage_sems[-1]

    def end_stage(self, nc):
        nc.clear_and_free_semaphores(self.stage_sems)
        nc.all_engine_barrier()
        self.stage_sems = []


def vec(st, name, c):
    n = 2 * VECS.index(name) + c
    return st.vecs[:, n:n + 1]


def col(w):
    return w.rearrange("(k p) n -> p k n", p=P)


def seq(u, i):
    return U * i + u


def is_first(u, i):
    return isinstance(i, int) and seq(u, i) == 0


def on(sequence, part, *which):
    if sequence is not None:
        part(*sequence, *which)


def setup_stage(nc, st, d):
    with ExitStack() as ctx:
        selrow = ctx.enter_context(nc.sbuf_tensor("setup_selrow", [P, HEADS, P], F32))
        loaded = st.semaphore(nc, "consts_loaded")
        zeroed = st.semaphore(nc, "consts_zeroed")
        shaped = st.semaphore(nc, "consts_shaped")
        padded = st.semaphore(nc, "slots_zeroed")
        decay = st.semaphore(nc, "decay_ready")
        block = ctx.enter_context(nc.Block())

        @block.sync
        def _(sp):
            sp.dma_start(st.vecs[:], d["vecs"]).then_inc(loaded, 16)
            sp.dma_start(st.ebias[:], d["L1_ffn_bias"].partition_broadcast(P)).then_inc(loaded, 16)
            sp.wait_ge(loaded, 32)
            sp.wait_ge(zeroed, 1)
            for r in range(0, SHARED1, 8 * P):
                n = min(8 * P, SHARED1 - r)
                sp.dma_start(st.xs1[r:r + n, :].rearrange("(n p) c -> p n c", p=P),
                             st.zero[:].unsqueeze(1).to_broadcast([P, n // P, D])).then_inc(padded, 16)
            sp.dma_start(st.ys1[DUMP1:ROWS1, :].rearrange("(n p) c -> p n c", p=P),
                         st.zero[:].unsqueeze(1).to_broadcast([P, TB, D])).then_inc(padded, 16)
            first, n = TILES0_MIN * S, E0 * TB
            sp.dma_start(st.ys0[first:first + E0 * S, :].rearrange("(n p) c -> p n c", p=P),
                         st.zero[:].unsqueeze(1).to_broadcast([P, n, D])).then_inc(padded, 16)
            sp.wait_ge(padded, 16 * (-(-SHARED1 // (8 * P)) + 2))

        @block.gpsimd
        def _(pool):
            pool.memset(st.zero[:], 0.0).then_inc(zeroed, 1)
            pool.memset(st.ident[:], 0.0).then_inc(zeroed, 1)
            pool.memset(st.lower[:], 1.0).then_inc(zeroed, 1)
            pool.memset(st.ones[:], 1.0).then_inc(zeroed, 1)
            pool.memset(st.hmask[:], 1.0).then_inc(zeroed, 1)
            pool.memset(selrow[:], 1.0).then_inc(zeroed, 1)
            pool.memset(st.eps[:], EPS).then_inc(zeroed, 1)
            pool.memset(st.blk[:], SCALE).then_inc(zeroed, 1)
            pool.memset(st.neghalf[:], -0.5).then_inc(zeroed, 1)
            pool.iota(st.iota[:], pattern=[[1, E1]], base=0, channel_multiplier=0,
                      allow_small_or_imprecise_dtypes=True).then_inc(zeroed, 1)
            pool.iota(st.base1[:], pattern=[[CAP1, E1]], base=0, channel_multiplier=0,
                      allow_small_or_imprecise_dtypes=True).then_inc(zeroed, 1)
            pool.wait_ge(zeroed, 11)
            pool.affine_select(out=st.ident[:], in_=st.ident[:], compare_op=ALU.not_equal, fill=1.0, base=0,
                               pattern=[[-1, P]], channel_multiplier=1).then_inc(shaped, 1)
            pool.affine_select(out=st.lower[:], in_=st.lower[:], compare_op=ALU.is_gt, fill=0.0, base=0,
                               pattern=[[1, P]], channel_multiplier=-1).then_inc(shaped, 1)
            pool.affine_select(out=st.hmask[:], in_=st.hmask[:], compare_op=ALU.is_ge, fill=0.0, base=0,
                               pattern=[[-DH, HPC]], channel_multiplier=1).then_inc(shaped, 1)
            pool.wait_ge(shaped, 3)
            pool.affine_select(out=st.hmask[:], in_=st.hmask[:], compare_op=ALU.is_ge, fill=0.0, base=DH - 1,
                               pattern=[[DH, HPC]], channel_multiplier=-1).then_inc(shaped, 1)
            pool.affine_select(out=selrow[:], in_=selrow[:], compare_op=ALU.is_equal, fill=0.0, base=0,
                               pattern=[[-1, HEADS], [0, P]], channel_multiplier=1).then_inc(shaped, 1)
            blk = st.blk[:].rearrange("p (h r) -> p h r", r=DH)
            pool.affine_select(out=blk, in_=blk, compare_op=ALU.is_ge, fill=0.0, base=0,
                               pattern=[[-DH, HPC], [0, DH]], channel_multiplier=1).then_inc(shaped, 1)
            pool.wait_ge(shaped, 6)
            pool.affine_select(out=blk, in_=blk, compare_op=ALU.is_ge, fill=0.0, base=DH - 1,
                               pattern=[[DH, HPC], [0, DH]], channel_multiplier=-1).then_inc(shaped, 1)
            pool.tensor_copy(st.identb[:], st.ident[:]).then_inc(shaped, 1)
            pool.wait_ge(shaped, 8)
            pool.tensor_copy(st.selrow[:], selrow[:]).then_inc(shaped, 1)
            pool.wait_ge(shaped, 9)
            pool.memset(st.eps[:], EPS).then_inc(st.consts_ready, 1)

        @block.scalar
        def _(act):
            act.wait_ge(loaded, 32)
            n = 2 * VECS.index("L0_attn_time_decay")
            act.activation(st.w[:], st.vecs[:, n:n + KC], ACT.Exp).then_inc(decay, 1)

        @block.vector
        def _(dve):
            dve.memset(st.macc0[:], 0.0).then_inc(decay, 1)
            dve.memset(st.macc1[:], 0.0).then_inc(decay, 1)
            dve.wait_ge(decay, 3)
            dve.wait_ge(zeroed, 11)
            dve.tensor_scalar(st.w[:], st.w[:], -1.0, None, ALU.mult).then_inc(decay, 1)
            dve.wait_ge(decay, 4)


def pool_rstd(pool, st, var, rstd, u, var_ready, rstd_ready, eps_added, count):
    pool.wait_ge(var_ready, count)
    pool.tensor_tensor(rstd[:, u, :], var[:, u, :, 1], st.eps[:, 0:TB], ALU.add).then_inc(eps_added, 1)
    pool.wait_ge(eps_added, count)
    pool.tensor_tensor(rstd[:, u, :], rstd[:, u, :], st.neghalf[:, 0:TB], ALU.pow).then_inc(rstd_ready, 1)


def dve_stats(dve, st, steps, x, stats, var, u, var_ready):
    for t in range(TB):
        n = steps.mark(dve.bn_stats(stats[:, u, t, :], x[:, t, :]))
    steps.after(n)
    dve.sem_inc(st.dve_passed, 1)
    dve.bn_aggr(var[:, u, 0, :], stats[:, u, 0, :])
    dve.bn_aggr(var[:, u, 1, :], stats[:, u, 1, :]).then_inc(var_ready, 1)


def dve_normalize(dve, out, x, var, rstd, u):
    for t in range(TB):
        ins = dve.tensor_scalar(out[:, t, :], x[:, t, :], var[:, u, t, 0:1], rstd[:, u, t:t + 1],
                                ALU.subtract, ALU.mult)
    return ins


def rwkv_stage(nc, st, d):
    with ExitStack() as ctx:
        def sb(name, shape, dt=F32):
            return ctx.enter_context(nc.sbuf_tensor("rw_" + name, shape, dt))

        def sem(name):
            return st.semaphore(nc, "rw_" + name)

        wk, wv, wr, wo, fr = (sb(n, [P, KC, D]) for n in ("wk", "wv", "wr", "wo", "fr"))
        fk = sb("fk", [P, KC, F])
        fv = sb("fv", [P, FC, D])
        x = sb("x", [P, U, TB, D])
        nrm = sb("nrm", [P, U, TB, D])
        h = sb("h", [P, U, KC, S + 1])
        dif = sb("dif", [P, U, KC, S])
        mix = sb("mix", [P, U, 3, KC, S])
        ex = sb("ex", [P, U, 4, KC, S])
        top = sb("top", [P, U, KC, S + 1])
        num = sb("num", [P, U, KC, S + 1])
        den = sb("den", [P, U, KC, S + 1])
        sr = sb("sr", [P, U, KC, S])
        e2bv = sb("e2bv", [P, U, KC, S])
        q = sb("q", [P, U, KC, S])
        y1 = sb("y1", [P, U, KC, S])
        y2 = sb("y2", [P, U, KC, S])
        rw = sb("rw", [P, U, KC, S])
        x2 = sb("x2", [P, U, TB, D])
        kf = sb("kf", [P, U, FC, S])
        sf = sb("sf", [P, U, TB, D])
        wdec = sb("wdec", [P, KC, S])
        stats = [sb(f"stats{n}", [P, U, TB, 6]) for n in range(3)]
        var = [sb(f"var{n}", [P, U, TB, 2]) for n in range(3)]
        rstd = [sb(f"rstd{n}", [P, U, TB]) for n in range(3)]
        ps = ctx.enter_context(nc.psum_tensor("rw_ps", [P, U, 4, 512], F32))

        def bank(u, n):
            return ps[:, u, n, :].rearrange("p (a b) -> p a b", a=2)

        w_loaded = sem("w_loaded")
        x_loaded = [sem(f"x_loaded{u}") for u in range(U)]
        var_ready = [sem(f"var{n}_ready") for n in range(3)]
        rstd_ready = [sem(f"rstd{n}_ready") for n in range(3)]
        eps_added = [sem(f"eps{n}_added") for n in range(3)]
        norm1, norm2, x1_ready = sem("norm1_ready"), sem("norm2_ready"), sem("x1_ready")
        t1_ready, t2_ready = sem("t1_ready"), sem("t2_ready")
        h_ready, g_ready = sem("h_ready"), sem("g_ready")
        mix_ready, gmix_ready = sem("mix_ready"), sem("gmix_ready")
        kvr_ready, sr_ready = sem("kvr_ready"), sem("sr_ready")
        args_ready, ex_ready = sem("args_ready"), sem("ex_ready")
        rw_ready, o_ready = sem("rw_ready"), sem("o_ready")
        hid_ready, relu_ready, kf_ready = sem("hid_ready"), sem("relu_ready"), sem("kf_ready")
        f_ready, sf_ready, kv_ready = sem("f_ready"), sem("sf_ready"), sem("kv_ready")
        edges_set, x_free, kv_taken = sem("edges_set"), sem("x_free"), sem("kv_taken")
        n_steps, a_steps, d_steps = sem("dve_blend_steps"), sem("dve_time_steps"), sem("dve_channel_steps")
        block = ctx.enter_context(nc.Block())
        xv = d["x"].rearrange("(n p) c -> p n c", p=P)

        def all_halves(eng, half):
            last = STEPS - 1
            half(None, None, None, (0, 0))
            half(None, None, (0, 0), (1, 0))
            half(None, (0, 0), (1, 0), (0, 1))
            with eng.Fori(0, last - 1) as i:
                half((0, i), (1, i), (0, i + 1), (1, i + 1))
                half((1, i), (0, i + 1), (1, i + 1), (0, i + 2))
            half((0, last - 1), (1, last - 1), (0, last), (1, last))
            half((1, last - 1), (0, last), (1, last), None)
            half((0, last), (1, last), None, None)
            half((1, last), None, None, None)

        @block.sync
        def _(sp):
            for u in range(U):
                sp.dma_start(x[:, u], xv[:, TB * u:TB * u + TB, :]).then_inc(x_loaded[u], 16)
            for t, n in ((wk, "L0_attn_Wk"), (wv, "L0_attn_Wv"), (wr, "L0_attn_Wr"), (wo, "L0_attn_Wo"),
                         (fk, "L0_attn_Fk"), (fr, "L0_attn_Fr"), (fv, "L0_attn_Fv")):
                sp.dma_start(t[:], col(d[n])).then_inc(w_loaded, 16)
            with sp.Fori(0, STEPS - 1) as i:
                for u in range(U):
                    sp.wait_ge(x_free, seq(u, i) + 1)
                    sp.dma_start(x[:, u], xv[:, bass.ds(TB * seq(u, i + 1), TB), :]).then_inc(x_loaded[u], 16)

        @block.gpsimd
        def _(pool):
            def rstd_of(u, i, n):
                pool_rstd(pool, st, var[n], rstd[n], u, var_ready[n], rstd_ready[n], eps_added[n], seq(u, i) + 1)

            def half(p, d, a, n):
                on(d, rstd_of, 1)
                on(n, rstd_of, 0)
                on(d, rstd_of, 2)

            all_halves(pool, half)

        @block.tensor
        def _(pe):
            pe.wait_ge(w_loaded, 16 * 7)

            def turn(u, dst):
                for t in range(TB):
                    for c in range(KC):
                        ins = pe.transpose(dst[:, c, t * P:t * P + P], nrm[:, u, t, c * P:c * P + P], st.ident[:])
                return ins

            def turn1(u, i):
                pe.wait_ge(norm1, seq(u, i) + 1)
                turn(u, bank(u, 3)).then_inc(t1_ready, 1)

            def keys_values_gates(u, i):
                pe.wait_ge(mix_ready, seq(u, i) + 1)
                for n, w in ((2, wr), (1, wv), (0, wk)):
                    if n == 0 and not is_first(u, i):
                        pe.wait_ge(kv_taken, seq(u, i))
                    for m in range(KC):
                        for c in range(KC):
                            ins = pe.matmul(bank(u, 1 + n)[:, m, :], w[:, c, m * P:m * P + P], mix[:, u, n, c, :],
                                            start=(c == 0), stop=(c == KC - 1))
                ins.then_inc(kvr_ready, 1)

            def time_output(u, i):
                pe.wait_ge(rw_ready, seq(u, i) + 1)
                for t in range(TB):
                    for c in range(KC):
                        ins = pe.matmul(bank(u, 0)[:, t, :], rw[:, u, c, t * P:t * P + P], wo[:, c, :],
                                        start=(c == 0), stop=(c == KC - 1))
                ins.then_inc(o_ready, 1)

            def turn2(u, i):
                pe.wait_ge(norm2, seq(u, i) + 1)
                turn(u, bank(u, 1)).then_inc(t2_ready, 1)

            def hidden(u, i):
                pe.wait_ge(gmix_ready, seq(u, i) + 1)
                for m in range(FC):
                    for c in range(KC):
                        ins = pe.matmul(bank(u, m // 2)[:, m % 2, :], fk[:, c, m * P:m * P + P], mix[:, u, 0, c, :],
                                        start=(c == 0), stop=(c == KC - 1))
                    if m % 2:
                        ins.then_inc(hid_ready, 1)

            def channel_gate(u, i):
                pe.wait_ge(relu_ready, 4 * seq(u, i) + 1)
                for t in range(TB):
                    for c in range(KC):
                        ins = pe.matmul(bank(u, 0)[:, t, :], mix[:, u, 1, c, t * P:t * P + P], fr[:, c, :],
                                        start=(c == 0), stop=(c == KC - 1))
                ins.then_inc(f_ready, 1)

            def channel_values(u, i):
                pe.wait_ge(kf_ready, 4 * seq(u, i) + 4)
                for t in range(TB):
                    for m in range(FC):
                        ins = pe.matmul(bank(u, 1)[:, t, :], kf[:, u, m, t * P:t * P + P], fv[:, m, :],
                                        start=(m == 0), stop=(m == FC - 1))
                ins.then_inc(kv_ready, 1)

            def half(p, d, a, n):
                on(a, keys_values_gates)
                on(d, turn2)
                on(d, hidden)
                on(d, channel_gate)
                if d is not None:
                    pe.wait_ge(relu_ready, 4 * seq(*d) + 4)
                on(n, turn1)
                on(d, channel_values)
                on(a, time_output)

            all_halves(pe, half)

        @block.scalar
        def _(act):
            act.wait_ge(edges_set, 4 + KC)

            def keep_h(u, i):
                act.wait_ge(t1_ready, seq(u, i) + 1)
                for c in range(KC):
                    ins = act.activation(h[:, u, c, 1:S + 1], bank(u, 3)[:, c, :], ACT.Identity,
                                         bias=vec(st, "L0_attn_ln1_b", c), scale=vec(st, "L0_attn_ln1_g", c))
                ins.then_inc(h_ready, 1)

            def keep_g(u, i):
                act.wait_ge(t2_ready, seq(u, i) + 1)
                for c in range(KC):
                    ins = act.activation(h[:, u, c, 1:S + 1], bank(u, 1)[:, c, :], ACT.Identity,
                                         bias=vec(st, "L0_attn_ln2_b", c), scale=vec(st, "L0_attn_ln2_g", c))
                ins.then_inc(g_ready, 1)

            def gate(u, i):
                act.wait_ge(kvr_ready, seq(u, i) + 1)
                act.activation(sr[:, u], bank(u, 3), ACT.Sigmoid).then_inc(sr_ready, 1)

            def exponentials(u, i):
                act.wait_ge(args_ready, seq(u, i) + 1)
                act.activation(ex[:, u], ex[:, u], ACT.Exp).then_inc(ex_ready, 1)

            def squares(u, i, n):
                act.wait_ge(hid_ready, 4 * seq(u, i) + n + 1)
                act.activation(kf[:, u, 2 * n:2 * n + 2], bank(u, n), ACT.Relu).then_inc(relu_ready, 1)
                act.wait_ge(relu_ready, 4 * seq(u, i) + n + 1)
                act.activation(kf[:, u, 2 * n:2 * n + 2], kf[:, u, 2 * n:2 * n + 2], ACT.Square).then_inc(kf_ready, 1)

            def channel_gate(u, i):
                act.wait_ge(f_ready, seq(u, i) + 1)
                act.activation(sf[:, u], bank(u, 0), ACT.Sigmoid).then_inc(sf_ready, 1)

            def half(p, d, a, n):
                on(a, gate)
                on(d, keep_g)
                on(d, squares, 0)
                on(a, exponentials)
                for part in range(1, 4):
                    on(d, squares, part)
                on(n, keep_h)
                on(d, channel_gate)

            all_halves(act, half)

        @block.vector
        def _(dve):
            dve.memset(h[:, :, :, 0:1], 0.0).then_inc(edges_set, 1)
            dve.memset(top[:, :, :, 0:1], NEG).then_inc(edges_set, 1)
            dve.memset(num[:, :, :, 0:1], 0.0).then_inc(edges_set, 1)
            dve.memset(den[:, :, :, 0:1], 0.0).then_inc(edges_set, 1)
            for c in range(KC):
                dve.tensor_scalar(wdec[:, c, :], st.zero[:, 0:S], st.w[:, c:c + 1], None, ALU.add).then_inc(edges_set, 1)
            dve.wait_ge(edges_set, 4 + KC)

            def stats1(u, i, s):
                dve.wait_ge(x_loaded[u], 16 * i + 16)
                dve_stats(dve, st, s, x[:, u], stats[0], var[0], u, var_ready[0])

            def normal1(u, i):
                dve.wait_ge(rstd_ready[0], seq(u, i) + 1)
                dve_normalize(dve, nrm[:, u], x[:, u], var[0], rstd[0], u).then_inc(norm1, 1)

            def blend(u, s, names):
                s.do(dve.tensor_tensor(dif[:, u], h[:, u, :, 1:S + 1], h[:, u, :, 0:S], ALU.subtract))
                for n, name in enumerate(names):
                    for c in range(KC):
                        ins = dve.scalar_tensor_tensor(mix[:, u, n, c, :], dif[:, u, c, :], vec(st, name, c),
                                                       h[:, u, c, 0:S], ALU.mult, ALU.add)
                return ins

            def time_blend(u, i, s):
                dve.wait_ge(h_ready, seq(u, i) + 1)
                blend(u, s, ("L0_attn_tm_k", "L0_attn_tm_v", "L0_attn_tm_r")).then_inc(mix_ready, 1)
                s.close()

            def exponents(u, i, s):
                k, ww = bank(u, 1), ex[:, u]
                dve.wait_ge(kvr_ready, seq(u, i) + 1)
                for c in range(KC):
                    s.mark(dve.tensor_tensor_scan(top[:, u, c, 1:S + 1], wdec[:, c, :], k[:, c, :], NEG, ALU.add, ALU.max))
                s.after(s.n)
                for c in range(KC):
                    s.mark(dve.scalar_tensor_tensor(q[:, u, c, :], k[:, c, :], vec(st, "L0_attn_time_first", c),
                                                    top[:, u, c, 0:S], ALU.add, ALU.max))
                n_q = s.n
                for c in range(KC):
                    dve.scalar_tensor_tensor(ww[:, 2, c, :], top[:, u, c, 0:S], st.w[:, c:c + 1],
                                             top[:, u, c, 1:S + 1], ALU.add, ALU.subtract)
                dve.tensor_tensor(ww[:, 3], k, top[:, u, :, 1:S + 1], ALU.subtract)
                s.after(n_q)
                for c in range(KC):
                    dve.scalar_tensor_tensor(ww[:, 1, c, :], k[:, c, :], vec(st, "L0_attn_time_first", c),
                                             q[:, u, c, :], ALU.add, ALU.subtract)
                dve.tensor_tensor(ww[:, 0], top[:, u, :, 0:S], q[:, u], ALU.subtract).then_inc(args_ready, 1)

            def sums(u, i, s):
                v = bank(u, 2)
                dve.wait_ge(ex_ready, seq(u, i) + 1)
                n_ev = s.mark(dve.tensor_tensor(e2bv[:, u], ex[:, u, 3], v, ALU.mult))
                for c in range(KC):
                    s.mark(dve.tensor_tensor_scan(den[:, u, c, 1:S + 1], ex[:, u, 2, c, :], ex[:, u, 3, c, :], 0.0,
                                                  ALU.mult, ALU.add))
                n_den = s.n
                s.after(n_ev)
                for c in range(KC):
                    s.mark(dve.tensor_tensor_scan(num[:, u, c, 1:S + 1], ex[:, u, 2, c, :], e2bv[:, u, c, :], 0.0,
                                                  ALU.mult, ALU.add))
                n_num = s.n
                n_y2 = s.mark(dve.tensor_tensor(y2[:, u], ex[:, u, 1], v, ALU.mult))
                s.after(n_den)
                n_q2 = s.mark(dve.tensor_tensor(q[:, u], ex[:, u, 0], den[:, u, :, 0:S], ALU.mult))
                s.after(n_num)
                n_y1 = s.mark(dve.tensor_tensor(y1[:, u], ex[:, u, 0], num[:, u, :, 0:S], ALU.mult))
                s.after(n_q2)
                n_q3 = s.mark(dve.tensor_tensor(q[:, u], q[:, u], ex[:, u, 1], ALU.add))
                s.after(n_y1)
                n_y3 = s.mark(dve.tensor_tensor(y1[:, u], y1[:, u], y2[:, u], ALU.add))
                s.after(n_q3)
                s.mark(dve.reciprocal(q[:, u], q[:, u]))
                s.after(n_y3)
                dve.wait_ge(sr_ready, seq(u, i) + 1)
                n_y4 = s.mark(dve.tensor_tensor(y1[:, u], y1[:, u], sr[:, u], ALU.mult))
                s.after(n_y4)
                dve.tensor_tensor(rw[:, u], y1[:, u], q[:, u], ALU.mult).then_inc(rw_ready, 1)
                s.close()

            def add_time(u, i, s):
                dve.wait_ge(o_ready, seq(u, i) + 1)
                s.do(dve.tensor_tensor(x2[:, u], bank(u, 0), x[:, u], ALU.add))
                dve_stats(dve, st, s, x2[:, u], stats[1], var[1], u, var_ready[1])

            def normal2(u, i):
                dve.wait_ge(rstd_ready[1], seq(u, i) + 1)
                dve_normalize(dve, nrm[:, u], x2[:, u], var[1], rstd[1], u).then_inc(norm2, 1)

            def channel_blend(u, i, s):
                dve.wait_ge(g_ready, seq(u, i) + 1)
                blend(u, s, ("L0_attn_fm_k", "L0_attn_fm_r")).then_inc(gmix_ready, 1)
                s.do(dve.tensor_tensor(x2[:, u], x2[:, u], x[:, u], ALU.add))
                dve.sem_inc(x_free, 1)

            def add_channel(u, i, s):
                dve.wait_ge(sf_ready, seq(u, i) + 1)
                dve.wait_ge(kv_ready, seq(u, i) + 1)
                s.do(dve.tensor_tensor(sf[:, u], sf[:, u], bank(u, 1), ALU.mult))
                dve.sem_inc(kv_taken, 1)
                s.do(dve.tensor_tensor(x2[:, u], x2[:, u], sf[:, u], ALU.add))
                dve_stats(dve, st, s, x2[:, u], stats[2], var[2], u, var_ready[2])
                s.close()

            def normal3(u, i):
                dve.wait_ge(rstd_ready[2], seq(u, i) + 1)
                dve_normalize(dve, st.res[:, bass.ds(TB * seq(u, i), TB), :], x2[:, u], var[2], rstd[2],
                              u).then_inc(x1_ready, 1)

            def half(p, d, a, n):
                sn = None if n is None else Steps(dve, n_steps, seq(*n), BLEND_STEPS)
                sa = None if a is None else Steps(dve, a_steps, seq(*a), TIME_STEPS)
                sd = None if d is None else Steps(dve, d_steps, seq(*d), CHANNEL_STEPS)
                on(d, add_time, sd)
                on(p, normal3)
                on(d, normal2)
                on(d, channel_blend, sd)
                on(a, exponents, sa)
                on(n, stats1, sn)
                on(n, normal1)
                on(a, sums, sa)
                on(n, time_blend, sn)
                on(d, add_channel, sd)

            dve.sem_inc(kv_taken, 1)
            all_halves(dve, half)
            dve.wait_ge(x1_ready, B)


def xattn_stage(nc, st, d, layer):
    masked = layer == 0
    pre = "x0_" if masked else "x1_"
    wq_n, wk_n, wv_n, wo_n = (("L0_xattn_w_q", "L0_xattn_w_k", "L0_xattn_w_v", "L0_xattn_w_o") if masked else
                              ("L1_xattn_Wq", "L1_xattn_Wk", "L1_xattn_Wv", "L1_xattn_Wo"))
    bq_n, bk_n = ("L0_xattn_b_q", "L0_xattn_b_k") if masked else ("L1_xattn_bq", "L1_xattn_bk")
    first_row = 0 if masked else 2
    experts, ecols, topk = (E0, E0P, K0) if masked else (E1, E1, K1)
    macc = st.macc0 if masked else st.macc1
    with ExitStack() as ctx:
        def sb(name, shape, dt=F32):
            return ctx.enter_context(nc.sbuf_tensor(pre + name, shape, dt))

        def sem(name):
            return st.semaphore(nc, pre + name)

        wq, wk, wv = (sb(n, [P, KC, D]) for n in ("wq", "wk", "wv"))
        wo = sb("wo", [P, KC, D])
        wg = sb("wg", [P, KC, ecols])
        rows = sb("rows", [P, 2, D])
        cx = sb("cx", [P, U, KC, S])
        xT = sb("xT", [P, U, KC, S])
        qT = sb("qT", [P, U, KC, S])
        kT = sb("kT", [P, U, KC, S])
        kh, kl = sb("kh", [P, U, KC, S], F32R), sb("kl", [P, U, KC, S], F32R)
        vp = sb("vp", [P, U, TB, HEADS, 32])
        qmh, qml = sb("qmh", [P, U, KC, HPC, S], F32R), sb("qml", [P, U, KC, HPC, S], F32R)
        nmx = sb("nmx", [P, U, TB, P])
        nmT = sb("nmT", [P, U, S], F32R)
        pt = sb("pt", [P, U, 2, TB, 4, S])
        o32 = sb("o32", [P, U, QUADS, S])
        aq = qT.rearrange("p u t (h r) -> p u t h r", r=DH)
        rec = sb("rec", [P, U, TB, HEADS])
        aT = kT
        xin = sb("xin", [P, U, TB, D])
        y = xin
        xn = sb("xn", [P, TB, D])
        stats = sb("stats", [P, U, TB, 6])
        var = sb("var", [P, U, TB, 2])
        rstd = sb("rstd", [P, U, TB])
        lg = sb("lg", [P, U, TB, ecols])
        sc = sb("sc", [P, U, TB, ecols])
        mx8 = sb("mx8", [P, U, TB, 8])
        ix8 = sb("ix8", [P, U, TB, 8], U32)
        ixf = sb("ixf", [P, U, TB, 8])
        hit = sb("hit", [P, U, TB, ecols], BF16)
        pos = sb("pos", [P, U, TB, ecols])
        o_flat = o32.rearrange("p u k s -> p u (k s)")
        oh = o_flat[:, :, 0:TB * topk * ecols].rearrange("p u (t j e) -> p u t j e", t=TB, j=topk)
        junk = o_flat[:, :, 2 * S:2 * S + TB * topk * ecols].rearrange("p u (t j e) -> p u t j e", t=TB, j=topk)
        at = sb("at", [P, U, TB, topk])
        gt = sb("gt", [P, U, TB, topk])
        tmp = sb("tmp", [P, U, TB, topk])
        dst = sb("dst", [P, U, TB, topk], U32)
        if masked:
            count, tiles, first = sb("count", [P, E0P]), sb("tiles", [P, E0P]), sb("first", [P, E0P])
            limits, over = sb("limits", [P, TILES_SHARED - 1]), sb("over", [P, E0P, TILES_SHARED - 1])
            mi = o32.bitcast(I32).rearrange("p u (t h) s -> p (u t) h s", t=QUADS // TB)
            mb = sb("mb", [P, 2, TB, S], BF16)
        else:
            wg_bf = sb("wg_bf", [P, KC, ecols], BF16)
        ps = ctx.enter_context(nc.psum_tensor(pre + "ps", [P, U, 4, 512], F32))

        def bank(u, n):
            return ps[:, u, n, :].rearrange("p (a b) -> p a b", a=2)

        w_loaded = sem("w_loaded")
        cx_loaded = [sem(f"cx_loaded{u}") for u in range(U)]
        preset, mask_ready, mask_loaded = sem("preset"), sem("mask_ready"), sem("mask_loaded")
        t_ready, xT_ready, qkv_ready = sem("t_ready"), sem("xT_ready"), sem("qkv_ready")
        kh_ready = sem("kh_ready")
        qk_ready, vp_ready, qm_ready = sem("qk_ready"), sem("vp_ready"), sem("qm_ready")
        ql_ready, qml_ready, kl_ready = sem("ql_ready"), sem("qml_ready"), sem("kl_ready")
        s_ready, max_ready = sem("s_ready"), sem("max_ready")
        mt_ready, nmT_ready = sem("mt_ready"), sem("nmT_ready")
        st_ready, pt_ready = sem("st_ready"), sem("pt_ready")
        pv_ready, o32_ready, oq_ready = sem("pv_ready"), sem("o32_ready"), sem("oq_ready")
        aq_ready, at_ready, aT_ready = sem("aq_ready"), sem("at_ready"), sem("aT_ready")
        xin_ready = sem("xin_ready")
        y_ready = sem("y_ready")
        varr, rstdr, epsr, xn_ready = sem("var_ready"), sem("rstd_ready"), sem("eps_added"), sem("xn_ready")
        rt_ready, rT_ready, lg_ready = sem("rt_ready"), sem("rT_ready"), sem("lg_ready")
        earg_ready, e_ready = sem("earg_ready"), sem("e_ready")
        hit_ready, pos_ready, dst_ready = sem("hit_ready"), sem("pos_ready"), sem("dst_ready")
        kept, xn_free = sem("kept"), sem("xn_free")
        sent = sem("rows_sent")
        stored = sem("rows_stored")
        a_steps, d_steps = sem("dve_query_steps"), sem("dve_output_steps")
        counted, tiles_ready = sem("counted"), sem("tiles_ready")
        block = ctx.enter_context(nc.Block())
        ctx_v = d["ctx"].rearrange("(k p) n -> p k n", p=P)
        shared_v = st.xs1[SHARED1:SHARED1 + N, :].rearrange("(n p) c -> p n c", p=P)

        GROUPS = QUADS * TB

        def group(u, t):
            return ps[:, u, 2 * t:2 * t + 2].rearrange("p k (a b) -> p (k a) b", a=2)

        def quad(q, u, j):
            return q[:, u, j // 2, 4 * (j % 2):4 * (j % 2) + 4]


        def all_halves(eng, half):
            half((0, 0), None, (1, 0))
            with eng.Fori(0, STEPS - 1) as i:
                half((1, i), (0, i), (0, i + 1))
                half((0, i + 1), (1, i), (1, i + 1))
            half((1, STEPS - 1), (0, STEPS - 1), None)
            half(None, (1, STEPS - 1), None)

        @block.sync
        def _(sp):
            for u in range(U):
                sp.dma_start(cx[:, u], ctx_v[:, :, S * u:S * u + S]).then_inc(cx_loaded[u], 16)
            for t, n in ((wq, wq_n), (wk, wk_n), (wv, wv_n), (wo, wo_n)):
                sp.dma_start(t[:], col(d[n])).then_inc(w_loaded, 16)
            sp.dma_start(rows[:], d["rows"][first_row:first_row + 2, :].partition_broadcast(P)).then_inc(w_loaded, 16)
            if masked:
                sp.dma_start(mi[:, 0], d["mask"].rearrange("(t p) k -> p t k", p=P)).then_inc(mask_loaded, 16)
                sp.dma_start(mi[:, 1], d["mask_t"].rearrange("(t p) k -> p t k", p=P)).then_inc(mask_loaded, 16)
                sp.wait_ge(preset, 3)
                sp.dma_start(wg[:, :, 0:experts], col(d["L0_ffn_router_w"])).then_inc(w_loaded, 16)
            else:
                sp.dma_start(wg_bf[:], col(d["L1_ffn_gate_w"])).then_inc(w_loaded, 16)

            def load(u, i):
                sp.wait_ge(qkv_ready, seq(u, i - 1) + 1)
                sp.dma_start(cx[:, u], ctx_v[:, :, bass.ds(S * seq(u, i), S)]).then_inc(cx_loaded[u], 16)

            def store(u, i):
                sp.wait_ge(xn_ready, seq(u, i) + 1)
                sp.dma_start(shared_v[:, bass.ds(TB * seq(u, i), TB), :], xn[:]).then_inc(stored, 16)

            with sp.Fori(1, STEPS) as i:
                for u in range(U):
                    load(u, i)
                    if not masked:
                        store(u, i - 1)
            if not masked:
                for u in range(U):
                    store(u, STEPS - 1)

        @block.gpsimd
        def _(pool):
            def rows_in(u, i):
                pool.tensor_copy(xin[:, u], st.res[:, bass.ds(TB * seq(u, i), TB), :]).then_inc(xin_ready, 1)

            def mask_low(u, i):
                pool.wait_ge(ql_ready, seq(u, i) + 1)
                for m in range(KC):
                    pool.tensor_tensor(qml[:, u, m], qT[:, u, m, :].unsqueeze(1).to_broadcast([P, HPC, S]),
                                       st.hmask[:].unsqueeze(2).to_broadcast([P, HPC, S]), ALU.mult).then_inc(qml_ready, 1)

            def rstd_of(u, i):
                pool_rstd(pool, st, var, rstd, u, varr, rstdr, epsr, seq(u, i) + 1)

            def normalized(u, i):
                pool.wait_ge(xn_ready, seq(u, i) + 1)
                pool.sem_inc(st.pool_passed, 1)

            def rows_out(u, i):
                here = bass.ds(TB * seq(u, i), TB)
                pool.tensor_copy(st.res[:, here, :], xn[:]).then_inc(kept, 1)

            def slots_out(u, i):
                here = bass.ds(TB * seq(u, i), TB)
                pool.wait_ge(dst_ready, seq(u, i) + 2)
                pool.sem_inc(st.pool_passed, 1)
                if masked:
                    pool.tensor_copy(st.expert0[:, here, :], ixf[:, u, :, 0:K0]).then_inc(kept, 1)
                    pool.tensor_copy(st.rank0[:, here, :], at[:, u]).then_inc(kept, 1)
                    pool.tensor_copy(st.gate0[:, here, :], gt[:, u]).then_inc(kept, 1)
                else:
                    pool.tensor_copy(st.slot1[:, here, :], dst[:, u]).then_inc(kept, 1)
                    pool.tensor_copy(st.gate1[:, here, :], gt[:, u]).then_inc(kept, 1)
                    for t in range(TB):
                        for j in range(topk):
                            pool.indirect_dma_start(
                                out=st.xs1, out_offset=bass.IndirectOffsetOnAxis(ap=dst[:, u, t, j:j + 1], axis=0),
                                in_=xn[:, t, :], in_offset=None, bounds_check=DUMP1 - 1,
                                oob_is_err=False).then_inc(sent, 16)

            def slots_sent(u, i):
                if not masked:
                    pool.wait_ge(sent, 16 * TB * topk * (seq(u, i) + 1))
                    pool.wait_ge(stored, 16 * (seq(u, i) + 1))
                pool.wait_ge(kept, (4 if masked else 3) * (seq(u, i) + 1))
                pool.sem_inc(xn_free, 1)

            pool.sem_inc(xn_free, 1)
            for u in range(U):
                rows_in(u, 0)
            mask_low(0, 0)

            def half(c, d, a):
                on(d, rstd_of)
                if d is not None:
                    on(d, normalized)
                    on(a, rows_in)
                on(d, rows_out)
                on(d, slots_out)
                on(a, mask_low)
                on(d, slots_sent)

            all_halves(pool, half)

        @block.tensor
        def _(pe):
            pe.wait_ge(w_loaded, 16 * 6)
            pe.wait_ge(preset, 3)
            if masked:
                pe.wait_ge(mask_ready, 2 * TB)
            else:
                pe.wait_ge(mask_ready, 1)

            def turn(dst, src):
                for t in range(TB):
                    for c in range(KC):
                        ins = pe.transpose(dst[:, c, t * P:t * P + P], src[:, t, c * P:c * P + P], st.ident[:])
                return ins

            def turn_in(u, i):
                pe.wait_ge(xin_ready, seq(u, i) + 1)
                turn(bank(u, 0), xin[:, u]).then_inc(t_ready, 1)

            def project(u, i):
                pe.wait_ge(cx_loaded[u], 16 * i + 16)
                pe.wait_ge(xT_ready, seq(u, i) + 1)
                for n, w, a in ((1, wq, xT), (2, wk, cx)):
                    for m in range(KC):
                        for c in range(KC):
                            pe.matmul(bank(u, n)[:, m, :], w[:, c, m * P:m * P + P], a[:, u, c, :],
                                      start=(c == 0), stop=(c == KC - 1))
                for t in range(TB):
                    for c in range(KC):
                        ins = pe.matmul(bank(u, 3)[:, t, :], cx[:, u, c, t * P:t * P + P], wv[:, c, :],
                                        start=(c == 0), stop=(c == KC - 1))
                ins.then_inc(qkv_ready, 1)

            def query_scores(u, i, g):
                j, t = g // TB, g % TB
                if g == 0:
                    pe.wait_ge(qm_ready, seq(u, i) + 1)
                    pe.wait_ge(kh_ready, seq(u, i) + 1)
                    pe.wait_ge(vp_ready, seq(u, i) + 1)
                elif g >= TB:
                    pe.wait_ge(max_ready, GROUPS * seq(u, i) + g - TB + 1)
                for k in range(4):
                    if masked:
                        pe.matmul(group(u, t)[:, k, :], st.identb[:], mb[:, 0, t, :], start=True, stop=False)
                    ins = pe.matmul(group(u, t)[:, k, :], quad(qmh, u, j)[:, k, t * P:t * P + P], kh[:, u, j // 2, :],
                                    start=not masked, stop=True)
                ins.then_inc(s_ready, 1)

            def turn_maxima(u, i):
                pe.wait_ge(max_ready, GROUPS * (seq(u, i) + 1))
                for t in range(TB):
                    ins = pe.transpose(bank(u, 0)[:, 0, t * P:t * P + P], nmx[:, u, t, :], st.ident[:])
                ins.then_inc(mt_ready, 1)

            def key_scores(u, i, g):
                j, t = g // TB, g % TB
                if g == 0:
                    pe.wait_ge(nmT_ready, seq(u, i) + 1)
                    pe.wait_ge(kl_ready, seq(u, i) + 1)
                elif j and t == 0:
                    pe.wait_ge(pt_ready, GROUPS * seq(u, i) + g - TB + 1)
                elif j:
                    pe.wait_ge(o32_ready, QUADS * seq(u, i) + j)
                if g % (GROUPS // KC) == 0:
                    pe.wait_ge(qml_ready, KC * seq(u, i) + j // 2 + 1)
                for k in range(4):
                    if masked:
                        pe.matmul(group(u, t)[:, k, :], st.identb[:], mb[:, 1, t, :], start=True, stop=False)
                    for n, (kp, qp) in enumerate(((kh, qmh), (kh, qml), (kl, qmh))):
                        pe.matmul(group(u, t)[:, k, :], kp[:, u, j // 2, t * P:t * P + P], quad(qp, u, j)[:, k, :],
                                  start=not masked and n == 0, stop=False)
                    ins = pe.matmul(group(u, t)[:, k, :], st.selrow[:, 4 * j + k, :], nmT[:, u, :], start=False, stop=True)
                ins.then_inc(st_ready, 1)

            def weigh(u, i, j):
                pe.wait_ge(pt_ready, GROUPS * seq(u, i) + j * TB + TB)
                for t in range(TB):
                    for k in range(4):
                        ins = pe.matmul(bank(u, 2)[32 * k:32 * k + 32, 0, :], vp[:, u, t, 4 * j + k, :],
                                        pt[:, u, j % 2, t, k, :], start=(t == 0), stop=(t == TB - 1))
                ins.then_inc(pv_ready, 1)

            def turn_output(u, i):
                pe.wait_ge(o32_ready, QUADS * (seq(u, i) + 1))
                for t in range(TB):
                    for qd in range(QUADS):
                        ins = pe.transpose(ps[:, u, 2 + t, qd * P:qd * P + P], o32[:, u, qd, t * P:t * P + P], st.ident[:])
                ins.then_inc(oq_ready, 1)

            def turn_scaled(u, i):
                pe.wait_ge(aq_ready, seq(u, i) + 1)
                turn(bank(u, 0), aq[:, u].rearrange("p t h r -> p t (h r)")).then_inc(at_ready, 1)

            def output(u, i):
                pe.wait_ge(aT_ready, seq(u, i) + 1)
                for t in range(TB):
                    for c in range(KC):
                        ins = pe.matmul(bank(u, 1)[:, t, :], aT[:, u, c, t * P:t * P + P], wo[:, c, :],
                                        start=(c == 0), stop=(c == KC - 1))
                ins.then_inc(y_ready, 1)

            def turn_rows(u, i):
                pe.wait_ge(xn_ready, seq(u, i) + 1)
                turn(bank(u, 2), xn).then_inc(rt_ready, 1)

            def route(u, i):
                pe.wait_ge(rT_ready, seq(u, i) + 1)
                for t in range(TB):
                    for c in range(KC):
                        ins = pe.matmul(bank(u, 3)[:, t, 0:ecols], xT[:, u, c, t * P:t * P + P], wg[:, c, :],
                                        start=(c == 0), stop=(c == KC - 1))
                ins.then_inc(lg_ready, 1)

            def rank(u, i):
                pe.wait_ge(hit_ready, seq(u, i) + 1)
                for t in range(TB):
                    place = bank(u, 0)[:, t, 0:ecols]
                    pe.matmul(place, st.ones[:], macc[:, u, :], start=True, stop=False)
                    if t == 1:
                        pe.matmul(place, st.ones[:], hit[:, u, 0, :], start=False, stop=False)
                    ins = pe.matmul(place, st.lower[:], hit[:, u, t, :], start=False, stop=True)
                ins.then_inc(pos_ready, 1)

            turn_in(0, 0)
            project(0, 0)
            for g in range(GROUPS):
                query_scores(0, 0, g)
            turn_maxima(0, 0)

            def half(c, d, a):
                on(c, key_scores, 0)
                on(d, turn_output)
                on(c, key_scores, 1)
                on(d, turn_scaled)
                on(c, key_scores, 2)
                on(d, output)
                on(c, weigh, 0)
                on(c, key_scores, 3)
                on(d, turn_rows)
                on(c, key_scores, 4)
                on(d, route)
                on(a, turn_in)
                on(c, weigh, 1)
                on(c, key_scores, 5)
                on(a, project)
                on(d, rank)
                on(c, key_scores, 6)
                on(c, weigh, 2)
                on(c, key_scores, 7)
                on(a, query_scores, 0)
                on(a, query_scores, 1)
                on(a, query_scores, 2)
                on(a, query_scores, 3)
                on(a, query_scores, 4)
                on(a, query_scores, 5)
                on(a, query_scores, 6)
                on(a, query_scores, 7)
                on(c, weigh, 3)
                on(a, turn_maxima)

            all_halves(pe, half)
            if masked:
                pe.wait_ge(counted, 1)
                pe.matmul(bank(0, 1)[:, 0, 0:E0P], st.ones[:], macc[:, 0, :], start=True, stop=True).then_inc(tiles_ready, 1)

        @block.scalar
        def _(act):
            def keep_rows(u, i):
                act.wait_ge(t_ready, seq(u, i) + 1)
                act.activation(xT[:, u], bank(u, 0), ACT.Copy).then_inc(xT_ready, 1)

            def keep_queries(u, i):
                act.wait_ge(qkv_ready, seq(u, i) + 1)
                for c in range(KC):
                    act.activation(qT[:, u, c, :], bank(u, 1)[:, c, :], ACT.Identity, bias=vec(st, bq_n, c), scale=1.0)
                for c in range(KC):
                    ins = act.activation(kl[:, u, c, :], bank(u, 1)[:, c, :], ACT.Identity, bias=vec(st, bq_n, c), scale=1.0)
                ins.then_inc(qk_ready, 1)

            def keep_keys(u, i):
                for c in range(KC):
                    act.activation(kh[:, u, c, :], bank(u, 2)[:, c, :], ACT.Identity, bias=vec(st, bk_n, c), scale=1.0)
                for c in range(KC):
                    ins = act.activation(kT[:, u, c, :], bank(u, 2)[:, c, :], ACT.Identity, bias=vec(st, bk_n, c), scale=1.0)
                ins.then_inc(kh_ready, 1)

            def keep_maxima(u, i):
                act.wait_ge(mt_ready, seq(u, i) + 1)
                act.activation(nmT[:, u, :], bank(u, 0)[:, 0, :], ACT.Copy).then_inc(nmT_ready, 1)

            def weights(u, i, g):
                j, t = g // TB, g % TB
                act.wait_ge(st_ready, GROUPS * seq(u, i) + g + 1)
                act.activation(pt[:, u, j % 2, t].rearrange("p k q -> p (k q)"),
                               ps[:, u, 2 * t:2 * t + 2].rearrange("p k q -> p (k q)"), ACT.Exp, scale=SCALE).then_inc(pt_ready, 1)

            def keep_values(u, i, j):
                act.wait_ge(pv_ready, QUADS * seq(u, i) + j + 1)
                act.activation(o32[:, u, j, :], bank(u, 2)[:, 0, :], ACT.Copy).then_inc(o32_ready, 1)

            def keep_scaled(u, i):
                act.wait_ge(at_ready, seq(u, i) + 1)
                act.activation(aT[:, u], bank(u, 0), ACT.Copy).then_inc(aT_ready, 1)

            def keep_normal(u, i):
                act.wait_ge(rt_ready, seq(u, i) + 1)
                act.activation(xT[:, u], bank(u, 2), ACT.Copy).then_inc(rT_ready, 1)

            def gates(u, i):
                act.wait_ge(earg_ready, seq(u, i) + 1)
                if masked:
                    act.activation(tmp[:, u, :, 0:1], tmp[:, u, :, 0:1], ACT.Exp).then_inc(e_ready, 1)
                else:
                    act.activation(sc[:, u], sc[:, u], ACT.Exp).then_inc(e_ready, 1)

            keep_rows(0, 0)
            keep_queries(0, 0)
            keep_keys(0, 0)
            keep_maxima(0, 0)

            def half(c, d, a):
                on(c, weights, 0)
                on(c, weights, 1)
                on(d, keep_scaled)
                on(c, weights, 2)
                on(c, keep_values, 0)
                on(c, weights, 3)
                on(d, keep_normal)
                on(c, weights, 4)
                on(d, gates)
                on(a, keep_rows)
                on(c, keep_values, 1)
                on(c, weights, 5)
                on(a, keep_queries)
                on(a, keep_keys)
                on(c, keep_values, 2)
                on(c, weights, 6)
                on(c, weights, 7)
                on(c, keep_values, 3)
                on(a, keep_maxima)

            all_halves(act, half)

        @block.vector
        def _(dve):
            dve.memset(vp[:, :, :, :, DH:32], 0.0).then_inc(preset, 1)
            dve.memset(nmx[:], 0.0).then_inc(preset, 1)
            dve.memset(wg[:], 0.0).then_inc(preset, 1)
            dve.wait_ge(preset, 3)
            dve.memset(vp[:, :, :, :, DH:DH + 1], 1.0).then_inc(preset, 1)
            dve.wait_ge(w_loaded, 16 * 6)
            if masked:
                dve.memset(lg[:], NEG).then_inc(preset, 1)
                dve.wait_ge(preset, 5)
                dve.wait_ge(mask_loaded, 32)
                for n in range(2):
                    for t in range(TB):
                        dve.tensor_scalar(mb[:, n, t, :], mi[:, n, t, :], 0, NEG, ALU.is_equal,
                                          ALU.mult).then_inc(mask_ready, 1)
            else:
                dve.wait_ge(preset, 4)
                dve.tensor_copy(wg[:], wg_bf[:]).then_inc(mask_ready, 1)
            dve.sem_inc(dst_ready, 1)

            def values(u, i):
                dve.wait_ge(qkv_ready, seq(u, i) + 1)
                for t in range(TB):
                    ins = dve.tensor_tensor(vp[:, u, t, :, 0:DH], bank(u, 3)[:, t, :].rearrange("p (h r) -> p h r", r=DH),
                                            rows[:, 0, :].rearrange("p (h r) -> p h r", r=DH), ALU.add)
                ins.then_inc(vp_ready, 1)

            def masked_queries(u, i):
                s = Steps(dve, a_steps, seq(u, i), 1)
                dve.wait_ge(qk_ready, seq(u, i) + 1)
                for m in range(KC):
                    for k in range(HPC):
                        ins = dve.tensor_scalar(qmh[:, u, m, k, :], kl[:, u, m, :].bitcast(F32), st.hmask[:, k:k + 1], None,
                                                ALU.mult)
                ins.then_inc(qm_ready, 1)
                n_low = s.mark(dve.tensor_tensor(qT[:, u], qT[:, u], kl[:, u].bitcast(F32), ALU.subtract))
                s.after(n_low)
                dve.sem_inc(ql_ready, 1)
                dve.wait_ge(qm_ready, seq(u, i) + 1)
                dve.wait_ge(kh_ready, seq(u, i) + 1)
                dve.tensor_tensor(kl[:, u], kT[:, u], kh[:, u].bitcast(F32), ALU.subtract).then_inc(kl_ready, 1)
                s.close()

            def maxima(u, i, g):
                j, t = g // TB, g % TB
                dve.wait_ge(s_ready, GROUPS * seq(u, i) + g + 1)
                dve.tensor_reduce(nmx[:, u, t, 4 * j:4 * j + 4], group(u, t), AX.X, ALU.max,
                                  negate=True).then_inc(max_ready, 1)

            def scaled(u, i, s):
                oq = ps[:, u, 2:4].rearrange("p t (h r) -> p t h r", r=32)
                s.mark(dve.tensor_tensor(y[:, u], xin[:, u], rows[:, 1:2, :].to_broadcast([P, TB, D]), ALU.add))
                dve.wait_ge(oq_ready, seq(u, i) + 1)
                s.do(dve.reciprocal(rec[:, u], oq[:, :, :, DH]))
                for t in range(TB):
                    ins = dve.tensor_tensor(aq[:, u, t], oq[:, t, :, 0:DH],
                                            rec[:, u, t].unsqueeze(2).to_broadcast([P, HEADS, DH]), ALU.mult)
                ins.then_inc(aq_ready, 1)

            def add_output(u, i, s):
                dve.wait_ge(y_ready, seq(u, i) + 1)
                s.do(dve.tensor_tensor(y[:, u], y[:, u], bank(u, 1), ALU.add))
                dve_stats(dve, st, s, y[:, u], stats, var, u, varr)

            def normalize(u, i):
                dve.wait_ge(rstdr, seq(u, i) + 1)
                dve.wait_ge(xn_free, seq(u, i) + 1)
                dve_normalize(dve, xn, y[:, u], var, rstd, u).then_inc(xn_ready, 1)

            def choose(u, i, s):
                logits = bank(u, 3)[:, :, 0:experts]
                dve.wait_ge(lg_ready, seq(u, i) + 1)
                if masked:
                    s.do(dve.tensor_copy(lg[:, u, :, 0:experts], logits))
                else:
                    dve.tensor_scalar(sc[:, u], logits, -1.0, EXP_MAX, ALU.mult, ALU.min).then_inc(earg_ready, 1)
                    dve.wait_ge(e_ready, seq(u, i) + 1)
                    s.do(dve.tensor_scalar(sc[:, u], sc[:, u], 1.0, None, ALU.add))
                    s.do(dve.reciprocal(sc[:, u], sc[:, u]))
                    s.do(dve.tensor_tensor(lg[:, u], sc[:, u],
                                           st.ebias[:].unsqueeze(1).to_broadcast([P, TB, E1]), ALU.add))
                dve.sem_inc(st.dve_passed, 1)
                for t in range(TB):
                    n_max = s.mark(dve.max(mx8[:, u, t, :], lg[:, u, t, :]))
                s.after(n_max)
                dve.sem_inc(st.dve_passed, 1)
                for t in range(TB):
                    n_max = s.mark(dve.max_index(ix8[:, u, t, :], mx8[:, u, t, :], lg[:, u, t, :]))
                s.after(n_max)
                if masked:
                    dve.tensor_tensor(tmp[:, u, :, 0], mx8[:, u, :, 1], mx8[:, u, :, 0], ALU.subtract).then_inc(earg_ready, 1)
                s.do(dve.tensor_copy(ixf[:, u], ix8[:, u]))
                for t in range(TB):
                    for j in range(topk):
                        s.mark(dve.tensor_scalar(oh[:, u, t, j, :], st.iota[:, 0:ecols], ixf[:, u, t, j:j + 1], None,
                                                 ALU.is_equal))
                s.after(s.n)
                with nc.allow_low_precision(reason="zeros and ones are exact in bfloat16"):
                    for t in range(TB):
                        s.mark(dve.tensor_reduce(hit[:, u, t, :], oh[:, u, t].rearrange("p j e -> p e j"), AX.X,
                                                 ALU.add))
                s.after(s.n)
                if u == 1:
                    dve.wait_ge(pos_ready, seq(0, i) + 1)
                s.do(dve.tensor_tensor(macc[:, 1 - u, :], macc[:, u, :], hit[:, u, 0, :], ALU.add))
                s.do(dve.tensor_tensor(macc[:, 1 - u, :], macc[:, 1 - u, :], hit[:, u, 1, :], ALU.add))
                dve.sem_inc(hit_ready, 1)
                if masked:
                    dve.wait_ge(e_ready, seq(u, i) + 1)
                    s.do(dve.tensor_scalar(tmp[:, u, :, 1], tmp[:, u, :, 0], 1.0, None, ALU.add))
                    s.do(dve.reciprocal(gt[:, u, :, 0], tmp[:, u, :, 1]))
                    s.do(dve.tensor_tensor(gt[:, u, :, 1], gt[:, u, :, 0], tmp[:, u, :, 0], ALU.mult))
                else:
                    for t in range(TB):
                        s.mark(dve.tensor_tensor(junk[:, u, t], oh[:, u, t],
                                                 sc[:, u, t, :].unsqueeze(1).to_broadcast([P, topk, ecols]), ALU.mult))
                    s.after(s.n)
                    s.do(dve.tensor_reduce(gt[:, u], junk[:, u], AX.X, ALU.add))
                    s.do(dve.tensor_reduce(tmp[:, u, :, 0], gt[:, u], AX.X, ALU.add))
                    s.do(dve.tensor_scalar(tmp[:, u, :, 0], tmp[:, u, :, 0], 1e-12, None, ALU.max))
                    s.do(dve.reciprocal(tmp[:, u, :, 1], tmp[:, u, :, 0]))
                    s.do(dve.tensor_tensor(gt[:, u], gt[:, u], tmp[:, u, :, 1:2].to_broadcast([P, TB, topk]), ALU.mult))

            def place(u, i, s):
                dve.wait_ge(pos_ready, seq(u, i) + 1)
                before = bank(u, 0)[:, :, 0:ecols]
                if masked:
                    s.do(dve.tensor_copy(pos[:, u], before))
                else:
                    s.do(dve.tensor_tensor(pos[:, u], before, st.base1[:].unsqueeze(1).to_broadcast([P, TB, E1]), ALU.add))
                if not masked:
                    s.do(dve.tensor_scalar(lg[:, u], before, CAP1 - 0.5, FAR, ALU.is_gt, ALU.mult))
                    s.do(dve.tensor_tensor(pos[:, u], pos[:, u], lg[:, u], ALU.add))
                for t in range(TB):
                    s.mark(dve.tensor_tensor(junk[:, u, t], oh[:, u, t],
                                             pos[:, u, t, :].unsqueeze(1).to_broadcast([P, topk, ecols]), ALU.mult))
                s.after(s.n)
                if masked:
                    dve.tensor_reduce(at[:, u], junk[:, u], AX.X, ALU.add).then_inc(dst_ready, 1)
                else:
                    s.do(dve.tensor_reduce(at[:, u], junk[:, u], AX.X, ALU.add))
                    s.do(dve.tensor_scalar(at[:, u], at[:, u], float(DUMP1), None, ALU.min))
                    s.do(dve.tensor_scalar(tmp[:, u], at[:, u], DUMP1 - 0.5, None, ALU.is_lt))
                    s.do(dve.tensor_tensor(gt[:, u], gt[:, u], tmp[:, u], ALU.mult))
                    dve.tensor_copy(dst[:, u], at[:, u]).then_inc(dst_ready, 1)
                s.close()

            values(0, 0)
            masked_queries(0, 0)
            for g in range(GROUPS):
                maxima(0, 0, g)

            def half(c, d, a):
                s = None if d is None else Steps(dve, d_steps, seq(*d), DVE_STEPS[layer])
                on(d, scaled, s)
                on(d, add_output, s)
                on(d, normalize)
                on(d, choose, s)
                on(d, place, s)
                on(a, values)
                on(a, masked_queries)
                for g in range(GROUPS):
                    on(a, maxima, g)

            all_halves(dve, half)
            if masked:
                dve.wait_ge(pos_ready, B)
                dve.sem_inc(counted, 1)
                dve.wait_ge(tiles_ready, 1)
                dve.tensor_copy(count[:], bank(0, 1)[:, 0, 0:E0P]).then_inc(counted, 1)
                dve.tensor_scalar(limits[:], st.iota[:, 1:TILES_SHARED], float(S), None, ALU.mult).then_inc(counted, 1)
                dve.wait_ge(counted, 3)
                dve.tensor_tensor(over[:], count[:].unsqueeze(2).to_broadcast([P, E0P, TILES_SHARED - 1]),
                                  limits[:].unsqueeze(1).to_broadcast([P, E0P, TILES_SHARED - 1]),
                                  ALU.is_gt).then_inc(counted, 1)
                dve.wait_ge(counted, 4)
                dve.tensor_reduce(tiles[:], over[:], AX.X, ALU.add).then_inc(counted, 1)
                dve.wait_ge(counted, 5)
                dve.tensor_scalar(tiles[:], tiles[:], 1.0, None, ALU.add).then_inc(counted, 1)
                dve.memset(first[:, 0:1], 0.0).then_inc(counted, 1)
                dve.wait_ge(counted, 7)
                dve.tensor_tensor_scan(first[:, 1:1 + E0], tiles[:, 0:E0], st.zero[:, 0:E0], 0.0,
                                       ALU.add, ALU.add).then_inc(counted, 1)
                dve.wait_ge(counted, 8)
                dve.tensor_copy(st.tile0[:], first[:]).then_inc(counted, 1)
                dve.tensor_copy(st.tiles0[:], tiles[:, 0:E0]).then_inc(counted, 1)
                dve.tensor_scalar(first[:], first[:], float(S), None, ALU.mult).then_inc(counted, 1)
                dve.wait_ge(counted, 11)
                dve.tensor_tensor(count[:], count[:], first[:], ALU.add).then_inc(counted, 1)
                dve.wait_ge(counted, 12)
                dve.tensor_copy(st.end0[:], count[:, 0:E0]).then_inc(counted, 1)
                dve.wait_ge(kept, 4 * B)
                pick = pt.rearrange("p u b t k s -> p (u b t k s)")[:, 0:NBLK * K0 * E0P].rearrange("p (n e) -> p n e", e=E0P)
                dve.tensor_tensor(pick, st.expert0[:].rearrange("p n j -> p (n j)").unsqueeze(2).to_broadcast([P, NBLK * K0, E0P]),
                                  st.iota[:, 0:E0P].unsqueeze(1).to_broadcast([P, NBLK * K0, E0P]),
                                  ALU.is_equal).then_inc(counted, 1)
                dve.wait_ge(counted, 14)
                dve.tensor_tensor(pick, pick, first[:].unsqueeze(1).to_broadcast([P, NBLK * K0, E0P]), ALU.mult).then_inc(counted, 1)
                dve.wait_ge(counted, 15)
                dve.tensor_reduce(st.expert0[:].rearrange("p n j -> p (n j)"), pick, AX.X, ALU.add).then_inc(counted, 1)
                dve.wait_ge(counted, 16)
                dve.tensor_tensor(st.rank0[:], st.rank0[:], st.expert0[:], ALU.add).then_inc(counted, 1)
                dve.wait_ge(counted, 17)
                dve.tensor_copy(st.slot0[:], st.rank0[:]).then_inc(counted, 1)
                dve.wait_ge(counted, 18)


def moe0_stage(nc, st, d):
    with ExitStack() as ctx:
        def sb(name, shape, dt=F32):
            return ctx.enter_context(nc.sbuf_tensor("m0_" + name, shape, dt))

        def sem(name):
            return st.semaphore(nc, "m0_" + name)

        raw = sb("raw", [P, 3, FC * D])
        w_hi, w_lo = sb("w_hi", [P, 2, 3, FC * D], F32R), sb("w_lo", [P, 2, 3, FC * D], F32R)
        x = sb("x", [P, TB, D])
        idx = sb("idx", [P, TB, K0], U32)
        x_hi, x_lo = sb("x_hi", [P, KC, S], F32R), sb("x_lo", [P, KC, S], F32R)
        sg = sb("sg", [P, 4, S])
        h = sb("h", [P, 4, S])
        h_hi, h_lo = sb("h_hi", [P, FC, S], F32R), sb("h_lo", [P, FC, S], F32R)
        y = sb("y", [P, TB, D])
        gu = ctx.enter_context(nc.psum_tensor("m0_gu", [P, 4, 2, S], F32))
        xp = ctx.enter_context(nc.psum_tensor("m0_xp", [P, KC, S], F32))
        yp = ctx.enter_context(nc.psum_tensor("m0_yp", [P, TB, 512], F32))
        raw_loaded, first_hi, first_lo = sem("raw_loaded"), sem("first_hi_ready"), sem("first_lo_ready")
        hi_ready, w_ready = sem("w_hi_ready"), sem("w_ready")
        padded, idx_ready, scattered = sem("slots_padded"), sem("idx_ready"), sem("rows_scattered")
        x_ready, t_ready, xh_ready, xl_ready = sem("x_ready"), sem("t_ready"), sem("xh_ready"), sem("xl_ready")
        gu_ready, silu_ready, h_ready = sem("gu_ready"), sem("silu_ready"), sem("h_ready")
        down_done, y_taken, y_stored = sem("down_done"), sem("y_taken"), sem("y_stored")
        steps = sem("dve_steps")
        block = ctx.enter_context(nc.Block())
        names = ("L0_ffn_w_gate", "L0_ffn_w_up", "L0_ffn_w_down")

        def tiles_of(eng, e):
            return (eng.value_load(st.tile0[0:1, bass.ds(e, 1)], min_val=0, max_val=TILES0_MAX),
                    eng.value_load(st.tiles0[0:1, bass.ds(e, 1)], min_val=1, max_val=TILES_SHARED))

        def all_tiles(eng):
            return eng.value_load(st.tile0[0:1, E0:E0 + 1], min_val=TILES0_MIN, max_val=TILES0_MAX)

        def rows(dram, row):
            return dram[bass.ds(row, S), :].rearrange("(n p) c -> p n c", p=P)

        def load_raw(eng, w):
            for n, name in enumerate(names):
                src = d[name].rearrange("e (k p) n -> p e k n", p=P)
                eng.dma_start(raw[:, n].rearrange("p (k n) -> p k n", k=src.shape[2]),
                              src[:, bass.ds(w, 1)].squeeze(1)).then_inc(raw_loaded, 16)

        def over_experts(eng, body):
            with eng.Fori(0, E0 // 2) as q:
                body(2 * q, 1, True)
                body(2 * q + 1, 0, True)
            body(E0 - 1, 1, False)

        @block.sync
        def _(sp):
            for e in range(E0):
                end = sp.value_load(st.end0[0:1, e:e + 1], min_val=0, max_val=TILES0_MAX * S)
                sp.dma_start(rows(st.xs0, end), st.zero[:].unsqueeze(1).to_broadcast([P, TB, D])).then_inc(padded, 16)
                sp.wait_ge(padded, 16 * (e + 1))
            total = all_tiles(sp)
            sp.dma_start(rows(st.xs0, total * S), st.zero[:].unsqueeze(1).to_broadcast([P, TB, D])).then_inc(padded, 16)
            sp.sem_inc(y_stored, 1)
            sp.wait_ge(t_ready, TILES_SHARED)
            sp.wait_ge(scattered, 16 * TB * K0 * TILES_SHARED)
            sp.dma_start(x[:], rows(st.xs0, 0)).then_inc(x_ready, 16)
            with sp.Fori(0, total) as j:
                sp.wait_ge(t_ready, TILES_SHARED + j + 1)
                sp.dma_start(x[:], rows(st.xs0, (j + 1) * S)).then_inc(x_ready, 16)
                sp.wait_ge(y_taken, TILES_SHARED + j + 2)
                sp.dma_start(rows(st.ys0, j * S), y[:]).then_inc(y_stored, 16)
            sp.wait_ge(y_stored, 16 * total + 1)
            sp.sem_inc(st.sp_passed, 1)

        @block.gpsimd
        def _(pool):
            def split(e, b, free):
                if free is not None:
                    pool.wait_ge(down_done, free)
                pool.wait_ge(raw_loaded, 16 * 3 * (e + 2))
                pool.sem_inc(st.pool_passed, 1)
                for n in range(3):
                    pool.tensor_copy(w_hi[:, b, n], raw[:, n]).then_inc(hi_ready, 1)
                for n in range(3):
                    pool.wait_ge(hi_ready, 3 * e + n + 1)
                    pool.tensor_tensor(w_lo[:, b, n], raw[:, n], w_hi[:, b, n].bitcast(F32), ALU.subtract).then_inc(w_ready, 1)

            def send(t):
                pool.tensor_copy(x[:], st.res[:, bass.ds(TB * t, TB), :]).then_inc(x_ready, 16)
                pool.tensor_copy(idx[:], st.slot0[:, bass.ds(TB * t, TB), :]).then_inc(idx_ready, 1)
                pool.wait_ge(idx_ready, t + 1)
                pool.wait_ge(x_ready, 16 * (t + 1))
                pool.sem_inc(st.pool_passed, 1)
                for n in range(TB):
                    for j in range(K0):
                        pool.indirect_dma_start(
                            out=st.xs0, out_offset=bass.IndirectOffsetOnAxis(ap=idx[:, n, j:j + 1], axis=0),
                            in_=x[:, n, :], in_offset=None).then_inc(scattered, 16)
                pool.wait_ge(scattered, 16 * TB * K0 * (t + 1))

            pool.wait_ge(padded, 16 * (E0 + 1))
            send(0)
            split(0, 1, None)
            with pool.Fori(1, TILES_SHARED) as t:
                pool.wait_ge(t_ready, t)
                pool.sem_inc(st.pool_passed, 1)
                send(t)

            def next_weights(e, b, more):
                if more:
                    first = pool.value_load(st.tile0[0:1, bass.ds(e, 1)], min_val=0, max_val=TILES0_MAX)
                    split(e + 1, 1 - b, TILES_SHARED + first)

            over_experts(pool, next_weights)

        @block.tensor
        def _(pe):
            def transpose(t):
                pe.wait_ge(x_ready, 16 * (t + 1))
                for n in range(TB):
                    for c in range(KC):
                        ins = pe.transpose(xp[:, c, n * P:n * P + P], x[:, n, c * P:c * P + P], st.ident[:])
                ins.then_inc(t_ready, 1)

            def tile(t, b):
                wh = [w_hi[:, b, n].rearrange("p (c f) -> p c f", f=f) for n, f in enumerate((F, F, D))]
                wl = [w_lo[:, b, n].rearrange("p (c f) -> p c f", f=f) for n, f in enumerate((F, F, D))]

                def down(m):
                    pe.wait_ge(h_ready, FC * t + m + 1)
                    if m == 0:
                        pe.wait_ge(y_taken, t + 1)
                    for n in range(TB):
                        for k, (hp, wp) in enumerate(((h_hi, wh), (h_hi, wl), (h_lo, wh))):
                            ins = pe.matmul(yp[:, n, 0:D], hp[:, m, n * P:n * P + P], wp[2][:, m, :],
                                            start=(m == 0 and k == 0), stop=(m == FC - 1 and k == 2))
                    return ins

                pe.wait_ge(xl_ready, t + 1)
                for m in range(FC):
                    if m >= 4:
                        pe.wait_ge(h_ready, FC * t + m - 3)
                    for n in range(2):
                        for c in range(KC):
                            for k, (wp, xp_) in enumerate(((wh, x_hi), (wl, x_hi), (wh, x_lo))):
                                ins = pe.matmul(gu[:, m % 4, n, :], wp[n][:, c, m * P:m * P + P], xp_[:, c, :],
                                                start=(c == 0 and k == 0), stop=(c == KC - 1 and k == 2))
                    ins.then_inc(gu_ready, 1)
                    if m >= 2:
                        down(m - 2)
                transpose(t + 1)
                down(FC - 2)
                down(FC - 1).then_inc(down_done, 1)

            transpose(0)
            pe.wait_ge(first_lo, 3)
            with pe.Fori(0, TILES_SHARED) as t:
                tile(t, 0)

            def expert(e, b, more):
                first, count = tiles_of(pe, e)
                pe.wait_ge(w_ready, 3 * (e + 1))
                pe.sem_inc(st.pe_passed, 1)
                with pe.Fori(0, count) as k:
                    tile(TILES_SHARED + first + k, b)

            over_experts(pe, expert)

        @block.scalar
        def _(act):
            load_raw(act, 0)
            act.wait_ge(raw_loaded, 16 * 3)
            for n in range(3):
                act.activation(w_hi[:, 0, n], raw[:, n], ACT.Copy).then_inc(first_hi, 1)

            def part(t):
                act.wait_ge(t_ready, t + 1)
                act.activation(x_hi[:], xp[:], ACT.Copy).then_inc(xh_ready, 1)

            def tile(t):
                for m in range(FC):
                    act.wait_ge(gu_ready, FC * t + m + 1)
                    act.activation(sg[:, m % 4, :], gu[:, m % 4, 0, :], ACT.Silu).then_inc(silu_ready, 1)
                part(t + 1)

            part(0)
            act.wait_ge(first_lo, 3)
            load_raw(act, 1)
            with act.Fori(0, TILES_SHARED) as t:
                tile(t)

            def expert(e, b, more):
                first, count = tiles_of(act, e)
                if more:
                    act.wait_ge(w_ready, 3 * (e + 1))
                    act.sem_inc(st.act_passed, 1)
                    load_raw(act, e + 2)
                with act.Fori(0, count) as k:
                    tile(TILES_SHARED + first + k)

            over_experts(act, expert)

        @block.vector
        def _(dve):
            dve.sem_inc(y_taken, 1)

            def part(t):
                dve.wait_ge(xh_ready, t + 1)
                dve.tensor_tensor(x_lo[:], xp[:], x_hi[:].bitcast(F32), ALU.subtract).then_inc(xl_ready, 1)

            def hidden(t):
                s = Steps(dve, steps, t, 2 * FC)
                for m in range(FC):
                    dve.wait_ge(silu_ready, FC * t + m + 1)
                    s.do(dve.tensor_tensor(h[:, m % 4, :], sg[:, m % 4, :], gu[:, m % 4, 1, :], ALU.mult))
                    s.do(dve.tensor_copy(h_hi[:, m, :], h[:, m % 4, :]))
                    dve.tensor_tensor(h_lo[:, m, :], h[:, m % 4, :], h_hi[:, m, :].bitcast(F32), ALU.subtract).then_inc(h_ready, 1)
                s.close()
                part(t + 1)
                dve.wait_ge(down_done, t + 1)

            for n in range(3):
                dve.wait_ge(first_hi, n + 1)
                dve.tensor_tensor(w_lo[:, 0, n], raw[:, n], w_hi[:, 0, n].bitcast(F32), ALU.subtract).then_inc(first_lo, 1)
            part(0)
            with dve.Fori(0, TILES_SHARED) as t:
                hidden(t)
                here = st.res[:, bass.ds(TB * t, TB), :]
                dve.tensor_tensor(here, here, yp[:, :, 0:D], ALU.add).then_inc(y_taken, 1)

            def expert(e, b, more):
                first, count = tiles_of(dve, e)
                with dve.Fori(0, count) as k:
                    hidden(TILES_SHARED + first + k)
                    dve.wait_ge(y_stored, 16 * (first + k) + 1)
                    dve.tensor_copy(y[:], yp[:, :, 0:D]).then_inc(y_taken, 1)

            over_experts(dve, expert)


def attn1_stage(nc, st, d):
    with ExitStack() as ctx:
        def sb(name, shape, dt=F32):
            return ctx.enter_context(nc.sbuf_tensor("a1_" + name, shape, dt))

        def sem(name):
            return st.semaphore(nc, "a1_" + name)

        w = [sb(n, [P, KC, D]) for n in ("wq", "wk", "wv")]
        wp = sb("wp", [P, KC, D])
        rows = sb("rows", [P, 1, D])
        qkv = sb("qkv", [P, 3, KC, N])
        acc = sb("acc", [P, U, TB, D])
        yr = sb("yr", [P, U, TB, K0, D])
        idx = sb("idx", [P, U, TB, K0], U32)
        xn = sb("xn", [P, U, TB, D])
        xT = sb("xT", [P, U, KC, S])
        bst = sb("bst", [P, 3, KC, B, 6])
        bnv = sb("bnv", [P, 3, KC, 2])
        bsc = sb("bsc", [P, 3, KC])
        bbi = sb("bbi", [P, 3, KC])
        sig = sb("sig", [P, U, 3, KC, S])
        vt = sb("vt", [P, U, TB, D])
        vvb = sb("vvb", [P, U, KC, P])
        oT = sb("oT", [P, U, KC, S])
        stats = sb("stats", [P, U, TB, 6])
        var = sb("var", [P, U, TB, 2])
        rstd = sb("rstd", [P, U, TB])
        ps = ctx.enter_context(nc.psum_tensor("a1_ps", [P, U, 4, 512], F32))

        def bank(u, n):
            return ps[:, u, n, :].rearrange("p (a b) -> p a b", a=2)

        w_loaded = sem("w_loaded")
        yr_loaded = [sem(f"yr_loaded{u}") for u in range(U)]
        idx_ready, summed = sem("idx_ready"), sem("summed")
        varr, rstdr, epsr, xn_ready = sem("var_ready"), sem("rstd_ready"), sem("eps_added"), sem("xn_ready")
        var2, rstd2, eps2, out_ready = sem("var2_ready"), sem("rstd2_ready"), sem("eps2_added"), sem("out_ready")
        t_ready, xT_ready, proj_ready = sem("t_ready"), sem("xT_ready"), sem("proj_ready")
        kept, counted = sem("proj_kept"), sem("proj_counted")
        bn_steps, bn_eps, bn_rstd, bn_ready = sem("bn_steps"), sem("bn_eps_added"), sem("bn_rstd_ready"), sem("bn_ready")
        sig_ready, qk_ready, vt_ready, vtok_ready = sem("sig_ready"), sem("qk_ready"), sem("vt_ready"), sem("vtok_ready")
        vv_ready, vvb_ready = sem("vv_ready"), sem("vvb_ready")
        o_ready, oT_ready, y_ready = sem("o_ready"), sem("oT_ready"), sem("y_ready")
        steps, steps2 = sem("dve_steps"), sem("dve_steps2")
        block = ctx.enter_context(nc.Block())

        @block.sync
        def _(sp):
            sp.dma_start(rows[:], d["rows"][len(ROWS) - 1:, :].partition_broadcast(P)).then_inc(w_loaded, 16)
            for t, n in zip(w + [wp], ("L1_attn_Wq", "L1_attn_Wk", "L1_attn_Wv", "L1_attn_Wp")):
                sp.dma_start(t[:], col(d[n])).then_inc(w_loaded, 16)

        @block.gpsimd
        def _(pool):
            def gather(i, u, start):
                pool.tensor_copy(idx[:, u], st.slot0[:, bass.ds(TB * U * i + TB * u, TB), :]).then_inc(idx_ready, 1)
                pool.wait_ge(idx_ready, start)
                pool.sem_inc(st.pool_passed, 1)
                for t in range(TB):
                    for j in range(K0):
                        pool.indirect_dma_start(
                            out=yr[:, u, t, j, :], out_offset=None, in_=st.ys0,
                            in_offset=bass.IndirectOffsetOnAxis(ap=idx[:, u, t, j:j + 1], axis=0)).then_inc(yr_loaded[u], 16)

            for u in range(U):
                gather(0, u, u + 1)
            with pool.Fori(0, STEPS - 1) as i:
                for u in range(U):
                    pool_rstd(pool, st, var, rstd, u, varr, rstdr, epsr, U * i + u + 1)
                for u in range(U):
                    pool.wait_ge(summed, U * i + u + 1)
                    pool.sem_inc(st.pool_passed, 1)
                    gather(i + 1, u, U * (i + 1) + u + 1)
            for u in range(U):
                pool_rstd(pool, st, var, rstd, u, varr, rstdr, epsr, U * (STEPS - 1) + u + 1)
            pool.wait_ge(bn_steps, 6)
            pool.tensor_tensor(bsc[:], bnv[:, :, :, 1], st.eps[:, 0:6].rearrange("p (a b) -> p a b", b=KC), ALU.add).then_inc(bn_eps, 1)
            pool.wait_ge(bn_eps, 1)
            pool.tensor_tensor(bsc[:], bsc[:], st.neghalf[:, 0:6].rearrange("p (a b) -> p a b", b=KC), ALU.pow).then_inc(bn_rstd, 1)
            with pool.Fori(0, STEPS) as i:
                for u in range(U):
                    pool_rstd(pool, st, var, rstd, u, var2, rstd2, eps2, U * i + u + 1)

        @block.tensor
        def _(pe):
            pe.wait_ge(w_loaded, 16 * 5)

            def turn(dst, src):
                for t in range(TB):
                    for c in range(KC):
                        ins = pe.transpose(dst[:, c, t * P:t * P + P], src[:, t, c * P:c * P + P], st.ident[:])
                return ins

            with pe.Fori(0, STEPS) as i:
                for u in range(U):
                    pe.wait_ge(xn_ready, U * i + u + 1)
                    turn(bank(u, 0), xn[:, u]).then_inc(t_ready, 1)
                for u in range(U):
                    pe.wait_ge(xT_ready, U * i + u + 1)
                    pe.wait_ge(kept, U * i + 1)
                    for n in range(3):
                        for m in range(KC):
                            for c in range(KC):
                                ins = pe.matmul(bank(u, 1 + n)[:, m, :], w[n][:, c, m * P:m * P + P], xT[:, u, c, :],
                                                start=(c == 0), stop=(c == KC - 1))
                    ins.then_inc(proj_ready, 1)
            pe.wait_ge(kept, B + 1)
            with pe.Fori(0, STEPS) as i:
                for u in range(U):
                    pe.wait_ge(sig_ready, U * i + u + 1)
                    for c in range(KC):
                        for t in range(TB):
                            ins = pe.transpose(bank(u, 0)[:, t, c * P:c * P + P], sig[:, u, 2, c, t * P:t * P + P], st.ident[:])
                    ins.then_inc(vt_ready, 1)
                for u in range(U):
                    pe.wait_ge(vtok_ready, U * i + u + 1)
                    for m in range(KC):
                        for t in range(TB):
                            v = vt[:, u, t, m * P:m * P + P]
                            ins = pe.matmul(bank(u, 1)[:, m, 0:P], v, v, start=(t == 0), stop=(t == TB - 1))
                    ins.then_inc(vv_ready, 1)
                for u in range(U):
                    pe.wait_ge(vvb_ready, U * i + u + 1)
                    pe.wait_ge(qk_ready, U * i + u + 1)
                    for m in range(KC):
                        ins = pe.matmul(bank(u, 2)[:, m, :], vvb[:, u, m, :], sig[:, u, 0, m, :], start=True, stop=True)
                    ins.then_inc(o_ready, 1)
                for u in range(U):
                    pe.wait_ge(oT_ready, U * i + u + 1)
                    for t in range(TB):
                        for c in range(KC):
                            ins = pe.matmul(bank(u, 3)[:, t, :], oT[:, u, c, t * P:t * P + P], wp[:, c, :],
                                            start=(c == 0), stop=(c == KC - 1))
                    ins.then_inc(y_ready, 1)

        @block.scalar
        def _(act):
            act.sem_inc(kept, 1)
            with act.Fori(0, STEPS) as i:
                for u in range(U):
                    act.wait_ge(t_ready, U * i + u + 1)
                    act.activation(xT[:, u], bank(u, 0), ACT.Copy).then_inc(xT_ready, 1)
                for u in range(U):
                    act.wait_ge(proj_ready, U * i + u + 1)
                    act.sem_inc(st.act_passed, 1)
                    for n in range(3):
                        ins = act.activation(qkv[:, n, :, bass.ds(S * U * i + S * u, S)], bank(u, 1 + n), ACT.Copy)
                    ins.then_inc(kept, 1)
            act.wait_ge(bn_ready, 1)
            act.wait_ge(kept, B + 1)
            with act.Fori(0, STEPS) as i:
                for u in range(U):
                    for n in (2, 0, 1):
                        for m in range(KC):
                            ins = act.activation(sig[:, u, n, m, :], qkv[:, n, m, bass.ds(S * U * i + S * u, S)], ACT.Sigmoid,
                                                 bias=bbi[:, n, m:m + 1], scale=bsc[:, n, m:m + 1])
                    ins.then_inc(sig_ready, 1)
                for u in range(U):
                    act.wait_ge(vt_ready, U * i + u + 1)
                    act.activation(vt[:, u], bank(u, 0), ACT.Copy).then_inc(vtok_ready, 1)
                for u in range(U):
                    act.wait_ge(o_ready, U * i + u + 1)
                    act.activation(oT[:, u], bank(u, 2), ACT.Copy).then_inc(oT_ready, 1)

        @block.vector
        def _(dve):
            with dve.Fori(0, STEPS) as i:
                s = Steps(dve, steps, i, U * 7)
                for u in range(U):
                    blk = TB * U * i + TB * u
                    dve.wait_ge(yr_loaded[u], 16 * TB * K0 * (i + 1))
                    for j in range(K0):
                        for t in range(TB):
                            before = acc[:, u, t, :] if j else st.res[:, bass.ds(blk + t, 1), :].squeeze(1)
                            n_sum = s.mark(dve.scalar_tensor_tensor(acc[:, u, t, :], yr[:, u, t, j, :],
                                                                    st.gate0[:, bass.ds(blk + t, 1), j:j + 1].squeeze(1),
                                                                    before, ALU.mult, ALU.add))
                        s.after(n_sum)
                    dve.sem_inc(summed, 1)
                    dve_stats(dve, st, s, acc[:, u], stats, var, u, varr)
                for u in range(U):
                    dve.wait_ge(rstdr, U * i + u + 1)
                    s.mark(dve_normalize(dve, xn[:, u], acc[:, u], var, rstd, u))
                    s.after(s.n)
                    dve.sem_inc(st.dve_passed, 1)
                    dve.tensor_copy(st.res[:, bass.ds(TB * U * i + TB * u, TB), :], xn[:, u]).then_inc(xn_ready, 1)
                for u in range(U):
                    dve.wait_ge(kept, U * i + u + 2)
                    dve.sem_inc(st.dve_passed, 1)
                    for n in range(3):
                        for m in range(KC):
                            ins = dve.bn_stats(bst[:, n, m, bass.ds(U * i + u, 1), :].squeeze(1), qkv[:, n, m, bass.ds(S * U * i + S * u, S)])
                    ins.then_inc(counted, 1)
                s.close()
            dve.wait_ge(counted, B)
            for n in range(3):
                for m in range(KC):
                    dve.bn_aggr(bnv[:, n, m, :], bst[:, n, m].rearrange("p b s -> p (b s)")).then_inc(bn_steps, 1)
            dve.wait_ge(bn_rstd, 1)
            g0, b0 = 2 * VECS.index("L1_attn_gq"), 2 * VECS.index("L1_attn_bq")
            g6 = st.vecs[:, g0:g0 + 6].rearrange("p (a b) -> p a b", b=KC)
            b6 = st.vecs[:, b0:b0 + 6].rearrange("p (a b) -> p a b", b=KC)
            dve.tensor_tensor(bsc[:], bsc[:], g6, ALU.mult).then_inc(bn_steps, 1)
            dve.wait_ge(bn_steps, 7)
            dve.tensor_tensor(bbi[:], bsc[:], bnv[:, :, :, 0], ALU.mult).then_inc(bn_steps, 1)
            dve.wait_ge(bn_steps, 8)
            dve.tensor_tensor(bbi[:], b6, bbi[:], ALU.subtract).then_inc(bn_steps, 1)
            dve.tensor_scalar(bsc[:], bsc[:], 4.0, None, ALU.mult).then_inc(bn_steps, 1)
            dve.wait_ge(bn_steps, 10)
            dve.tensor_scalar(bbi[:], bbi[:], -1.0, 4.0, ALU.add, ALU.mult).then_inc(bn_ready, 1)
            dve.sem_inc(out_ready, 1)
            with dve.Fori(0, STEPS) as i:
                s = Steps(dve, steps2, i, U * 4)
                for u in range(U):
                    dve.wait_ge(sig_ready, U * i + u + 1)
                    dve.tensor_tensor(sig[:, u, 0], sig[:, u, 0], sig[:, u, 1], ALU.mult).then_inc(qk_ready, 1)
                dve.wait_ge(w_loaded, 16 * 5)
                dve.wait_ge(out_ready, U * i + 1)
                for u in range(U):
                    s.mark(dve.tensor_tensor(xn[:, u], st.res[:, bass.ds(TB * U * i + TB * u, TB), :],
                                             rows[:].to_broadcast([P, TB, D]), ALU.add))
                for u in range(U):
                    dve.wait_ge(vv_ready, U * i + u + 1)
                    dve.tensor_tensor(vvb[:, u], bank(u, 1)[:, :, 0:P],
                                      st.blk[:].unsqueeze(1).to_broadcast([P, KC, P]), ALU.mult).then_inc(vvb_ready, 1)
                for u in range(U):
                    dve.wait_ge(y_ready, U * i + u + 1)
                    s.after(s.n)
                    s.do(dve.tensor_tensor(xn[:, u], xn[:, u], bank(u, 3), ALU.add))
                    dve_stats(dve, st, s, xn[:, u], stats, var, u, var2)
                for u in range(U):
                    dve.wait_ge(rstd2, U * i + u + 1)
                    dve_normalize(dve, st.res[:, bass.ds(TB * U * i + TB * u, TB), :], xn[:, u], var, rstd,
                                  u).then_inc(out_ready, 1)
                s.close()
            dve.wait_ge(out_ready, B + 1)


def moe1_stage(nc, st, d):
    with ExitStack() as ctx:
        def sb(name, shape, dt=F32):
            return ctx.enter_context(nc.sbuf_tensor("m1_" + name, shape, dt))

        def sem(name):
            return st.semaphore(nc, "m1_" + name)

        w1_all = sb("w1_all", [P, TILES1, KC, I1], BF16)
        w3_all = sb("w3_all", [P, TILES1, KC, I1], BF16)
        w2_all = sb("w2_all", [P, TILES1, D], BF16)
        w1, w3 = sb("w1", [P, U, KC, I1]), sb("w3", [P, U, KC, I1])
        w2 = sb("w2", [P, U, D])
        x = sb("x", [P, U, TB, D])
        xT = sb("xT", [P, U, KC, S])
        sg = sb("sg", [P, U, S])
        h = sb("h", [P, U, S])
        y = sb("y", [P, U, TB, D])
        ps = ctx.enter_context(nc.psum_tensor("m1_ps", [P, U, 4, 512], F32))

        def bank(u, n):
            return ps[:, u, n, :].rearrange("p (a b) -> p a b", a=2)

        w_loaded, w_ready = sem("w_loaded"), sem("w_ready")
        x_loaded, y_stored = [sem(f"x_loaded{u}") for u in range(U)], [sem(f"y_stored{u}") for u in range(U)]
        t_ready, xT_ready, gu_ready = sem("t_ready"), sem("xT_ready"), sem("gu_ready")
        silu_ready, h_ready, down_done, y_ready = sem("silu_ready"), sem("h_ready"), sem("down_done"), sem("y_ready")
        block = ctx.enter_context(nc.Block())

        @block.sync
        def _(sp):
            def rows(dram, i, u):
                return dram[bass.ds(S * (U * i + u), S), :].rearrange("(n p) c -> p n c", p=P)

            for u in range(U):
                sp.sem_inc(y_stored[u], 1)
                sp.dma_start(x[:, u], rows(st.xs1, 0, u)).then_inc(x_loaded[u], 16)
            w1v = d["L1_ffn_W1"].rearrange("e (k p) n -> p e k n", p=P)
            w3v = d["L1_ffn_W3"].rearrange("e (k p) n -> p e k n", p=P)
            w2v = d["L1_ffn_W2"].rearrange("e p n -> p e n")
            for k in range(KC):
                sp.dma_start(w1_all[:, 0:E1, k, :], w1v[:, 0:E1, k, :]).then_inc(w_loaded, 16)
                sp.dma_start(w3_all[:, 0:E1, k, :], w3v[:, 0:E1, k, :]).then_inc(w_loaded, 16)
                sp.dma_start(w1_all[:, E1:, k, :], w1v[:, E1:, k, :].to_broadcast([P, TILES_SHARED, I1])).then_inc(w_loaded, 16)
                sp.dma_start(w3_all[:, E1:, k, :], w3v[:, E1:, k, :].to_broadcast([P, TILES_SHARED, I1])).then_inc(w_loaded, 16)
            sp.dma_start(w2_all[:, 0:E1, :], w2v[:, 0:E1, :]).then_inc(w_loaded, 16)
            sp.dma_start(w2_all[:, E1:, :], w2v[:, E1:, :].to_broadcast([P, TILES_SHARED, D])).then_inc(w_loaded, 16)

            def store(i):
                for u in range(U):
                    sp.wait_ge(y_ready, U * i + u + 2)
                    sp.dma_start(rows(st.ys1, i, u), y[:, u]).then_inc(y_stored[u], 16)

            with sp.Fori(0, TILES1 // U - 1) as i:
                for u in range(U):
                    sp.wait_ge(t_ready, U * i + u + 1)
                    sp.dma_start(x[:, u], rows(st.xs1, i + 1, u)).then_inc(x_loaded[u], 16)
                store(i)
            store(TILES1 // U - 1)
            for u in range(U):
                sp.wait_ge(y_stored[u], 16 * TILES1 // U + 1)

        @block.gpsimd
        def _(pool):
            pool.wait_ge(w_loaded, 16 * (4 * KC + 2))

            def widen(i, u):
                t = U * i + u
                pool.tensor_copy(w1[:, u], w1_all[:, bass.ds(t, 1)].squeeze(1)).then_inc(w_ready, 1)
                pool.tensor_copy(w3[:, u], w3_all[:, bass.ds(t, 1)].squeeze(1)).then_inc(w_ready, 1)
                pool.tensor_copy(w2[:, u], w2_all[:, bass.ds(t, 1)].squeeze(1)).then_inc(w_ready, 1)

            for u in range(U):
                widen(0, u)
            with pool.Fori(0, TILES1 // U - 1) as i:
                for u in range(U):
                    pool.wait_ge(down_done, U * i + u + 1)
                    pool.sem_inc(st.pool_passed, 1)
                    widen(i + 1, u)

        @block.tensor
        def _(pe):
            with pe.Fori(0, TILES1 // U) as i:
                for u in range(U):
                    pe.wait_ge(x_loaded[u], 16 * (i + 1))
                    for t in range(TB):
                        for c in range(KC):
                            ins = pe.transpose(bank(u, 0)[:, c, t * P:t * P + P], x[:, u, t, c * P:c * P + P], st.ident[:])
                    ins.then_inc(t_ready, 1)
                for u in range(U):
                    pe.wait_ge(xT_ready, U * i + u + 1)
                    pe.wait_ge(w_ready, 3 * (U * i + u + 1))
                    for n, w in enumerate((w1, w3)):
                        for c in range(KC):
                            ins = pe.matmul(bank(u, 1)[:, n, :], w[:, u, c, :], xT[:, u, c, :], start=(c == 0), stop=(c == KC - 1))
                    ins.then_inc(gu_ready, 1)
                for u in range(U):
                    pe.wait_ge(h_ready, U * i + u + 1)
                    pe.wait_ge(y_ready, U * i + 1)
                    for t in range(TB):
                        ins = pe.matmul(bank(u, 2)[:, t, :], h[:, u, t * P:t * P + P], w2[:, u, :], start=True, stop=True)
                    ins.then_inc(down_done, 1)

        @block.scalar
        def _(act):
            with act.Fori(0, TILES1 // U) as i:
                for u in range(U):
                    act.wait_ge(t_ready, U * i + u + 1)
                    act.activation(xT[:, u], bank(u, 0), ACT.Copy).then_inc(xT_ready, 1)
                for u in range(U):
                    act.wait_ge(gu_ready, U * i + u + 1)
                    act.activation(sg[:, u, :], bank(u, 1)[:, 0, :], ACT.Silu).then_inc(silu_ready, 1)

        @block.vector
        def _(dve):
            dve.sem_inc(y_ready, 1)
            with dve.Fori(0, TILES1 // U) as i:
                for u in range(U):
                    dve.wait_ge(silu_ready, U * i + u + 1)
                    dve.tensor_tensor(h[:, u, :], sg[:, u, :], bank(u, 1)[:, 1, :], ALU.mult).then_inc(h_ready, 1)
                for u in range(U):
                    dve.wait_ge(down_done, U * i + u + 1)
                    dve.wait_ge(y_stored[u], 16 * i + 1)
                    dve.tensor_copy(y[:, u], bank(u, 2)).then_inc(y_ready, 1)


def output_stage(nc, st, d, out):
    with ExitStack() as ctx:
        def sb(name, shape, dt=F32):
            return ctx.enter_context(nc.sbuf_tensor("out_" + name, shape, dt))

        def sem(name):
            return st.semaphore(nc, "out_" + name)

        sh = sb("sh", [P, U, TB, D])
        yr = sb("yr", [P, U, TB, K1, D])
        idx = sb("idx", [P, U, TB, K1], U32)
        xn = sb("xn", [P, U, TB, D])
        stats = sb("stats", [P, U, TB, 6])
        var = sb("var", [P, U, TB, 2])
        rstd = sb("rstd", [P, U, TB])
        sh_loaded, yr_loaded = [sem(f"sh_loaded{u}") for u in range(U)], [sem(f"yr_loaded{u}") for u in range(U)]
        stored = [sem(f"stored{u}") for u in range(U)]
        idx_ready, summed, steps = sem("idx_ready"), sem("summed"), sem("dve_steps")
        varr, rstdr, epsr, xn_ready = sem("var_ready"), sem("rstd_ready"), sem("eps_added"), sem("xn_ready")
        block = ctx.enter_context(nc.Block())
        sh_v = st.ys1[SHARED1:SHARED1 + N, :].rearrange("(n p) c -> p n c", p=P)
        out_v = out.rearrange("(n p) c -> p n c", p=P)

        @block.sync
        def _(sp):
            for u in range(U):
                sp.dma_start(sh[:, u], sh_v[:, TB * u:TB * u + TB, :]).then_inc(sh_loaded[u], 16)
            with sp.Fori(0, STEPS - 1) as i:
                for u in range(U):
                    sp.wait_ge(xn_ready, U * i + u + 1)
                    sp.dma_start(sh[:, u], sh_v[:, bass.ds(TB * U * (i + 1) + TB * u, TB), :]).then_inc(sh_loaded[u], 16)

        @block.scalar
        def _(act):
            for u in range(U):
                act.sem_inc(stored[u], 1)
            with act.Fori(0, STEPS) as i:
                for u in range(U):
                    act.wait_ge(xn_ready, U * i + u + 1)
                    act.dma_start(out_v[:, bass.ds(TB * U * i + TB * u, TB), :], xn[:, u]).then_inc(stored[u], 16)
            for u in range(U):
                act.wait_ge(stored[u], 16 * STEPS + 1)

        @block.gpsimd
        def _(pool):
            def gather(i, u, count):
                pool.tensor_copy(idx[:, u], st.slot1[:, bass.ds(TB * U * i + TB * u, TB), :]).then_inc(idx_ready, 1)
                pool.wait_ge(idx_ready, count)
                pool.sem_inc(st.pool_passed, 1)
                for t in range(TB):
                    for j in range(K1):
                        pool.indirect_dma_start(
                            out=yr[:, u, t, j, :], out_offset=None, in_=st.ys1,
                            in_offset=bass.IndirectOffsetOnAxis(ap=idx[:, u, t, j:j + 1], axis=0)).then_inc(yr_loaded[u], 16)

            for u in range(U):
                gather(0, u, u + 1)
            with pool.Fori(0, STEPS - 1) as i:
                for u in range(U):
                    pool_rstd(pool, st, var, rstd, u, varr, rstdr, epsr, U * i + u + 1)
                for u in range(U):
                    pool.wait_ge(summed, U * i + u + 1)
                    pool.sem_inc(st.pool_passed, 1)
                    gather(i + 1, u, U * (i + 1) + u + 1)
            for u in range(U):
                pool_rstd(pool, st, var, rstd, u, varr, rstdr, epsr, U * (STEPS - 1) + u + 1)

        @block.vector
        def _(dve):
            with dve.Fori(0, STEPS) as i:
                s = Steps(dve, steps, i, U * (3 + TB * K1))
                for u in range(U):
                    blk = TB * U * i + TB * u
                    dve.wait_ge(sh_loaded[u], 16 * (i + 1))
                    s.do(dve.tensor_tensor(sh[:, u], sh[:, u], st.res[:, bass.ds(blk, TB), :], ALU.add))
                    dve.wait_ge(yr_loaded[u], 16 * TB * K1 * (i + 1))
                    for j in range(K1):
                        for t in range(TB):
                            n_sum = s.mark(dve.scalar_tensor_tensor(sh[:, u, t, :], yr[:, u, t, j, :],
                                                                    st.gate1[:, bass.ds(blk + t, 1), j:j + 1].squeeze(1),
                                                                    sh[:, u, t, :], ALU.mult, ALU.add))
                        s.after(n_sum)
                    dve.sem_inc(summed, 1)
                    dve_stats(dve, st, s, sh[:, u], stats, var, u, varr)
                for u in range(U):
                    dve.wait_ge(rstdr, U * i + u + 1)
                    dve.wait_ge(stored[u], 16 * i + 1)
                    dve_normalize(dve, xn[:, u], sh[:, u], var, rstd, u).then_inc(xn_ready, 1)
                s.close()


def xattn0_stage(nc, st, d):
    xattn_stage(nc, st, d, 0)


def xattn1_stage(nc, st, d):
    xattn_stage(nc, st, d, 1)


STAGES = [setup_stage, rwkv_stage, xattn0_stage, moe0_stage, attn1_stage, xattn1_stage, moe1_stage]


def decoder(nc, d, out):
    st = Store()
    with ExitStack() as ctx:
        def sb(name, shape, dt=F32):
            return ctx.enter_context(nc.sbuf_tensor(name, shape, dt))

        def dram(name, shape):
            return nc.dram_tensor(name, shape, F32, kind="Internal").ap()

        st.res = sb("res", [P, NBLK, D])
        st.vecs = sb("vecs", [P, KC * len(VECS)])
        st.ebias = sb("ebias", [P, E1])
        st.zero = sb("zero", [P, D])
        st.ident = sb("ident", [P, P])
        st.identb = sb("identb", [P, P], BF16)
        st.lower = sb("lower", [P, P], BF16)
        st.ones = sb("ones", [P, P], BF16)
        st.hmask = sb("hmask", [P, HPC])
        st.selrow = sb("selrow", [P, HEADS, P], F32R)
        st.eps = sb("eps", [P, 8])
        st.dve_passed = ctx.enter_context(nc.semaphore("dve_passed"))
        st.act_passed = ctx.enter_context(nc.semaphore("act_passed"))
        st.sp_passed = ctx.enter_context(nc.semaphore("sp_passed"))
        st.pe_passed = ctx.enter_context(nc.semaphore("pe_passed"))
        st.pool_passed = ctx.enter_context(nc.semaphore("pool_passed"))
        st.consts_ready = ctx.enter_context(nc.semaphore("consts_ready"))
        st.blk = sb("blk", [P, P])
        st.neghalf = sb("neghalf", [P, 8])
        st.iota = sb("iota", [P, E1])
        st.base1 = sb("base1", [P, E1])
        st.w = sb("w", [P, KC])
        st.macc0 = sb("macc0", [P, U, E0P], BF16)
        st.macc1 = sb("macc1", [P, U, E1], BF16)
        st.slot0 = sb("slot0", [P, NBLK, K0], U32)
        st.gate0 = sb("gate0", [P, NBLK, K0])
        st.slot1 = sb("slot1", [P, NBLK, K1], U32)
        st.gate1 = sb("gate1", [P, NBLK, K1])
        st.expert0 = sb("expert0", [P, NBLK, K0])
        st.rank0 = sb("rank0", [P, NBLK, K0])
        st.tile0 = sb("tile0", [P, E0P], I32)
        st.tiles0 = sb("tiles0", [P, E0], I32)
        st.end0 = sb("end0", [P, E0], I32)
        st.xs0, st.ys0 = dram("xs0", [(TILES0_MAX + 1) * S, D]), dram("ys0", [TILES0_MAX * S, D])
        st.xs1, st.ys1 = dram("xs1", [ROWS1, D]), dram("ys1", [ROWS1, D])

        for stage in STAGES:
            stage(nc, st, d)
            st.end_stage(nc)
        output_stage(nc, st, d, out)


_T = ["L0_attn_Wk", "L0_attn_Wv", "L0_attn_Wr", "L0_attn_Wo", "L0_attn_Fk", "L0_attn_Fr", "L0_attn_Fv",
      "L0_xattn_w_q", "L0_xattn_w_k", "L0_xattn_w_v", "L0_ffn_router_w",
      "L1_attn_Wq", "L1_attn_Wk", "L1_attn_Wv", "L1_attn_Wp",
      "L1_xattn_Wq", "L1_xattn_Wk", "L1_xattn_Wv", "L1_ffn_gate_w", "L0_xattn_w_o", "L1_xattn_Wo"]


def kernel(**inputs):
    import numpy as _np
    import concourse.bacc as _bacc
    from concourse import mybir as _mybir
    from concourse.bass_utils import run_bass_kernel_spmd as _run

    a = {k: _np.asarray(v) for k, v in inputs.items()}
    arrays = {n: _np.ascontiguousarray(a[n].T) for n in _T}
    arrays["x"] = a["x"].reshape(N, D)
    arrays["ctx"] = _np.ascontiguousarray(a["ctx_1024"].reshape(N, D).T)
    mask = a["mask_1x1xSxS2_ik0"].reshape(S, S)
    arrays["mask"] = _np.ascontiguousarray(mask)
    arrays["mask_t"] = _np.ascontiguousarray(mask.T)
    arrays["vecs"] = _np.ascontiguousarray(_np.stack([a[n] for n in VECS]).reshape(len(VECS), KC, P)
                                           .transpose(2, 0, 1).reshape(P, -1))
    arrays["rows"] = _np.stack([a[n] for n in ROWS])
    arrays["L1_ffn_bias"] = a["L1_ffn_bias"]
    for n, m in (("L0_ffn_w_gate", "L0_ffn_sw_gate"), ("L0_ffn_w_up", "L0_ffn_sw_up"), ("L0_ffn_w_down", "L0_ffn_sw_down")):
        arrays[n] = _np.concatenate([a[m], a[n]])
    for n, m in (("L1_ffn_W1", "L1_ffn_sw1"), ("L1_ffn_W3", "L1_ffn_sw3"), ("L1_ffn_W2", "L1_ffn_sw2")):
        arrays[n] = _np.concatenate([a[n], a[m].T[None]])

    nc = _bacc.Bacc("TRN2", target_bir_lowering=False, num_devices=1)
    d = {n: nc.dram_tensor("in_" + n, v.shape, _mybir.dt.from_np(v.dtype), kind="ExternalInput").ap()
         for n, v in arrays.items()}
    out = nc.dram_tensor("out", (N, D), F32, kind="ExternalOutput").ap()
    decoder(nc, d, out)
    r = _run(nc, [{"in_" + n: v for n, v in arrays.items()}], core_ids=[0])
    return r.results[0]["out"].reshape(B, S, D)
```
